# Optimizing a Trainium2 kernel written in Bass

```python
import numpy as np
import jax
import jax.numpy as jnp

def _softmax(x, axis=-1):
    return jax.nn.softmax(x, axis=axis)

def _gelu(x):
    return jax.nn.gelu(x, approximate=True)

def _silu(x):
    return jax.nn.silu(x)

def _sigmoid(x):
    return jax.nn.sigmoid(x)

def _layernorm(x, axis=-1, eps=1e-05):
    m = jnp.mean(x, axis=axis, keepdims=True)
    v = jnp.var(x, axis=axis, keepdims=True)
    return (x - m) / jnp.sqrt(v + eps)

def _scatter_add(tgt, idx, src, axis=0):
    return tgt.at[idx].add(src)

def _segment_sum(src, seg, n):
    return jax.ops.segment_sum(src, seg, n)
kernel_name = 'mk_gps_d1_gnn_r8_e206db'

def setup_inputs(seed: int=0):
    np.random.seed(seed)
    _w = jnp.asarray

    def _rec_inputs():
        import jax
        import jax.numpy as jnp
        _gk = jax.random.key(seed)
        x = -0.0002949 + 1 * jax.random.normal(jax.random.fold_in(_gk, 1), (1250, 512), jnp.float32)
        _s = jax.random.randint(jax.random.fold_in(_gk, 2), (20000,), 0, 1250, jnp.int32)
        _d = jax.random.randint(jax.random.fold_in(_gk, 3), (20000,), 0, 1250, jnp.int32)
        _loop = jnp.arange(1250, dtype=jnp.int32)
        src = jnp.concatenate([_s, _d, _loop])
        dst = jnp.concatenate([_d, _s, _loop])
        _o = jnp.argsort(dst, stable=True)
        src = src[_o]
        dst = dst[_o]
        node_vec1 = jax.random.uniform(jax.random.fold_in(_gk, 12), (1250, 1), jnp.float32, 0.0, 0.999957)
        return (x, src, dst, node_vec1)
    x, src, dst, node_vec1 = _rec_inputs()

    def _L0_gnn_setup():
        import jax, jax.numpy as jnp
        import numpy as np
        N_NODES = 40962
        LATENT_DIM = 512
        N_EDGES = 81924
        NUM_BLOCKS = 4
        NUM_HEADS = 4
        NUM_FREQ = 32
        BASE_PERIOD = 16
        NOISE_EMB_DIM = 16
        EPS = 1e-05

        def _cond_layer_norm(x, cond, sw, sb, bw, bb):
            mu = jnp.mean(x, axis=-1, keepdims=True)
            var = jnp.var(x, axis=-1, keepdims=True)
            xn = (x - mu) * jax.lax.rsqrt(var + EPS)
            scale = cond @ sw + sb
            bias = cond @ bw + bb
            return xn * (1.0 + scale) + bias

        def _sparse_attention(x, src, dst, wq, bq, wk, bk, wv, bv, wo, bo):
            N, D = x.shape
            H, Dh = (NUM_HEADS, D // NUM_HEADS)
            q = (x @ wq + bq).reshape(N, H, Dh) * Dh ** (-0.5)
            k = (x @ wk + bk).reshape(N, H, Dh)
            v = (x @ wv + bv).reshape(N, H, Dh)
            scores = jnp.einsum('ehd,ehd->eh', q[src], k[dst])
            smax = jax.ops.segment_max(scores, src, num_segments=N)
            ex = jnp.exp(scores - smax[src])
            denom = jax.ops.segment_sum(ex, src, num_segments=N)
            attn = ex / denom[src]
            out = jax.ops.segment_sum(attn[:, :, None] * v[dst], src, num_segments=N)
            return out.reshape(N, D) @ wo + bo

        def _forward(x, edge_index, noise_levels, f_w1, f_b1, f_w2, f_b2, s1_w, s1_b, b1_w, b1_b, wq, bq, wk, bk, wv, bv, wo, bo, s2_w, s2_b, b2_w, b2_b, m_w1, m_b1, m_w2, m_b2):
            src, dst = (edge_index[0], edge_index[1])
            freqs = jnp.arange(1, NUM_FREQ + 1, dtype=x.dtype) * (2.0 * np.pi / BASE_PERIOD)
            ph = noise_levels * freqs
            emb = jnp.concatenate([jnp.sin(ph), jnp.cos(ph)], axis=-1)
            cond = jax.nn.silu(emb @ f_w1 + f_b1) @ f_w2 + f_b2
            for i in range(NUM_BLOCKS):
                y = _cond_layer_norm(x, cond, s1_w[i], s1_b[i], b1_w[i], b1_b[i])
                y = _sparse_attention(y, src, dst, wq[i], bq[i], wk[i], bk[i], wv[i], bv[i], wo[i], bo[i])
                x = x + y
                y = _cond_layer_norm(x, cond, s2_w[i], s2_b[i], b2_w[i], b2_b[i])
                y = jax.nn.relu(y @ m_w1[i] + m_b1[i]) @ m_w2[i] + m_b2[i]
                x = x + y
            return x
        key = jax.random.key(seed)
        ks = jax.random.split(key, 20)

        def w(k, shape, s=0.02):
            return jax.random.normal(k, shape, dtype=jnp.float32) * s
        D, B, C = (LATENT_DIM, NUM_BLOCKS, NOISE_EMB_DIM)
        z = lambda *s: jnp.zeros(s, jnp.float32)
        return {'latent_mesh_nodes': jax.random.normal(ks[0], (N_NODES, D), dtype=jnp.float32), 'edge_index': jax.random.randint(ks[1], (2, N_EDGES), 0, N_NODES, dtype=jnp.int32), 'noise_levels': jax.random.uniform(ks[2], (N_NODES, 1), dtype=jnp.float32), 'f_w1': w(ks[3], (2 * NUM_FREQ, C)), 'f_b1': z(C), 'f_w2': w(ks[4], (C, C)), 'f_b2': z(C), 's1_w': w(ks[5], (B, C, D)), 's1_b': z(B, D), 'b1_w': w(ks[6], (B, C, D)), 'b1_b': z(B, D), 'wq': w(ks[7], (B, D, D)), 'bq': z(B, D), 'wk': w(ks[8], (B, D, D)), 'bk': z(B, D), 'wv': w(ks[9], (B, D, D)), 'bv': z(B, D), 'wo': w(ks[10], (B, D, D)), 'bo': z(B, D), 's2_w': w(ks[11], (B, C, D)), 's2_b': z(B, D), 'b2_w': w(ks[12], (B, C, D)), 'b2_b': z(B, D), 'm_w1': w(ks[13], (B, D, D)), 'm_b1': z(B, D), 'm_w2': w(ks[14], (B, D, D)), 'm_b2': z(B, D)}
    _L0_gnn_all = _L0_gnn_setup()
    _L0_gnn_in = {k: v for k, v in _L0_gnn_all.items() if k in ('f_w1', 'f_b1', 'f_w2', 'f_b2', 's1_w', 's1_b', 'b1_w', 'b1_b', 'wq', 'bq', 'wk', 'bk', 'wv', 'bv', 'wo', 'bo', 's2_w', 's2_b', 'b2_w', 'b2_b', 'm_w1', 'm_b1', 'm_w2', 'm_b2')}
    del _L0_gnn_all

    def _L0_mix_setup():
        import jax, jax.numpy as jnp
        import numpy as np
        import math
        B, N, DIM = (4, 512, 512)
        HEADS, DH, NBF = (8, 64, 256)
        MLP_H = DIM * 2

        def layernorm(x, g, b, eps=1e-05):
            mu = jnp.mean(x, axis=-1, keepdims=True)
            var = jnp.mean(jnp.square(x - mu), axis=-1, keepdims=True)
            return (x - mu) * jax.lax.rsqrt(var + eps) * g + b

        def softmax_kernel(x, pmat):
            xp = jnp.einsum('bhnd,df->bhnf', x, pmat)
            xp = xp - jnp.max(xp, axis=-1, keepdims=True)
            return jnp.exp(xp) / math.sqrt(pmat.shape[-1])
        key = jax.random.key(seed)
        ks = jax.random.split(key, 8)
        s = lambda d: 1.0 / math.sqrt(d)
        return {'x': jax.random.normal(ks[0], (B, N, DIM), jnp.float32), 'Wqkv': jax.random.normal(ks[1], (DIM, 3 * HEADS * DH), jnp.float32) * s(DIM), 'bqkv': jnp.zeros((3 * HEADS * DH,), jnp.float32), 'Pmat': jax.random.normal(ks[2], (DH, NBF), jnp.float32), 'Wproj': jax.random.normal(ks[3], (HEADS * DH, DIM), jnp.float32) * s(HEADS * DH), 'bproj': jnp.zeros((DIM,), jnp.float32), 'W1': jax.random.normal(ks[4], (DIM, MLP_H), jnp.float32) * s(DIM), 'b1': jnp.zeros((MLP_H,), jnp.float32), 'W2': jax.random.normal(ks[5], (MLP_H, DIM), jnp.float32) * s(MLP_H), 'b2': jnp.zeros((DIM,), jnp.float32), 'g1': jnp.ones((DIM,), jnp.float32), 'be1': jnp.zeros((DIM,), jnp.float32), 'g2': jnp.ones((DIM,), jnp.float32), 'be2': jnp.zeros((DIM,), jnp.float32)}
    _L0_mix_all = _L0_mix_setup()
    _L0_mix_in = {k: v for k, v in _L0_mix_all.items() if k in ('Wqkv', 'bqkv', 'Pmat', 'Wproj', 'bproj', 'W1', 'b1', 'W2', 'b2', 'g1', 'be1', 'g2', 'be2')}
    del _L0_mix_all

    def _L0_ffn_setup():
        import jax, jax.numpy as jnp
        import numpy as np
        B, S, D = (4, 256, 512)
        I = 384
        E = 16
        K = 2

        def _inv_softplus(v):
            return float(np.log(np.expm1(v)))

        def swiglu5(h, alpha, gate_scale, up_shift, gate_clamp_raw, up_clamp_raw):
            gate_clamp = jax.nn.softplus(gate_clamp_raw)
            up_clamp = jax.nn.softplus(up_clamp_raw)
            g = jnp.clip(h[..., ::2], -gate_clamp, gate_clamp)
            u = jnp.clip(h[..., 1::2], -up_clamp, up_clamp)
            return g * jax.nn.sigmoid(g * alpha) * gate_scale * (u + up_shift)
        key = jax.random.key(seed)
        ks = jax.random.split(key, 10)
        std = 0.02
        raw = _inv_softplus(7.0)
        act = jnp.array([1.702, 1.0, 1.0, raw, raw], dtype=jnp.float32)
        return {'x': jax.random.normal(ks[0], (B, S, D), dtype=jnp.float32), 'gate_w': jax.random.normal(ks[1], (D, E), dtype=jnp.float32) * 0.01, 'gate_b': jnp.zeros((E,), dtype=jnp.float32), 'shared_w1': jax.random.normal(ks[2], (D, 2 * I), dtype=jnp.float32) * std, 'shared_b1': jnp.zeros((2 * I,), dtype=jnp.float32), 'shared_w2': jax.random.normal(ks[3], (I, D), dtype=jnp.float32) * std, 'shared_b2': jnp.zeros((D,), dtype=jnp.float32), 'shared_act': act, 'expert_w1': jax.random.normal(ks[4], (E, D, 2 * I), dtype=jnp.float32) * std, 'expert_b1': jnp.zeros((E, 2 * I), dtype=jnp.float32), 'expert_w2': jax.random.normal(ks[5], (E, I, D), dtype=jnp.float32) * std, 'expert_b2': jnp.zeros((E, D), dtype=jnp.float32), 'expert_act': jnp.tile(act[None, :], (E, 1))}
    _L0_ffn_all = _L0_ffn_setup()
    _L0_ffn_in = {k: v for k, v in _L0_ffn_all.items() if k in ('gate_w', 'gate_b', 'shared_w1', 'shared_b1', 'shared_w2', 'shared_b2', 'shared_act', 'expert_w1', 'expert_b1', 'expert_w2', 'expert_b2', 'expert_act')}
    del _L0_ffn_all
    return {'x': x, 'src': src, 'dst': dst, 'node_vec1': node_vec1, 'L0_gnn_f_w1': _L0_gnn_in['f_w1'], 'L0_gnn_f_b1': _L0_gnn_in['f_b1'], 'L0_gnn_f_w2': _L0_gnn_in['f_w2'], 'L0_gnn_f_b2': _L0_gnn_in['f_b2'], 'L0_gnn_s1_w': _L0_gnn_in['s1_w'], 'L0_gnn_s1_b': _L0_gnn_in['s1_b'], 'L0_gnn_b1_w': _L0_gnn_in['b1_w'], 'L0_gnn_b1_b': _L0_gnn_in['b1_b'], 'L0_gnn_wq': _L0_gnn_in['wq'], 'L0_gnn_bq': _L0_gnn_in['bq'], 'L0_gnn_wk': _L0_gnn_in['wk'], 'L0_gnn_bk': _L0_gnn_in['bk'], 'L0_gnn_wv': _L0_gnn_in['wv'], 'L0_gnn_bv': _L0_gnn_in['bv'], 'L0_gnn_wo': _L0_gnn_in['wo'], 'L0_gnn_bo': _L0_gnn_in['bo'], 'L0_gnn_s2_w': _L0_gnn_in['s2_w'], 'L0_gnn_s2_b': _L0_gnn_in['s2_b'], 'L0_gnn_b2_w': _L0_gnn_in['b2_w'], 'L0_gnn_b2_b': _L0_gnn_in['b2_b'], 'L0_gnn_m_w1': _L0_gnn_in['m_w1'], 'L0_gnn_m_b1': _L0_gnn_in['m_b1'], 'L0_gnn_m_w2': _L0_gnn_in['m_w2'], 'L0_gnn_m_b2': _L0_gnn_in['m_b2'], 'L0_mix_Wqkv': _L0_mix_in['Wqkv'], 'L0_mix_bqkv': _L0_mix_in['bqkv'], 'L0_mix_Pmat': _L0_mix_in['Pmat'], 'L0_mix_Wproj': _L0_mix_in['Wproj'], 'L0_mix_bproj': _L0_mix_in['bproj'], 'L0_mix_W1': _L0_mix_in['W1'], 'L0_mix_b1': _L0_mix_in['b1'], 'L0_mix_W2': _L0_mix_in['W2'], 'L0_mix_b2': _L0_mix_in['b2'], 'L0_mix_g1': _L0_mix_in['g1'], 'L0_mix_be1': _L0_mix_in['be1'], 'L0_mix_g2': _L0_mix_in['g2'], 'L0_mix_be2': _L0_mix_in['be2'], 'L0_ffn_gate_w': _L0_ffn_in['gate_w'], 'L0_ffn_gate_b': _L0_ffn_in['gate_b'], 'L0_ffn_shared_w1': _L0_ffn_in['shared_w1'], 'L0_ffn_shared_b1': _L0_ffn_in['shared_b1'], 'L0_ffn_shared_w2': _L0_ffn_in['shared_w2'], 'L0_ffn_shared_b2': _L0_ffn_in['shared_b2'], 'L0_ffn_shared_act': _L0_ffn_in['shared_act'], 'L0_ffn_expert_w1': _L0_ffn_in['expert_w1'], 'L0_ffn_expert_b1': _L0_ffn_in['expert_b1'], 'L0_ffn_expert_w2': _L0_ffn_in['expert_w2'], 'L0_ffn_expert_b2': _L0_ffn_in['expert_b2'], 'L0_ffn_expert_act': _L0_ffn_in['expert_act']}

def reference(x, src, dst, node_vec1, L0_gnn_f_w1, L0_gnn_f_b1, L0_gnn_f_w2, L0_gnn_f_b2, L0_gnn_s1_w, L0_gnn_s1_b, L0_gnn_b1_w, L0_gnn_b1_b, L0_gnn_wq, L0_gnn_bq, L0_gnn_wk, L0_gnn_bk, L0_gnn_wv, L0_gnn_bv, L0_gnn_wo, L0_gnn_bo, L0_gnn_s2_w, L0_gnn_s2_b, L0_gnn_b2_w, L0_gnn_b2_b, L0_gnn_m_w1, L0_gnn_m_b1, L0_gnn_m_w2, L0_gnn_m_b2, L0_mix_Wqkv, L0_mix_bqkv, L0_mix_Pmat, L0_mix_Wproj, L0_mix_bproj, L0_mix_W1, L0_mix_b1, L0_mix_W2, L0_mix_b2, L0_mix_g1, L0_mix_be1, L0_mix_g2, L0_mix_be2, L0_ffn_gate_w, L0_ffn_gate_b, L0_ffn_shared_w1, L0_ffn_shared_b1, L0_ffn_shared_w2, L0_ffn_shared_b2, L0_ffn_shared_act, L0_ffn_expert_w1, L0_ffn_expert_b1, L0_ffn_expert_w2, L0_ffn_expert_b2, L0_ffn_expert_act):
    import jax
    import jax.numpy as jnp

    def _L0_gnn_ref(latent_mesh_nodes, edge_index, noise_levels, f_w1, f_b1, f_w2, f_b2, s1_w, s1_b, b1_w, b1_b, wq, bq, wk, bk, wv, bv, wo, bo, s2_w, s2_b, b2_w, b2_b, m_w1, m_b1, m_w2, m_b2):
        import jax, jax.numpy as jnp
        import numpy as np
        N_NODES = 40962
        LATENT_DIM = 512
        N_EDGES = 81924
        NUM_BLOCKS = 4
        NUM_HEADS = 4
        NUM_FREQ = 32
        BASE_PERIOD = 16
        NOISE_EMB_DIM = 16
        EPS = 1e-05

        def _cond_layer_norm(x, cond, sw, sb, bw, bb):
            mu = jnp.mean(x, axis=-1, keepdims=True)
            var = jnp.var(x, axis=-1, keepdims=True)
            xn = (x - mu) * jax.lax.rsqrt(var + EPS)
            scale = cond @ sw + sb
            bias = cond @ bw + bb
            return xn * (1.0 + scale) + bias

        def _sparse_attention(x, src, dst, wq, bq, wk, bk, wv, bv, wo, bo):
            N, D = x.shape
            H, Dh = (NUM_HEADS, D // NUM_HEADS)
            q = (x @ wq + bq).reshape(N, H, Dh) * Dh ** (-0.5)
            k = (x @ wk + bk).reshape(N, H, Dh)
            v = (x @ wv + bv).reshape(N, H, Dh)
            scores = jnp.einsum('ehd,ehd->eh', q[src], k[dst])
            smax = jax.ops.segment_max(scores, src, num_segments=N)
            ex = jnp.exp(scores - smax[src])
            denom = jax.ops.segment_sum(ex, src, num_segments=N)
            attn = ex / denom[src]
            out = jax.ops.segment_sum(attn[:, :, None] * v[dst], src, num_segments=N)
            return out.reshape(N, D) @ wo + bo

        def _forward(x, edge_index, noise_levels, f_w1, f_b1, f_w2, f_b2, s1_w, s1_b, b1_w, b1_b, wq, bq, wk, bk, wv, bv, wo, bo, s2_w, s2_b, b2_w, b2_b, m_w1, m_b1, m_w2, m_b2):
            src, dst = (edge_index[0], edge_index[1])
            freqs = jnp.arange(1, NUM_FREQ + 1, dtype=x.dtype) * (2.0 * np.pi / BASE_PERIOD)
            ph = noise_levels * freqs
            emb = jnp.concatenate([jnp.sin(ph), jnp.cos(ph)], axis=-1)
            cond = jax.nn.silu(emb @ f_w1 + f_b1) @ f_w2 + f_b2
            for i in range(NUM_BLOCKS):
                y = _cond_layer_norm(x, cond, s1_w[i], s1_b[i], b1_w[i], b1_b[i])
                y = _sparse_attention(y, src, dst, wq[i], bq[i], wk[i], bk[i], wv[i], bv[i], wo[i], bo[i])
                x = x + y
                y = _cond_layer_norm(x, cond, s2_w[i], s2_b[i], b2_w[i], b2_b[i])
                y = jax.nn.relu(y @ m_w1[i] + m_b1[i]) @ m_w2[i] + m_b2[i]
                x = x + y
            return x
        return _forward(latent_mesh_nodes, edge_index, noise_levels, f_w1, f_b1, f_w2, f_b2, s1_w, s1_b, b1_w, b1_b, wq, bq, wk, bk, wv, bv, wo, bo, s2_w, s2_b, b2_w, b2_b, m_w1, m_b1, m_w2, m_b2)

    def _L0_mix_ref(x, Wqkv, bqkv, Pmat, Wproj, bproj, W1, b1, W2, b2, g1, be1, g2, be2):
        import jax, jax.numpy as jnp
        import numpy as np
        import math
        B, N, DIM = (4, 512, 512)
        HEADS, DH, NBF = (8, 64, 256)
        MLP_H = DIM * 2

        def layernorm(x, g, b, eps=1e-05):
            mu = jnp.mean(x, axis=-1, keepdims=True)
            var = jnp.mean(jnp.square(x - mu), axis=-1, keepdims=True)
            return (x - mu) * jax.lax.rsqrt(var + eps) * g + b

        def softmax_kernel(x, pmat):
            xp = jnp.einsum('bhnd,df->bhnf', x, pmat)
            xp = xp - jnp.max(xp, axis=-1, keepdims=True)
            return jnp.exp(xp) / math.sqrt(pmat.shape[-1])
        b, n, d = x.shape
        h = layernorm(x, g1, be1)
        qkv = h @ Wqkv + bqkv
        q, k, v = jnp.split(qkv, 3, axis=-1)
        to_heads = lambda t: t.reshape(b, n, HEADS, DH).transpose(0, 2, 1, 3)
        q, k, v = (to_heads(q), to_heads(k), to_heads(v))
        q_prime = softmax_kernel(q, Pmat)
        k_prime = softmax_kernel(k, Pmat)
        kv = jnp.einsum('bhnf,bhne->bhfe', k_prime, v)
        k_sum = jnp.sum(k_prime, axis=2) + 1e-06
        z = 1.0 / jnp.einsum('bhnf,bhf->bhn', q_prime, k_sum)[..., None]
        attn = jnp.einsum('bhnf,bhfe->bhne', q_prime, kv) * z
        attn = attn.transpose(0, 2, 1, 3).reshape(b, n, HEADS * DH)
        x = x + attn @ Wproj + bproj
        h2 = layernorm(x, g2, be2)
        mlp = jax.nn.gelu(h2 @ W1 + b1, approximate=False) @ W2 + b2
        return x + mlp

    def _L0_ffn_ref(x, gate_w, gate_b, shared_w1, shared_b1, shared_w2, shared_b2, shared_act, expert_w1, expert_b1, expert_w2, expert_b2, expert_act):
        import jax, jax.numpy as jnp
        import numpy as np
        B, S, D = (4, 256, 512)
        I = 384
        E = 16
        K = 2

        def _inv_softplus(v):
            return float(np.log(np.expm1(v)))

        def swiglu5(h, alpha, gate_scale, up_shift, gate_clamp_raw, up_clamp_raw):
            gate_clamp = jax.nn.softplus(gate_clamp_raw)
            up_clamp = jax.nn.softplus(up_clamp_raw)
            g = jnp.clip(h[..., ::2], -gate_clamp, gate_clamp)
            u = jnp.clip(h[..., 1::2], -up_clamp, up_clamp)
            return g * jax.nn.sigmoid(g * alpha) * gate_scale * (u + up_shift)
        shape = x.shape
        xf = x.reshape(-1, shape[-1])
        h = xf @ shared_w1 + shared_b1
        t = swiglu5(h, shared_act[0], shared_act[1], shared_act[2], shared_act[3], shared_act[4])
        z = t @ shared_w2 + shared_b2
        gate_logits = xf @ gate_w + gate_b
        gate_probs = jax.nn.softmax(gate_logits, -1)
        w, idx = jax.lax.top_k(gate_probs, K)
        w = w / jnp.sum(w, axis=-1, keepdims=True)
        cw = jnp.sum(jax.nn.one_hot(idx, E, dtype=xf.dtype) * w[..., None], axis=1)
        he = jnp.einsum('nd,edh->enh', xf, expert_w1) + expert_b1[:, None, :]
        a = expert_act
        te = swiglu5(he, a[:, 0, None, None], a[:, 1, None, None], a[:, 2, None, None], a[:, 3, None, None], a[:, 4, None, None])
        oe = jnp.einsum('enh,ehd->end', te, expert_w2) + expert_b2[:, None, :]
        y = jnp.einsum('ne,end->nd', cw, oe)
        return (y + z).reshape(shape)
    edge_index = jnp.stack([src, dst])
    xn = _layernorm(x, axis=-1)
    x = x + _L0_gnn_ref(xn, edge_index, node_vec1, L0_gnn_f_w1, L0_gnn_f_b1, L0_gnn_f_w2, L0_gnn_f_b2, L0_gnn_s1_w, L0_gnn_s1_b, L0_gnn_b1_w, L0_gnn_b1_b, L0_gnn_wq, L0_gnn_bq, L0_gnn_wk, L0_gnn_bk, L0_gnn_wv, L0_gnn_bv, L0_gnn_wo, L0_gnn_bo, L0_gnn_s2_w, L0_gnn_s2_b, L0_gnn_b2_w, L0_gnn_b2_b, L0_gnn_m_w1, L0_gnn_m_b1, L0_gnn_m_w2, L0_gnn_m_b2) + _L0_mix_ref(xn[None], L0_mix_Wqkv, L0_mix_bqkv, L0_mix_Pmat, L0_mix_Wproj, L0_mix_bproj, L0_mix_W1, L0_mix_b1, L0_mix_W2, L0_mix_b2, L0_mix_g1, L0_mix_be1, L0_mix_g2, L0_mix_be2)[0]
    x = x + _L0_ffn_ref(_layernorm(x, axis=-1)[None], L0_ffn_gate_w, L0_ffn_gate_b, L0_ffn_shared_w1, L0_ffn_shared_b1, L0_ffn_shared_w2, L0_ffn_shared_b2, L0_ffn_shared_act, L0_ffn_expert_w1, L0_ffn_expert_b1, L0_ffn_expert_w2, L0_ffn_expert_b2, L0_ffn_expert_act)[0]
    return x

_drawn_inputs = setup_inputs


def setup_inputs(seed=0):
    import zlib

    import numpy as np

    out = dict(_drawn_inputs(seed))
    spreads = {'L0_gnn_f_b1': (0.0, 0.8),
     'L0_gnn_f_b2': (0.0, 0.8),
     'L0_gnn_s1_b': (0.0, 0.8),
     'L0_gnn_b1_b': (0.0, 0.57),
     'L0_gnn_bq': (0.0, 0.8),
     'L0_gnn_bk': (0.0, 0.8),
     'L0_gnn_bv': (0.0, 0.1),
     'L0_gnn_bo': (0.0, 0.1),
     'L0_gnn_s2_b': (0.0, 0.8),
     'L0_gnn_b2_b': (0.0, 0.8),
     'L0_gnn_m_b1': (0.0, 0.381),
     'L0_gnn_m_b2': (0.0, 0.1),
     'L0_mix_bqkv': (0.0, 0.1),
     'L0_mix_bproj': (0.0, 0.1),
     'L0_mix_b1': (0.0, 0.346),
     'L0_mix_b2': (0.0, 0.1),
     'L0_mix_g1': (1.0, 0.2),
     'L0_mix_be1': (0.0, 0.1),
     'L0_mix_g2': (1.0, 0.2),
     'L0_mix_be2': (0.0, 0.347),
     'L0_ffn_gate_b': (0.0, 0.304),
     'L0_ffn_shared_b1': (0.0, 0.8),
     'L0_ffn_shared_b2': (0.0, 0.1),
     'L0_ffn_expert_b1': (0.0, 0.8),
     'L0_ffn_expert_b2': (0.0, 0.351)}
    factors = {'node_vec1': 8.0,
     'L0_gnn_f_w1': 8.0,
     'L0_gnn_f_w2': 8.0,
     'L0_gnn_s1_w': 8.0,
     'L0_gnn_b1_w': 8.0,
     'L0_gnn_wq': 8.0,
     'L0_gnn_wk': 8.0,
     'L0_gnn_s2_w': 8.0,
     'L0_gnn_b2_w': 8.0}
    for name, (base, spread) in spreads.items():
        noise = np.random.default_rng([zlib.crc32(name.encode()), seed]).standard_normal(out[name].shape)
        drawn = base * np.exp(spread * noise) if base else spread * noise
        out[name] = jnp.asarray(drawn.astype(out[name].dtype))
    for name, factor in factors.items():
        out[name] = (out[name] * factor).astype(out[name].dtype)
    return out
```

```python
from contextlib import ExitStack

import concourse.bass as bass
from concourse import mybir

F32 = mybir.dt.float32
F16 = mybir.dt.float16
I32 = mybir.dt.int32
U32 = mybir.dt.uint32
ALU = mybir.AluOpType
ACT = mybir.ActivationFunctionType
AX = mybir.AxisListType
ENG = mybir.EngineType
ds = bass.ds

N = 1250
D = 512
P = 125
NT = N // P
KC = D // 128
EPS = 1e-5
NOT_AN_EDGE = -1e30
BANK = 512
SPANS = [(0, 500), (500, 500), (1000, 250)]
GNN_LAYERS = 4
GNN_HEADS = 4
COND = 16
FREQ = 32
E_EDGES = 41250
EDGE_TILES = 8
EDGE_GROUPS = -(-E_EDGES // (128 * EDGE_TILES))
MIX_HEADS = 8
MIX_DH = 64
MIX_F = 256
MIX_H = 1024
EXPERTS = 16
FFN_I = 384
IC = FFN_I // 128


class Queue:

    def __init__(self, eng, sem):
        self.eng, self.sem = eng, sem
        self.count, self.seen = 0, {}

    def did(self, ins):
        ins.then_inc(self.sem, 1)
        self.count += 1
        return (self.sem, self.count)

    def need(self, *done):
        for d in done:
            if d is None:
                continue
            sem, value = d
            if self.seen.get(sem.name, 0) < value:
                self.eng.wait_ge(sem, value)
                self.seen[sem.name] = value


class Core:
    def __init__(self, nc, ctx):
        self.nc = nc
        mk = lambda name: ctx.enter_context(nc.semaphore(name))
        self.pe = Queue(nc.tensor, mk("pe_done"))
        self.dve = Queue(nc.vector, mk("dve_done"))
        self.act = Queue(nc.scalar, mk("act_done"))
        self.pool = Queue(nc.gpsimd, mk("pool_done"))
        self.sp = Queue(nc.sync, mk("sp_unused"))
        self.dma_sems = [mk(f"dma_done{i}") for i in range(24)]
        self.cleared = mk("group_cleared")
        self.queues = [self.pe, self.dve, self.act, self.pool, self.sp]
        sems = [q.sem for q in self.queues] + self.dma_sems + [self.cleared]
        self.first = min(s.num for s in sems)
        self.last = max(s.num for s in sems)
        assert self.last - self.first == len(sems) - 1
        self.dma_count = [0] * len(self.dma_sems)
        self.next_dma = 0
        self.bank_free = [None] * 8
        self.next_bank = 0

    def load(self, out, in_, *after, by=None):
        q = by or self.sp
        q.need(*after)
        n = self.next_dma
        self.next_dma = (n + 1) % len(self.dma_sems)
        if self.dma_count[n]:
            q.need((self.dma_sems[n], 16 * self.dma_count[n]))
        q.eng.dma_start(out, in_, allow_slow_non_contiguous=True).then_inc(self.dma_sems[n], 16)
        self.dma_count[n] += 1
        return (self.dma_sems[n], 16 * self.dma_count[n])

    def restart(self):
        for n, c in enumerate(self.dma_count):
            if c:
                self.sp.need((self.dma_sems[n], 16 * c))
        self.nc.all_engine_barrier(sems_to_clear=range(self.first, self.last + 1))
        for q in self.queues:
            q.count, q.seen = 0, {}
        self.dma_count = [0] * len(self.dma_sems)
        self.next_dma = 0
        self.bank_free = [None] * 8
        self.next_bank = 0

    def bank(self):
        b = self.next_bank
        self.next_bank = (b + 1) % 8
        self.pe.need(self.bank_free[b])
        return b


def build(nc, a, out):
    with ExitStack() as ctx:
        core = Core(nc, ctx)
        psum = ctx.enter_context(nc.psum_tensor("psum", [128, 8 * BANK], F32))
        ident = ctx.enter_context(nc.sbuf_tensor("ident", [128, 128], F32))
        xn_dram = nc.dram_tensor("xn_scratch", [N, D], F32)
        gnn_dram = nc.dram_tensor("gnn_scratch", [N, D], F32)
        sum_dram = nc.dram_tensor("sum_scratch", [N, D], F32)
        flag_dram = nc.dram_tensor("flag_scratch", [EDGE_GROUPS, NT], I32)
        core.psum, core.ident = psum, ident

        m = core.pool.did(nc.gpsimd.memset(ident[:], 0.0))
        core.pool.need(m)
        core.pool.did(nc.gpsimd.affine_select(out=ident[:], in_=ident[:], compare_op=ALU.not_equal, fill=1.0,
                                              base=0, pattern=[[-1, 128]], channel_multiplier=1))
        core.restart()
        with nc.sbuf_tensor("ln_count", [P, NT, N], F32) as ln_count:
            edge_counts(nc, core, a["src"], a["dst"], flag_dram, ln_count)
            gnn(nc, core, a, ln_count, xn_dram, gnn_dram)
        performer(nc, core, a, xn_dram, gnn_dram, sum_dram)
        moe(nc, core, a, sum_dram, out)
        core.restart()


def rows_view(dram):
    return dram[:, :].rearrange("(t p) d -> p t d", p=P)


def layer_norm_rows(nc, core, x, out, stat, mv, rstd, after=(), out_free=()):
    dve, act = core.dve, core.act
    for t in range(NT):
        dve.need(*after)
        s = dve.did(nc.vector.bn_stats(stat[:, t, :], x[:, t, :]))
    dve.need(s)
    for t in range(NT):
        s = dve.did(nc.vector.bn_aggr(mv[:, t, :], stat[:, t, :]))
    dve.need(s)
    s = dve.did(nc.vector.tensor_scalar(rstd[:, 0:NT], mv[:, :, 1], EPS, None, ALU.add))
    act.need(s)
    s = act.did(nc.scalar.activation(rstd[:, NT:2 * NT], rstd[:, 0:NT], ACT.Sqrt))
    dve.need(s)
    s = dve.did(nc.vector.reciprocal(rstd[:, 0:NT], rstd[:, NT:2 * NT]))
    dve.need(s, *out_free)
    return [dve.did(nc.vector.tensor_scalar(out[:, t, :], x[:, t, :], mv[:, t, 0:1], rstd[:, t:t + 1],
                                            ALU.subtract, ALU.mult)) for t in range(NT)]


def turn_tile(nc, core, src, n_chunks, done, width=128):
    pe = core.pe
    pe.need(done)
    b = core.bank()
    for c in range(n_chunks):
        ins = nc.tensor.transpose(core.psum[0:width, b * BANK + c * P:b * BANK + (c + 1) * P],
                                  src[:, c * width:(c + 1) * width], core.ident[0:P, 0:P])
    return b, pe.did(ins)


def turned(core, b, rows=128, n=KC):
    return core.psum[0:rows, b * BANK:b * BANK + n * P].rearrange("p (c n) -> p c n", n=P)


def rows_to_cols(nc, core, rows, cols, ready, free=()):
    out = []
    for t in range(NT):
        b, s = turn_tile(nc, core, rows[:, t, :], KC, ready[t])
        q = core.act if t % 2 else core.dve
        q.need(s, *free)
        dst = cols[:, :, t * P:(t + 1) * P]
        ins = nc.scalar.copy(dst, turned(core, b)) if t % 2 else nc.vector.tensor_copy(dst, turned(core, b))
        core.bank_free[b] = q.did(ins)
        out.append(core.bank_free[b])
    return out


def cols_product(nc, core, w, x, n_out, k_chunks, ready, evacuate):
    pe = core.pe
    for start, width in SPANS:
        pe.need(*ready)
        for o in range(n_out):
            b = core.bank()
            for k in range(k_chunks):
                ins = nc.tensor.matmul(core.psum[0:128, b * BANK:b * BANK + width], w(k, o), x(k, start, width),
                                       start=(k == 0), stop=(k == k_chunks - 1))
            s = pe.did(ins)
            core.bank_free[b] = evacuate(o, start, width, core.psum[0:128, b * BANK:b * BANK + width], s)


def rows_product(nc, core, x, w, k_chunks, ready, evacuate):
    pe = core.pe
    for t in range(NT):
        pe.need(*ready)
        b = core.bank()
        acc = core.psum[0:P, b * BANK:b * BANK + D]
        for k in range(k_chunks):
            ins = nc.tensor.matmul(acc, x(k, t * P, P), w(k), start=(k == 0), stop=(k == k_chunks - 1))
        core.bank_free[b] = evacuate(t, acc, pe.did(ins))


def edge_counts(nc, core, src, dst, flag_dram, ln_count):
    pe, dve, act, pool = core.pe, core.dve, core.act, core.pool
    T, G = EDGE_TILES, EDGE_GROUPS
    whole = G - 1
    rest = E_EDGES - whole * 128 * T
    rest_p, rest_e = rest // T, rest % T
    psum = core.psum
    with ExitStack() as ctx:
        sb = lambda name, shape, dt=F32: ctx.enter_context(nc.sbuf_tensor(name, shape, dt))
        ends_i = sb("ends_i", [128, 2, G, T], I32)
        ends = sb("ends", [128, 2, G, T])
        low = sb("low", [128, G, T])
        iota = sb("iota", [128, N], F16)
        edge_of = sb("block_starts", [G, 2, NT])
        cur = sb("cur", [128, 2, T])
        hot_src = sb("hot_src", [128, T, N], F16)
        hot_dst = sb("hot_dst", [128, T, 128], F16)
        zeros = sb("zeros", [128, 500], F16)
        span = sb("span", [128, 2, G])
        span_g = sb("span_g", [G, 2])
        meets = sb("meets", [G, 2, NT])
        flags_g = sb("flags_g", [G, NT], I32)
        flags = sb("flags", [1, G * NT], I32)
        none = sb("none", [P, NT, P])
        once = sb("once", [P, NT, P])

        fill = dve.did(nc.vector.memset(ends_i[:], -1))
        z = dve.did(nc.vector.memset(zeros[:], 0.0))
        it = pool.did(nc.gpsimd.iota(iota[:], [[1, N]], base=0, channel_multiplier=0,
                                     allow_small_or_imprecise_dtypes=True))
        lo = pool.did(nc.gpsimd.iota(edge_of[:, 0, :], [[P, NT]], base=0, channel_multiplier=0,
                                     allow_small_or_imprecise_dtypes=True))
        hi = pool.did(nc.gpsimd.iota(edge_of[:, 1, :], [[P, NT]], base=P - 1, channel_multiplier=0,
                                     allow_small_or_imprecise_dtypes=True))
        got = []
        for n, e in enumerate((src, dst)):
            got.append(core.load(ends_i[:, n, 0:whole, :],
                                 e[0:whole * 128 * T].rearrange("(g p t) -> p g t", p=128, t=T), fill))
            got.append(core.load(ends_i[0:rest_p, n, whole, :],
                                 e[whole * 128 * T:whole * 128 * T + rest_p * T].rearrange("(p t) -> p t", t=T)))
            if rest_e:
                got.append(core.load(ends_i[rest_p:rest_p + 1, n, whole, 0:rest_e],
                                     e[E_EDGES - rest_e:E_EDGES].rearrange("(p t) -> p t", t=rest_e)))
        dve.need(*got)
        e = dve.did(nc.vector.tensor_copy(ends[:], ends_i[:]))
        dve.need(e)
        s = dve.did(nc.vector.tensor_scalar(low[:], ends[:, 1], 0.0, 4096.0, ALU.is_lt, ALU.mult))
        dve.need(s)
        s = dve.did(nc.vector.tensor_tensor(low[:], low[:], ends[:, 1], ALU.add))
        dve.need(s)
        dve.did(nc.vector.tensor_reduce(span[:, 0, :], low[:], AX.X, ALU.min))
        s = dve.did(nc.vector.tensor_reduce(span[:, 1, :], ends[:, 1], AX.X, ALU.max))
        pe.need(s)
        for n in range(2):
            ins = nc.tensor.transpose(psum[0:G, n * 128:(n + 1) * 128], span[:, n, :], core.ident[:, :])
        s = pe.did(ins)
        dve.need(s)
        dve.did(nc.vector.tensor_reduce(span_g[:, 0:1], psum[0:G, 0:128], AX.X, ALU.min))
        s = dve.did(nc.vector.tensor_reduce(span_g[:, 1:2], psum[0:G, 128:256], AX.X, ALU.max))
        dve.need(s, lo, hi)
        dve.did(nc.vector.tensor_scalar(meets[:, 0, :], edge_of[:, 1, :], span_g[:, 0:1], None, ALU.is_ge))
        s = dve.did(nc.vector.tensor_scalar(meets[:, 1, :], edge_of[:, 0, :], span_g[:, 1:2], None, ALU.is_le))
        dve.need(s)
        s = dve.did(nc.vector.tensor_tensor(flags_g[:], meets[:, 0, :], meets[:, 1, :], ALU.mult))
        s = core.load(flag_dram[:, :], flags_g[:], s)
        s = core.load(flags[:, :], flag_dram[:, :].rearrange("g j -> (g j)").rearrange("(a f) -> a f", a=1), s)
        core.sp.need(s)
        core.restart()

        counts = psum[0:P, 0:3 * BANK]

        def block_counts(i):
            at = (i // 4) * BANK + (i % 4) * P
            return psum[0:P, at:at + P]

        with nc.Fori(0, NT) as j:
            for b in range(3):
                ins = nc.tensor.matmul(psum[0:P, b * BANK:b * BANK + 500], zeros[:, 0:P], zeros[:, :],
                                       start=True, stop=True)
            pe.did(ins)
            core.restart()
            with nc.Fori(0, G) as g:
                flag = nc.values_load(flags[0:1, ds(g * NT + j, 1)],
                                      min_val=0, max_val=1)
                hot = []
                with nc.If(flag == 1):
                    c = dve.did(nc.vector.tensor_copy(cur[:], ends[:, :, ds(g, 1), :].rearrange(
                        "p n g t -> p n (g t)")))
                    dve.need(c)
                    for t in range(T):
                        dve.did(nc.vector.tensor_scalar(hot_dst[:, t, 0:P], iota[:, ds(j * P, P)],
                                                        cur[:, 1, t:t + 1], None, ALU.is_equal))
                        hot.append(dve.did(nc.vector.tensor_scalar(hot_src[:, t, :], iota[:, :],
                                                                   cur[:, 0, t:t + 1], None, ALU.is_equal)))
                    nc.vector.wait_ge(pe.sem, 1)
                    nc.vector.sem_clear(range(core.first, core.first + 2))
                    nc.vector.sem_inc(core.cleared, 1)
                    for t in range(T):
                        pe.need(hot[t])
                        for i in range(NT):
                            ins = nc.tensor.matmul(block_counts(i), hot_src[:, t, i * P:(i + 1) * P],
                                                   hot_dst[:, t, 0:P], start=False, stop=(t == T - 1),
                                                   skip_group_check=True)
                    pe.did(ins)
                    nc.tensor.wait_ge(core.cleared, 1)
                    nc.tensor.sem_clear(core.cleared)
                pe.count = dve.count = 0
                pe.seen, dve.seen = {}, {}
            core.restart()
            for b, n in ((0, 4), (1, 4), (2, 2)):
                dve.did(nc.vector.tensor_scalar(
                    none[:, 4 * b:4 * b + n, :],
                    psum[0:P, b * BANK:b * BANK + n * P].rearrange("p (i j) -> p i j", j=P),
                    0.0, NOT_AN_EDGE, ALU.is_equal, ALU.mult))
                s = dve.did(nc.vector.tensor_scalar(
                    once[:, 4 * b:4 * b + n, :],
                    psum[0:P, b * BANK:b * BANK + n * P].rearrange("p (i j) -> p i j", j=P),
                    1.0, None, ALU.max))
            act.need(s)
            s = act.did(nc.scalar.activation(once[:], once[:], ACT.Ln))
            dve.need(s)
            dve.did(nc.vector.tensor_tensor(ln_count[:, :, ds(j * P, P)], once[:], none[:], ALU.add))
            core.restart()


def gnn(nc, core, a, ln_count, xn_dram, gnn_dram):
    pe, dve, act, pool = core.pe, core.dve, core.act, core.pool
    psum = core.psum
    H = GNN_HEADS
    Q_SCALE = float(128) ** -0.5
    with ExitStack() as ctx:
        sb = lambda name, shape, dt=F32: ctx.enter_context(nc.sbuf_tensor(name, shape, dt))
        x = sb("g_x", [P, NT, D])
        y_cols = sb("g_y_cols", [128, KC, N])
        q_cols = sb("g_q_cols", [128, KC, N])
        k_cols = sb("g_k_cols", [128, KC, N])
        v_rows = sb("g_v_rows", [P, NT, D])
        w = [sb(f"g_w{i}", [128, KC, D]) for i in range(3)]
        cond = sb("g_cond", [COND + 2, N])
        cond_w = sb("g_cond_w", [COND + 2, 4, D])
        prob = sb("g_prob", [P, 2, N])
        bias_rows = sb("g_bias_rows", [P, D])
        bias_cols = sb("g_bias_cols", [128, 3, KC])
        stat = sb("g_stat", [P, NT, 6])
        mv = sb("g_mv", [P, NT, 2])
        rstd = sb("g_rstd", [P, 2 * NT])
        row_max = sb("g_row_max", [P, 2, 4])
        f_w1 = sb("g_f_w1", [2 * FREQ, COND])
        f_w2 = sb("g_f_w2", [COND, COND])
        f_b = sb("g_f_b", [COND, 2])
        freq = sb("g_freq", [2 * FREQ, 2])
        turned_prob = y_cols[0:P, :, :].rearrange("p a b -> p (a b)").rearrange("p (u j i) -> p u j i", u=2, i=2 * P)

        noise = q_cols[0:2 * FREQ, 0, :]
        emb = q_cols[0:2 * FREQ, 1, :]
        whole_turns = q_cols[0:2 * FREQ, 2, :]
        hidden = q_cols[0:COND, 3, :]
        gate = k_cols[0:COND, 0, :]
        f = pool.did(nc.gpsimd.iota(freq[0:FREQ, 0:1], [[0, 1]], base=1, channel_multiplier=1,
                                    allow_small_or_imprecise_dtypes=True))
        f2 = pool.did(nc.gpsimd.iota(freq[FREQ:2 * FREQ, 0:1], [[0, 1]], base=1, channel_multiplier=1,
                                     allow_small_or_imprecise_dtypes=True))
        dve.did(nc.vector.memset(freq[0:FREQ, 1:2], 0.0))
        dve.did(nc.vector.memset(freq[FREQ:2 * FREQ, 1:2], 0.25))
        ones = dve.did(nc.vector.memset(cond[:], 1.0))
        dve.did(nc.vector.memset(cond_w[:, 1, :], 0.0))
        dve.did(nc.vector.memset(cond_w[:, 3, :], 0.0))
        dve.did(nc.vector.memset(cond_w[:, 0, :], 1.0))
        s = dve.did(nc.vector.memset(cond_w[:, 2, :], 1.0))
        got_x = core.load(x[:], a["x"].rearrange("(t p) d -> p t d", p=P))
        got_n = core.load(noise, a["node_vec1"].rearrange("n a -> (n a)").partition_broadcast(2 * FREQ))
        got_f = [core.load(f_w1[:], a["L0_gnn_f_w1"]), core.load(f_w2[:], a["L0_gnn_f_w2"]),
                 core.load(f_b[:, 0:1], a["L0_gnn_f_b1"].rearrange("(p a) -> p a", a=1)),
                 core.load(f_b[:, 1:2], a["L0_gnn_f_b2"].rearrange("(p a) -> p a", a=1))]
        dve.need(f, f2)
        s = dve.did(nc.vector.tensor_scalar(freq[:, 0:1], freq[:, 0:1], 1.0 / 16.0, None, ALU.mult))
        dve.need(got_n, s)
        s = dve.did(nc.vector.tensor_scalar(emb, noise, freq[:, 0:1], freq[:, 1:2], ALU.mult, ALU.add))
        dve.need(s)
        s = dve.did(nc.vector.tensor_scalar(whole_turns, emb, 12582912.0, None, ALU.add))
        dve.need(s)
        s = dve.did(nc.vector.tensor_scalar(whole_turns, whole_turns, -12582912.0, None, ALU.add))
        dve.need(s)
        s = dve.did(nc.vector.tensor_tensor(emb, emb, whole_turns, ALU.subtract))
        act.need(s)
        s = act.did(nc.scalar.activation(emb, emb, ACT.Sin, scale=6.2831850))
        pe.need(s, *got_f)
        act.need(*got_f)
        for n, (start, width) in enumerate(SPANS):
            ins = nc.tensor.matmul(psum[0:COND, n * BANK:n * BANK + width], f_w1[:, :], emb[:, start:start + width],
                                   start=True, stop=True)
            s = pe.did(ins)
            act.need(s)
            act.did(nc.scalar.activation(hidden[:, start:start + width], psum[0:COND, n * BANK:n * BANK + width],
                                         ACT.Identity, bias=f_b[:, 0:1]))
            act.did(nc.scalar.activation(gate[:, start:start + width], psum[0:COND, n * BANK:n * BANK + width],
                                         ACT.Sigmoid, bias=f_b[:, 0:1]))
        dve.need((act.sem, act.count))
        s = dve.did(nc.vector.tensor_tensor(hidden, hidden, gate, ALU.mult))
        pe.need(s)
        dve.need(*got_f)
        for n, (start, width) in enumerate(SPANS):
            ins = nc.tensor.matmul(psum[0:COND, (3 + n) * BANK:(3 + n) * BANK + width], f_w2[:, :],
                                   hidden[:, start:start + width], start=True, stop=True)
            s = pe.did(ins)
            dve.need(s)
            dve.did(nc.vector.tensor_scalar(cond[0:COND, start:start + width],
                                            psum[0:COND, (3 + n) * BANK:(3 + n) * BANK + width],
                                            f_b[:, 1:2], None, ALU.add))
        done = layer_norm_rows(nc, core, x, x, stat, mv, rstd, after=(got_x,))
        core.load(rows_view(xn_dram), x[:], done[-1])
        core.restart()

        def weight_rows(name, layer):
            return a[name][ds(layer, 1), :, :].rearrange("l (c p) o -> p (l c) o", p=128)

        def bias_row(name, layer, n=P):
            return a[name][ds(layer, 1), :].rearrange("l o -> (l o)").partition_broadcast(n)

        def conditioned_norm(which, got, x_free_rows):
            y = v_rows
            done = layer_norm_rows(nc, core, x, y, stat, mv, rstd)
            pe.need(*got)
            out = []
            for t in range(NT):
                pair = []
                for n in range(2):
                    b = core.bank()
                    ins = nc.tensor.matmul(psum[0:P, b * BANK:b * BANK + D], cond[:, t * P:(t + 1) * P],
                                           cond_w[:, 2 * which + n, :], start=True, stop=True)
                    pair.append((b, pe.did(ins)))
                dve.need(done[t], pair[0][1])
                b = pair[0][0]
                s = dve.did(nc.vector.tensor_tensor(y[:, t, :], y[:, t, :], psum[0:P, b * BANK:b * BANK + D],
                                                    ALU.mult))
                core.bank_free[b] = s
                b = pair[1][0]
                dve.need(s, pair[1][1])
                s = dve.did(nc.vector.tensor_tensor(y[:, t, :], y[:, t, :], psum[0:P, b * BANK:b * BANK + D],
                                                    ALU.add))
                core.bank_free[b] = s
                out.append(s)
                if t >= 1:
                    turn(t - 1, out[t - 1])
            turn(NT - 1, out[NT - 1])
            return (act.sem, act.count)

        def turn(t, ready):
            b, s = turn_tile(nc, core, v_rows[:, t, :], KC, ready)
            act.need(s)
            core.bank_free[b] = act.did(nc.scalar.copy(y_cols[:, :, t * P:(t + 1) * P], turned(core, b)))

        with nc.Fori(0, GNN_LAYERS) as layer:
            got_c = []
            for n, (wn, bn) in enumerate((("s1_w", "s1_b"), ("b1_w", "b1_b"), ("s2_w", "s2_b"), ("b2_w", "b2_b"))):
                got_c.append(core.load(cond_w[0:COND, n, :], a["L0_gnn_" + wn][ds(layer, 1), :, :].rearrange(
                    "l c d -> (l c) d")))
                got_c.append(core.load(cond_w[COND:COND + 1, n, :], a["L0_gnn_" + bn][ds(layer, 1), :]))
            got_w = {}
            for n, name in enumerate(("wq", "wk", "wv")):
                got_w[name] = core.load(w[n][:], weight_rows("L0_gnn_" + name, layer))
            got_bc = [core.load(bias_cols[:, n, :], a["L0_gnn_" + name][ds(layer, 1), :].rearrange(
                "l (c p) -> p (l c)", p=128)) for n, name in enumerate(("bq", "bk", "m_b1"))]
            got_bv = core.load(bias_rows[:, :], bias_row("L0_gnn_bv", layer))

            y_ready = conditioned_norm(0, got_c, None)
            act.need(*got_bc)
            dve.need(*got_bc)
            s = act.did(nc.scalar.mul(bias_cols[:, 0, :], bias_cols[:, 0, :], Q_SCALE))
            act.need(s)

            def to_q(o, start, width, acc, s):
                act.need(s)
                return act.did(nc.scalar.activation(q_cols[:, o, start:start + width], acc, ACT.Identity,
                                                    bias=bias_cols[:, 0, o:o + 1], scale=Q_SCALE))

            def to_k(o, start, width, acc, s):
                dve.need(s)
                return dve.did(nc.vector.tensor_scalar(k_cols[:, o, start:start + width], acc,
                                                       bias_cols[:, 1, o:o + 1], None, ALU.add))

            def to_v(t, acc, s):
                dve.need(s)
                return dve.did(nc.vector.tensor_tensor(v_rows[:, t, :], acc, bias_rows[:, :], ALU.add))

            ys = lambda k, start, width: y_cols[:, k, start:start + width]
            cols_product(nc, core, lambda k, o: w[0][:, k, o * 128:(o + 1) * 128], ys, KC, KC,
                         (y_ready, got_w["wq"]), to_q)
            q_done, pe_q = (act.sem, act.count), (pe.sem, pe.count)
            got_wo = core.load(w[0][:], weight_rows("L0_gnn_wo", layer), pe_q)
            cols_product(nc, core, lambda k, o: w[1][:, k, o * 128:(o + 1) * 128], ys, KC, KC,
                         (y_ready, got_w["wk"]), to_k)
            k_done, pe_k = (dve.sem, dve.count), (pe.sem, pe.count)
            got_m1 = core.load(w[1][:], weight_rows("L0_gnn_m_w1", layer), pe_k)
            dve.need(got_bv)
            rows_product(nc, core, ys, lambda k: w[2][:, k, :], KC, (y_ready, got_w["wv"]), to_v)
            v_done, pe_v = (dve.sem, dve.count), (pe.sem, pe.count)
            got_m2 = core.load(w[2][:], weight_rows("L0_gnn_m_w2", layer), pe_v)
            got_bo = core.load(bias_rows[:, :], bias_row("L0_gnn_bo", layer), v_done)
            pool.need(got_bo, v_done)
            for t in range(NT):
                x_bo = pool.did(nc.gpsimd.tensor_tensor(x[:, t, :], x[:, t, :], bias_rows[:, :], ALU.add))
            got_b2 = core.load(bias_rows[:, :], bias_row("L0_gnn_m_b2", layer), x_bo)

            steps = [(h, t) for h in range(H) for t in range(NT)]
            soft = {}
            scores_free = core.bank_free[:]
            turn_free = [core.bank_free[3:6]]
            out_free = [core.bank_free[6], core.bank_free[7]]
            prob_free = [None, None]
            pair_done, out_done = {}, {}
            pe.need(*core.bank_free)
            s_free = None

            def scores(n):
                nonlocal s_free
                h, t = steps[n]
                u = n % 2
                pe.need(q_done, k_done, s_free)
                for start in range(0, N, BANK):
                    width = min(BANK, N - start)
                    ins = nc.tensor.matmul(psum[0:P, start:start + width], q_cols[:, h, t * P:(t + 1) * P],
                                           k_cols[:, h, start:start + width], start=True, stop=True)
                s = pe.did(ins)
                dve.need(s, prob_free[u])
                s = s_free = dve.did(nc.vector.tensor_tensor_reduce(
                    prob[:, u, :], psum[0:P, 0:N], ln_count[:, t, :], 1.0, NOT_AN_EDGE / 10, ALU.add, ALU.max,
                    row_max[:, u, 0:1]))
                dve.need(s)
                s = dve.did(nc.vector.tensor_scalar(row_max[:, u, 1:2], row_max[:, u, 0:1], -1.0, None, ALU.mult))
                act.need(s)
                s = act.did(nc.scalar.activation(prob[:, u, :], prob[:, u, :], ACT.Exp, bias=row_max[:, u, 1:2],
                                                 accum_out=row_max[:, u, 2:3]))
                return s

            def normalise(n, s):
                u = n % 2
                dve.need(s)
                s = dve.did(nc.vector.tensor_scalar(row_max[:, u, 2:3], row_max[:, u, 2:3], 1e-30, None, ALU.max))
                dve.need(s)
                s = dve.did(nc.vector.reciprocal(row_max[:, u, 3:4], row_max[:, u, 2:3]))
                dve.need(s)
                return dve.did(nc.vector.tensor_scalar(prob[:, u, :], prob[:, u, :], row_max[:, u, 3:4], None,
                                                       ALU.mult))

            def turn_probs(n, ready):
                u, g = n % 2, n // 2
                half = (n % 2) * P
                pe.need(ready, *turn_free[0])
                frees = []
                for b, j0, nj in ((3, 0, 4), (4, 4, 4), (5, 8, 2)):
                    for j in range(nj):
                        ins = nc.tensor.transpose(psum[0:P, b * BANK + j * P:b * BANK + (j + 1) * P],
                                                  prob[:, u, (j0 + j) * P:(j0 + j + 1) * P],
                                                  core.ident[0:P, 0:P])
                    s = pe.did(ins)
                    q = dve if b == 4 else act
                    q.need(s, out_done.get(g - 2))
                    dst = turned_prob[:, g % 2, j0:j0 + nj, half:half + P]
                    src_ = psum[0:P, b * BANK:b * BANK + nj * P].rearrange("p (j i) -> p j i", i=P)
                    ins = nc.vector.tensor_copy(dst, src_) if b == 4 else nc.scalar.copy(dst, src_)
                    frees.append(q.did(ins))
                prob_free[u] = s
                turn_free[0] = frees
                pair_done[g] = (pair_done.get(g) or []) + frees

            def weigh(g, part):
                h, t = steps[2 * g]
                b = 6 + g % 2
                pe.need(v_done, *pair_done[g])
                if part == 0:
                    pe.need(out_free[g % 2])
                for j in range(5 * part, 5 * part + 5):
                    ins = nc.tensor.matmul(psum[0:128, b * BANK:b * BANK + 2 * P],
                                           v_rows[:, j, h * 128:(h + 1) * 128], turned_prob[:, g % 2, j, :],
                                           start=(j == 0), stop=(j == NT - 1))
                s = pe.did(ins)
                if part == 1:
                    out_done[g] = s
                    act.need(s)
                    out_free[g % 2] = act.did(nc.scalar.copy(q_cols[:, h, t * P:(t + 2) * P],
                                                             psum[0:128, b * BANK:b * BANK + 2 * P]))

            act.need(pe_v)
            dve.need(pe_v)
            pending = {}
            last = len(steps)
            for n in range(last + 1):
                if n < last:
                    pending[n] = scores(n)
                g = (n - 3) // 2
                if g >= 0 and n <= last:
                    if (n - 3) % 2 == 0:
                        weigh(g, 0)
                    else:
                        weigh(g, 1)
                if n >= 1:
                    turn_probs(n - 1, normalise(n - 1, pending[n - 1]))
            weigh(last // 2 - 2, 1) if out_done.get(last // 2 - 2) is None else None
            weigh(last // 2 - 1, 0)
            weigh(last // 2 - 1, 1)
            o_done = (act.sem, act.count)
            core.bank_free = [s_free] * 3 + turn_free[0] + out_free
            core.next_bank = 0

            def add_to_x(t, acc, s):
                dve.need(s, x_bo)
                return dve.did(nc.vector.tensor_tensor(x[:, t, :], x[:, t, :], acc, ALU.add))

            os_ = lambda k, start, width: q_cols[:, k, start:start + width]
            rows_product(nc, core, os_, lambda k: w[0][:, k, :], KC, (o_done, got_wo), add_to_x)
            dve.need((dve.sem, dve.count))

            y_ready = conditioned_norm(1, got_c, None)
            pool.need(got_b2, y_ready, (dve.sem, dve.count))
            for t in range(NT):
                x_b2 = pool.did(nc.gpsimd.tensor_tensor(x[:, t, :], x[:, t, :], bias_rows[:, :], ALU.add))

            def to_hidden(o, start, width, acc, s):
                act.need(s)
                return act.did(nc.scalar.activation(k_cols[:, o, start:start + width], acc, ACT.Relu,
                                                    bias=bias_cols[:, 2, o:o + 1]))

            def add_mlp(t, acc, s):
                dve.need(s, x_b2)
                return dve.did(nc.vector.tensor_tensor(x[:, t, :], x[:, t, :], acc, ALU.add))

            cols_product(nc, core, lambda k, o: w[1][:, k, o * 128:(o + 1) * 128], ys, KC, KC,
                         (y_ready, got_m1), to_hidden)
            h_done = (act.sem, act.count)
            rows_product(nc, core, lambda k, s0, n: k_cols[:, k, s0:s0 + n], lambda k: w[2][:, k, :], KC,
                         (h_done, got_m2), add_mlp)
            core.restart()
        core.load(rows_view(gnn_dram), x[:])
        core.restart()


def performer(nc, core, a, xn_dram, gnn_dram, sum_dram):
    pe, dve, act, pool = core.pe, core.dve, core.act, core.pool
    psum = core.psum
    H, DH, F = MIX_HEADS, MIX_DH, MIX_F
    K_SUM_SMALL = 1e-6 * 16.0
    with ExitStack() as ctx:
        sb = lambda name, shape, dt=F32: ctx.enter_context(nc.sbuf_tensor(name, shape, dt))
        x = sb("p_x", [P, NT, D])
        h_rows = sb("p_h_rows", [P, NT, D])
        cols = sb("p_cols", [128, KC, N])
        v_rows = sb("p_v_rows", [P, NT, H, DH + 1])
        q_cols = sb("p_q_cols", [128, KC, N])
        k_cols = sb("p_k_cols", [128, KC, N])
        w = [sb(f"p_w{i}", [128, KC, D]) for i in range(4)]
        pmat = sb("p_pmat", [128, F])
        kf = sb("p_kf", [P, 4, F])
        qf_cols = sb("p_qf_cols", [128, 2, 2, P])
        kv = sb("p_kv", [128, H, 2, DH + 1])
        bias_rows = sb("p_bias_rows", [P, 3, D])
        gb = sb("p_gb", [128, 4, KC])
        bqk = sb("p_bqk", [128, 2, KC])
        b1 = sb("p_b1", [128, MIX_H // 128])
        stat = sb("p_stat", [P, NT, 6])
        mv = sb("p_mv", [P, NT, 2])
        rstd = sb("p_rstd", [P, 2 * NT])
        mx = sb("p_mx", [P, 8])
        rden = sb("p_rden", [P, 4])

        got_x = core.load(x[:], rows_view(xn_dram))
        wqkv = a["L0_mix_Wqkv"].rearrange("(c p) o -> p c o", p=128)
        got_w = [core.load(w[n][:], wqkv[:, :, n * D:(n + 1) * D]) for n in range(3)]
        got_p = [core.load(pmat[0:64, :], a["L0_mix_Pmat"]), core.load(pmat[64:128, :], a["L0_mix_Pmat"])]
        cvec = lambda v: v.rearrange("(c p) -> p c", p=128)
        got_gb = [core.load(gb[:, n, :], cvec(a["L0_mix_" + s])) for n, s in enumerate(("g1", "be1", "g2", "be2"))]
        got_bqk = [core.load(bqk[:, n, :], cvec(a["L0_mix_bqkv"][n * D:(n + 1) * D])) for n in range(2)]
        got_b1 = core.load(b1[:, :], cvec(a["L0_mix_b1"]))
        got_br = [core.load(bias_rows[:, 0, :], a["L0_mix_bqkv"][2 * D:3 * D].partition_broadcast(P)),
                  core.load(bias_rows[:, 1, :], a["L0_mix_bproj"].partition_broadcast(P)),
                  core.load(bias_rows[:, 2, :], a["L0_mix_b2"].partition_broadcast(P))]
        got_wp = core.load(w[3][:], a["L0_mix_Wproj"].rearrange("(c p) o -> p c o", p=128))
        act.need(*got_gb, *got_bqk, got_b1)
        dve.need(*got_bqk, *got_br)

        def norm_to_cols(which, after):
            done = layer_norm_rows(nc, core, x, h_rows, stat, mv, rstd, after=after)
            for t in range(NT):
                b, s = turn_tile(nc, core, h_rows[:, t, :], KC, done[t])
                act.need(s)
                for c in range(KC):
                    ins = nc.scalar.activation(cols[:, c, t * P:(t + 1) * P],
                                               psum[0:128, b * BANK + c * P:b * BANK + (c + 1) * P], ACT.Identity,
                                               bias=gb[:, 2 * which + 1, c:c + 1], scale=gb[:, 2 * which, c:c + 1])
                    core.bank_free[b] = act.did(ins)
            return core.bank_free[b]

        ready = norm_to_cols(0, (got_x,))
        cs = lambda k, start, width: cols[:, k, start:start + width]

        def to_q(o, start, width, acc, s):
            act.need(s)
            return act.did(nc.scalar.activation(q_cols[:, o, start:start + width], acc, ACT.Identity,
                                                bias=bqk[:, 0, o:o + 1]))

        def to_k(o, start, width, acc, s):
            dve.need(s)
            return dve.did(nc.vector.tensor_scalar(k_cols[:, o, start:start + width], acc, bqk[:, 1, o:o + 1],
                                                   None, ALU.add))

        def to_v(t, acc, s):
            dve.need(s)
            return dve.did(nc.vector.tensor_tensor(v_rows[:, t, :, 0:DH], acc.rearrange("p (h d) -> p h d", d=DH),
                                                   bias_rows[:, 0, :].rearrange("p (h d) -> p h d", d=DH), ALU.add))

        one = dve.did(nc.vector.memset(v_rows[:, :, :, DH:DH + 1], 1.0))
        for n, evac in ((1, to_k), (0, to_q)):
            cols_product(nc, core, lambda k, o: w[n][:, k, o * 128:(o + 1) * 128], cs, KC, KC,
                         (ready, got_w[n]), evac)
        rows_product(nc, core, cs, lambda k: w[2][:, k, :], KC, (ready, got_w[2]), to_v)
        qkv_done = [(act.sem, act.count), (dve.sem, dve.count)]
        w1_view = a["L0_mix_W1"].rearrange("(c p) o -> p c o", p=128)
        w2_view = a["L0_mix_W2"].rearrange("(c p) o -> p c o", p=128)
        pe_qkv = (pe.sem, pe.count)
        got_w1 = [core.load(w[0][:], w1_view[:, :, 0:D], pe_qkv), core.load(w[1][:], w1_view[:, :, D:2 * D], pe_qkv)]

        kf_free = [None] * 4

        def feature_map(src, h, t, slot):
            r0 = (h % 2) * DH
            b = core.bank()
            pe.need(*qkv_done, *got_p)
            s = pe.did(nc.tensor.matmul(psum[0:P, b * BANK:b * BANK + F],
                                        src[r0:r0 + DH, h // 2, t * P:(t + 1) * P], pmat[r0:r0 + DH, :],
                                        start=True, stop=True))
            dve.need(s, kf_free[slot])
            s = dve.did(nc.vector.tensor_reduce(mx[:, slot:slot + 1], psum[0:P, b * BANK:b * BANK + F], AX.X,
                                                ALU.max, negate=True))
            act.need(s, kf_free[slot])
            core.bank_free[b] = act.did(nc.scalar.activation(kf[:, slot, :], psum[0:P, b * BANK:b * BANK + F],
                                                             ACT.Exp, bias=mx[:, slot:slot + 1]))
            return core.bank_free[b]

        LAG = 2
        work = [(h, t) for h in range(H) for t in range(NT)]
        got_f = {}
        held = {}
        core.next_bank = 0
        free_acc = {6: core.bank_free[6], 7: core.bank_free[7]}
        for n in range(len(work) + LAG):
            if n < len(work):
                if core.next_bank >= 6:
                    core.next_bank = 0
                got_f[n] = feature_map(k_cols, *work[n], n % 4)
            if n >= LAG:
                m = n - LAG
                h, t = work[m]
                pe.need(got_f[m])
                for half in range(2):
                    if t == 0:
                        pe.need(free_acc[6 + half])
                    ins = nc.tensor.matmul(psum[0:128, (6 + half) * BANK:(6 + half) * BANK + DH + 1],
                                           kf[:, m % 4, half * 128:(half + 1) * 128], v_rows[:, t, h, :],
                                           start=(t == 0), stop=(t == NT - 1))
                s = pe.did(ins)
                kf_free[m % 4] = s
                if t == NT - 1:
                    for half in range(2):
                        dve.need(s)
                        free_acc[6 + half] = dve.did(nc.vector.tensor_copy(
                            kv[:, h, half, :], psum[0:128, (6 + half) * BANK:(6 + half) * BANK + DH + 1]))
        kv_done = free_acc[7]
        dve.need(kv_done)
        kv_done = dve.did(nc.vector.tensor_scalar(kv[:, :, :, DH:DH + 1], kv[:, :, :, DH:DH + 1], K_SUM_SMALL,
                                                  None, ALU.add))
        core.bank_free[6], core.bank_free[7] = free_acc[6], free_acc[7]

        work = [(h, t) for t in range(NT) for h in range(H)]
        qf_free = [None, None]
        qf_ready = {}
        tile_done = {}
        for n in range(len(work) + 2 * LAG):
            if n < len(work):
                h, t = work[n]
                got_f[n] = feature_map(q_cols, h, t, n % 4)
            if LAG <= n < len(work) + LAG:
                m = n - LAG
                b, s = turn_tile(nc, core, kf[:, m % 4, :], 2, got_f[m])
                kf_free[m % 4] = s
                q = act
                q.need(s, qf_free[m % 2])
                core.bank_free[b] = q.did(nc.scalar.copy(qf_cols[:, m % 2, :, :], turned(core, b, n=2)))
                qf_ready[m] = core.bank_free[b]
            if n >= LAG + 1 and n - LAG - 1 < len(work):
                m = n - LAG - 1
                h, t = work[m]
                b = core.bank()
                pe.need(qf_ready[m], kv_done)
                for half in range(2):
                    ins = nc.tensor.matmul(psum[0:P, b * BANK:b * BANK + DH + 1], qf_cols[:, m % 2, half, :],
                                           kv[:, h, half, :], start=(half == 0), stop=(half == 1))
                s = pe.did(ins)
                qf_free[m % 2] = s
                dve.need(s)
                s = dve.did(nc.vector.reciprocal(rden[:, m % 4:m % 4 + 1],
                                                 psum[0:P, b * BANK + DH:b * BANK + DH + 1]))
                dve.need(s)
                core.bank_free[b] = dve.did(nc.vector.tensor_scalar(
                    h_rows[:, t, h * DH:(h + 1) * DH], psum[0:P, b * BANK:b * BANK + DH], rden[:, m % 4:m % 4 + 1],
                    None, ALU.mult))
                tile_done[t] = core.bank_free[b]

        pool.need(*got_br, *qkv_done)
        for t in range(NT):
            x_b = pool.did(nc.gpsimd.tensor_tensor(x[:, t, :], x[:, t, :], bias_rows[:, 1, :], ALU.add))
        rows_to_cols(nc, core, h_rows, cols, tile_done)
        c_done = [(act.sem, act.count), (dve.sem, dve.count)]

        def add_to_x(t, acc, s):
            dve.need(s, x_b)
            return dve.did(nc.vector.tensor_tensor(x[:, t, :], x[:, t, :], acc, ALU.add))

        rows_product(nc, core, cs, lambda k: w[3][:, k, :], KC, (*c_done, got_wp), add_to_x)
        proj_done = (pe.sem, pe.count)
        got_w2 = [core.load(w[2][:], w2_view[:, 0:KC, :], proj_done), core.load(w[3][:], w2_view[:, KC:2 * KC, :], proj_done)]
        ready = norm_to_cols(1, ((dve.sem, dve.count),))
        pool.need(ready, (dve.sem, dve.count))
        for t in range(NT):
            x_b = pool.did(nc.gpsimd.tensor_tensor(x[:, t, :], x[:, t, :], bias_rows[:, 2, :], ALU.add))

        def to_hidden(o, start, width, acc, s):
            act.need(s)
            dst = q_cols if o < KC else k_cols
            return act.did(nc.scalar.activation(dst[:, o % KC, start:start + width], acc, ACT.Gelu,
                                                bias=b1[:, o:o + 1]))

        cols_product(nc, core, lambda k, o: w[o // KC][:, k, (o % KC) * 128:(o % KC + 1) * 128], cs, 2 * KC, KC,
                     (ready, *got_w1), to_hidden)
        h_done = (act.sem, act.count)
        cols_read = (pe.sem, pe.count)
        h2 = v_rows[:, :, :, :].rearrange("p t h d -> p (t h d)")[:, 0:NT * D].rearrange("p (t d) -> p t d", d=D)
        got_g = core.load(h_rows[:], rows_view(gnn_dram), cols_read)
        got_i = core.load(h2, a["x"].rearrange("(t p) d -> p t d", p=P), cols_read)
        pool.need(got_g, got_i)
        for t in range(NT):
            other = pool.did(nc.gpsimd.tensor_tensor(h_rows[:, t, :], h_rows[:, t, :], h2[:, t, :], ALU.add))
        pool.need(other, x_b)
        for t in range(NT):
            x_b = pool.did(nc.gpsimd.tensor_tensor(x[:, t, :], x[:, t, :], h_rows[:, t, :], ALU.add))
        rows_product(nc, core, lambda k, s0, n: (q_cols if k < KC else k_cols)[:, k % KC, s0:s0 + n],
                     lambda k: w[2 + k // KC][:, k % KC, :], 2 * KC, (h_done, *got_w2), add_to_x)
        core.load(rows_view(sum_dram), x[:], (dve.sem, dve.count))
        core.restart()


def moe(nc, core, a, sum_dram, out):
    pe, dve, act, pool = core.pe, core.dve, core.act, core.pool
    psum = core.psum
    with ExitStack() as ctx:
        sb = lambda name, shape, dt=F32: ctx.enter_context(nc.sbuf_tensor(name, shape, dt))
        x = sb("m_x", [P, NT, D])
        n_rows = sb("m_n_rows", [P, NT, D])
        cols = sb("m_cols", [128, KC, N])
        w1 = sb("m_w1", [128, KC, 2 * FFN_I])
        w2 = sb("m_w2", [128, IC, D])
        hidden = sb("m_hidden", [128, IC, N])
        scratch = [sb(f"m_scratch{i}", [128, 3, 500]) for i in range(2)]
        gate_w = sb("m_gate_w", [128, KC, EXPERTS])
        gate_b = sb("m_gate_b", [P, EXPERTS])
        cw = sb("m_cw", [P, NT, EXPERTS + 1])
        cw_cur = sb("m_cw_cur", [P, NT])
        cw_cols = sb("m_cw_cols", [EXPERTS, N])
        b2 = sb("m_b2", [EXPERTS, D])
        shared_b2 = sb("m_shared_b2", [P, D])
        b1 = sb("m_b1", [128, 2, IC])
        actp = sb("m_act", [128, 5])
        clamp = sb("m_clamp", [128, 4])
        stat = sb("m_stat", [P, NT, 6])
        mv = sb("m_mv", [P, NT, 2])
        rstd = sb("m_rstd", [P, 2 * NT])
        logit = sb("m_logit", [P, NT, EXPERTS])
        top = sb("m_top", [P, NT, 8])
        top_i = sb("m_top_i", [P, NT, 8], U32)
        top_f = sb("m_top_f", [P, NT, 2])
        small = sb("m_small", [P, NT, 4])
        lane = sb("m_lane", [P, EXPERTS])
        pick = sb("m_pick", [P, 2, EXPERTS])

        got_x = core.load(x[:], rows_view(sum_dram))
        got = [core.load(gate_w[:], a["L0_ffn_gate_w"].rearrange("(c p) e -> p c e", p=128)),
               core.load(gate_b[:], a["L0_ffn_gate_b"].partition_broadcast(P)),
               core.load(b2[:], a["L0_ffn_expert_b2"]),
               core.load(shared_b2[:], a["L0_ffn_shared_b2"].partition_broadcast(P))]
        ln = pool.did(nc.gpsimd.iota(lane[:], [[1, EXPERTS]], base=0, channel_multiplier=0,
                                     allow_small_or_imprecise_dtypes=True))
        done = layer_norm_rows(nc, core, x, n_rows, stat, mv, rstd, after=(got_x,))
        rows_to_cols(nc, core, n_rows, cols, done)
        ready = [(act.sem, act.count), (dve.sem, dve.count)]
        pe.need(*ready, *got)
        dve.need(*got, ln)
        for t in range(NT):
            b = core.bank()
            for k in range(KC):
                ins = nc.tensor.matmul(psum[0:P, b * BANK:b * BANK + EXPERTS], cols[:, k, t * P:(t + 1) * P],
                                       gate_w[:, k, :], start=(k == 0), stop=(k == KC - 1))
            s = pe.did(ins)
            dve.need(s)
            core.bank_free[b] = s = dve.did(nc.vector.tensor_tensor(
                logit[:, t, :], psum[0:P, b * BANK:b * BANK + EXPERTS], gate_b[:, :], ALU.add))
        dve.need(s)
        s = dve.did(nc.vector.tensor_reduce(small[:, :, 0], logit[:], AX.X, ALU.max))
        dve.need(s)
        s = dve.did(nc.vector.tensor_scalar(small[:, :, 0], small[:, :, 0], -1.0, None, ALU.mult))
        act.need(s)
        for t in range(NT):
            s = act.did(nc.scalar.activation(logit[:, t, :], logit[:, t, :], ACT.Exp, bias=small[:, t, 0:1],
                                             accum_out=small[:, t, 1:2]))
        dve.need(s)
        s = dve.did(nc.vector.reciprocal(small[:, :, 2], small[:, :, 1]))
        dve.need(s)
        for t in range(NT):
            s = dve.did(nc.vector.tensor_scalar(logit[:, t, :], logit[:, t, :], small[:, t, 2:3], None, ALU.mult))
        dve.need(s)
        for t in range(NT):
            s = dve.did(nc.vector.max(top[:, t, :], logit[:, t, :]))
        dve.need(s)
        for t in range(NT):
            s = dve.did(nc.vector.max_index(top_i[:, t, :], top[:, t, :], logit[:, t, :]))
        dve.need(s)
        dve.did(nc.vector.tensor_copy(top_f[:], top_i[:, :, 0:2]))
        s = dve.did(nc.vector.tensor_tensor(small[:, :, 0], top[:, :, 0], top[:, :, 1], ALU.add))
        dve.need(s)
        s = dve.did(nc.vector.reciprocal(small[:, :, 1], small[:, :, 0]))
        dve.need(s)
        for n in range(2):
            s = dve.did(nc.vector.tensor_tensor(small[:, :, 2 + n], top[:, :, n], small[:, :, 1], ALU.mult))
        s = dve.did(nc.vector.memset(cw[:, :, EXPERTS], 1.0))
        dve.need(s)
        for t in range(NT):
            for n in range(2):
                s = dve.did(nc.vector.tensor_scalar(pick[:, n, :], lane[:, :], top_f[:, t, n:n + 1],
                                                    small[:, t, 2 + n:3 + n], ALU.is_equal, ALU.mult))
            dve.need(s)
            s = dve.did(nc.vector.tensor_tensor(cw[:, t, 0:EXPERTS], pick[:, 0, :], pick[:, 1, :], ALU.add))
            b, s2 = turn_tile(nc, core, cw[:, t, 0:EXPERTS], 1, s, width=EXPERTS)
            dve.need(s2)
            core.bank_free[b] = s = dve.did(nc.vector.tensor_copy(cw_cols[:, t * P:(t + 1) * P],
                                                                  psum[0:EXPERTS, b * BANK:b * BANK + P]))
        pool.need(*got, done[-1])
        for t in range(NT):
            x_b = pool.did(nc.gpsimd.tensor_tensor(x[:, t, :], x[:, t, :], shared_b2[:, :], ALU.add))
        pe.need(s)
        for t in range(NT):
            b = core.bank()
            s = pe.did(nc.tensor.matmul(psum[0:P, b * BANK:b * BANK + D], cw_cols[:, t * P:(t + 1) * P], b2[:, :],
                                        start=True, stop=True))
            dve.need(s, x_b)
            core.bank_free[b] = dve.did(nc.vector.tensor_tensor(x[:, t, :], x[:, t, :],
                                                                psum[0:P, b * BANK:b * BANK + D], ALU.add))
        core.restart()

        def expert(w1_src, w2_src, b1_src, act_src, weight_of):
            got_w1 = core.load(w1[:], w1_src)
            got_s = [core.load(b1[:, n, :], b1_src(n)) for n in range(2)] + [core.load(actp[:], act_src)]
            got_w2 = core.load(w2[:], w2_src)
            s = dve.did(nc.vector.tensor_copy(cw_cur[:], weight_of))
            act.need(*got_s)
            dve.need(*got_s)
            s = dve.did(nc.vector.scalar_tensor_tensor(clamp[:, 0:2], actp[:, 3:5], -1.0, actp[:, 3:5],
                                                       ALU.mult, ALU.max))
            act.need(s)
            s = act.did(nc.scalar.activation(clamp[:, 0:2], clamp[:, 0:2], ACT.Exp, scale=-1.0))
            act.need(s)
            s = act.did(nc.scalar.activation(clamp[:, 0:2], clamp[:, 0:2], ACT.Ln, bias=1.0))
            dve.need(s)
            s = dve.did(nc.vector.scalar_tensor_tensor(clamp[:, 0:2], actp[:, 3:5], 0.0, clamp[:, 0:2],
                                                       ALU.max, ALU.add))
            dve.need(s)
            s = dve.did(nc.vector.tensor_scalar(clamp[:, 2:4], clamp[:, 0:2], -1.0, None, ALU.mult))
            dve.need(s)
            free = [None, None]
            n = 0
            for start, width in SPANS:
                for c in range(IC):
                    g_, u_, sg = (scratch[n % 2][:, i, 0:width] for i in range(3))
                    banks = []
                    for half in range(2):
                        b = core.bank()
                        pe.need(got_w1)
                        for k in range(KC):
                            first = c * 256 + half
                            ins = nc.tensor.matmul(psum[0:128, b * BANK:b * BANK + width],
                                                   w1[:, k, first:first + 255:2],
                                                   cols[:, k, start:start + width],
                                                   start=(k == 0), stop=(k == KC - 1))
                        banks.append((b, pe.did(ins)))
                    act.need(free[n % 2])
                    for half, dst in enumerate((g_, u_)):
                        b, s = banks[half]
                        act.need(s)
                        core.bank_free[b] = act.did(nc.scalar.activation(
                            dst, psum[0:128, b * BANK:b * BANK + width], ACT.Identity, bias=b1[:, half, c:c + 1]))
                        dve.need(core.bank_free[b])
                        s = dve.did(nc.vector.tensor_scalar(dst, dst, clamp[:, half:half + 1],
                                                            clamp[:, 2 + half:3 + half], ALU.min, ALU.max))
                        if half == 0:
                            act.need(s)
                            sig = act.did(nc.scalar.activation(sg, g_, ACT.Sigmoid, scale=actp[:, 0:1]))
                    dve.need(sig)
                    s = dve.did(nc.vector.scalar_tensor_tensor(sg, g_, actp[:, 1:2], sg, ALU.mult, ALU.mult))
                    dve.need(s)
                    free[n % 2] = dve.did(nc.vector.scalar_tensor_tensor(
                        hidden[:, c, start:start + width], u_, actp[:, 2:3], sg, ALU.add, ALU.mult))
                    n += 1
            h_done = (dve.sem, dve.count)

            def add_weighed(t, acc, s):
                dve.need(s)
                return dve.did(nc.vector.scalar_tensor_tensor(x[:, t, :], acc, cw_cur[:, t:t + 1], x[:, t, :],
                                                              ALU.mult, ALU.add))

            rows_product(nc, core, lambda k, s0, m: hidden[:, k, s0:s0 + m], lambda k: w2[:, k, :], IC,
                         (h_done, got_w2), add_weighed)

        pvec = lambda v: v.partition_broadcast(128)
        with nc.Fori(0, EXPERTS) as e:
            one = lambda v: v[ds(e, 1)]
            expert(a["L0_ffn_expert_w1"][ds(e, 1), :, :].rearrange("l (c p) o -> p (l c) o", p=128),
                   a["L0_ffn_expert_w2"][ds(e, 1), :, :].rearrange("l (c p) o -> p (l c) o", p=128),
                   lambda n: a["L0_ffn_expert_b1"][ds(e, 1), :].rearrange("l (c p n) -> p n (l c)", p=128, n=2)[:, n, :],
                   a["L0_ffn_expert_act"][ds(e, 1), :].rearrange("l o -> (l o)").partition_broadcast(128),
                   cw[:, :, ds(e, 1)].rearrange("p t e -> p (t e)"))
            core.restart()
        expert(a["L0_ffn_shared_w1"].rearrange("(c p) o -> p c o", p=128),
               a["L0_ffn_shared_w2"].rearrange("(c p) o -> p c o", p=128),
               lambda n: a["L0_ffn_shared_b1"].rearrange("(c p n) -> p n c", p=128, n=2)[:, n, :],
               a["L0_ffn_shared_act"].partition_broadcast(128), cw[:, :, EXPERTS])
        core.load(out.rearrange("(t p) d -> p t d", p=P), x[:], (dve.sem, dve.count))
        core.restart()


_INS = ['x', 'src', 'dst', 'node_vec1', 'L0_gnn_f_w1', 'L0_gnn_f_b1', 'L0_gnn_f_w2', 'L0_gnn_f_b2', 'L0_gnn_s1_w',
        'L0_gnn_s1_b', 'L0_gnn_b1_w', 'L0_gnn_b1_b', 'L0_gnn_wq', 'L0_gnn_bq', 'L0_gnn_wk', 'L0_gnn_bk',
        'L0_gnn_wv', 'L0_gnn_bv', 'L0_gnn_wo', 'L0_gnn_bo', 'L0_gnn_s2_w', 'L0_gnn_s2_b', 'L0_gnn_b2_w',
        'L0_gnn_b2_b', 'L0_gnn_m_w1', 'L0_gnn_m_b1', 'L0_gnn_m_w2', 'L0_gnn_m_b2', 'L0_mix_Wqkv', 'L0_mix_bqkv',
        'L0_mix_Pmat', 'L0_mix_Wproj', 'L0_mix_bproj', 'L0_mix_W1', 'L0_mix_b1', 'L0_mix_W2', 'L0_mix_b2',
        'L0_mix_g1', 'L0_mix_be1', 'L0_mix_g2', 'L0_mix_be2', 'L0_ffn_gate_w', 'L0_ffn_gate_b',
        'L0_ffn_shared_w1', 'L0_ffn_shared_b1', 'L0_ffn_shared_w2', 'L0_ffn_shared_b2', 'L0_ffn_shared_act',
        'L0_ffn_expert_w1', 'L0_ffn_expert_b1', 'L0_ffn_expert_w2', 'L0_ffn_expert_b2', 'L0_ffn_expert_act']


def kernel(**inputs):
    import numpy as _np
    import concourse.bacc as _bacc
    from concourse import mybir as _mybir
    from concourse.bass_utils import run_bass_kernel_spmd as _run

    nc = _bacc.Bacc("TRN2", target_bir_lowering=False, num_devices=1)
    arrays, aps = {}, {}
    for name in _INS:
        v = _np.ascontiguousarray(inputs[name])
        arrays[f"in_{name}"] = v
        aps[name] = nc.dram_tensor(f"in_{name}", v.shape, _mybir.dt.from_np(v.dtype), kind="ExternalInput").ap()
    out = nc.dram_tensor("out_0", (N, D), F32, kind="ExternalOutput").ap()
    build(nc, aps, out)
    r = _run(nc, [arrays], core_ids=[0])
    return r.results[0]["out_0"]
```

```python
from contextlib import ExitStack

import concourse.bass as bass
from concourse import mybir

F32 = mybir.dt.float32
F16 = mybir.dt.float16
I32 = mybir.dt.int32
U32 = mybir.dt.uint32
ALU = mybir.AluOpType
ACT = mybir.ActivationFunctionType
AX = mybir.AxisListType
ENG = mybir.EngineType
ds = bass.ds

N = 1250
D = 512
P = 125
NT = N // P
KC = D // 128
EPS = 1e-5
NOT_AN_EDGE = -1e30
BANK = 512
SPANS = [(0, 500), (500, 500), (1000, 250)]
GNN_LAYERS = 4
GNN_HEADS = 4
COND = 16
FREQ = 32
E_EDGES = 41250
EDGE_TILES = 4
HOT_RING = 8
HOT_DST = 8
EDGE_GROUPS = -(-E_EDGES // (128 * EDGE_TILES))
WINDOW = E_EDGES * P * 11 // (N * 10 * 128 * EDGE_TILES) + 2
MIX_HEADS = 8
MIX_DH = 64
MIX_F = 256
MIX_H = 1024
EXPERTS = 16
FFN_I = 384
IC = FFN_I // 128
SLOT_TILES = (2 * N + EXPERTS * 127) // 128
SLOT_UNROLL = 4
SLOT_ROUNDS = -(-SLOT_TILES // SLOT_UNROLL)
SLOT_TILES_PADDED = SLOT_UNROLL * SLOT_ROUNDS + 2
HW_DMAS, SW_DMAS = 24, 8
ROUND = 1.5 * 2.0 ** 23


class Queue:

    def __init__(self, eng, sem):
        self.eng, self.sem = eng, sem
        self.count, self.seen = 0, {}

    def did(self, ins):
        ins.then_inc(self.sem, 1)
        self.count += 1
        return (self.sem, self.count)

    def need(self, *done):
        for d in done:
            if d is None:
                continue
            sem, value = d
            if self.seen.get(sem.name, 0) < value:
                self.eng.wait_ge(sem, value)
                self.seen[sem.name] = value


class Core:
    def __init__(self, nc, ctx):
        self.nc = nc
        mk = lambda name: ctx.enter_context(nc.semaphore(name))
        self.pe = Queue(nc.tensor, mk("pe_done"))
        self.dve = Queue(nc.vector, mk("dve_done"))
        self.act = Queue(nc.scalar, mk("act_done"))
        self.pool = Queue(nc.gpsimd, mk("pool_done"))
        self.sp = Queue(nc.sync, mk("sp_unused"))
        self.dma_sems = [mk(f"dma_done{i}") for i in range(HW_DMAS)]
        self.queues = [self.pe, self.dve, self.act, self.pool, self.sp]
        sems = [q.sem for q in self.queues] + self.dma_sems
        self.first = min(s.num for s in sems)
        self.last = max(s.num for s in sems)
        assert self.last - self.first == len(sems) - 1
        self.dma_count = [0] * len(self.dma_sems)
        self.next_dma = 0
        self.sw_sems = [mk(f"pool_dma_done{i}") for i in range(SW_DMAS)]
        self.sw_count, self.next_sw_dma = [0] * SW_DMAS, 0
        self.bank_free = [None] * 8
        self.next_bank = 0

    def load(self, out, in_, *after, by=None):
        q = by or self.sp
        q.need(*after)
        n = self.next_dma
        self.next_dma = (n + 1) % HW_DMAS
        if self.dma_count[n]:
            q.need((self.dma_sems[n], 16 * self.dma_count[n]))
        q.eng.dma_start(out, in_, allow_slow_non_contiguous=True).then_inc(self.dma_sems[n], 16)
        self.dma_count[n] += 1
        return (self.dma_sems[n], 16 * self.dma_count[n])

    def indirect(self, dram, sbuf, index, scatter):
        n = self.next_sw_dma
        self.next_sw_dma = (n + 1) % SW_DMAS
        if self.sw_count[n]:
            self.pool.need((self.sw_sems[n], 16 * self.sw_count[n]))
        at = bass.IndirectOffsetOnAxis(ap=index, axis=0)
        if scatter:
            ins = self.nc.gpsimd.indirect_dma_start(out=dram, out_offset=at, in_=sbuf, in_offset=None)
        else:
            ins = self.nc.gpsimd.indirect_dma_start(out=sbuf, out_offset=None, in_=dram, in_offset=at)
        ins.then_inc(self.sw_sems[n], 16)
        self.sw_count[n] += 1
        return (self.sw_sems[n], 16 * self.sw_count[n])

    def restart(self):
        for n, c in enumerate(self.dma_count):
            if c:
                self.sp.need((self.dma_sems[n], 16 * c))
        for n, c in enumerate(self.sw_count):
            if c:
                self.sp.need((self.sw_sems[n], 16 * c))
        self.nc.all_engine_barrier(sems_to_clear=range(self.first, self.last + 1))
        for q in self.queues:
            q.count, q.seen = 0, {}
        self.dma_count = [0] * len(self.dma_sems)
        self.next_dma = 0
        self.bank_free = [None] * 8
        self.next_bank = 0

    def bank(self):
        b = self.next_bank
        self.next_bank = (b + 1) % 8
        self.pe.need(self.bank_free[b])
        return b


def build(nc, a, out):
    with ExitStack() as ctx:
        core = Core(nc, ctx)
        psum = ctx.enter_context(nc.psum_tensor("psum", [128, 8 * BANK], F32))
        ident = ctx.enter_context(nc.sbuf_tensor("ident", [128, 128], F32))
        xn_dram = nc.dram_tensor("xn_scratch", [N, D], F32)
        gnn_dram = nc.dram_tensor("gnn_scratch", [N, D], F32)
        sum_dram = nc.dram_tensor("sum_scratch", [N, D], F32)
        flag_dram = nc.dram_tensor("flag_scratch", [NT, EDGE_GROUPS], I32)
        window_dram = nc.dram_tensor("window_scratch", [NT, 2], I32)
        core.psum, core.ident = psum, ident

        m = core.pool.did(nc.gpsimd.memset(ident[:], 0.0))
        core.pool.need(m)
        core.pool.did(nc.gpsimd.affine_select(out=ident[:], in_=ident[:], compare_op=ALU.not_equal, fill=1.0,
                                              base=0, pattern=[[-1, 128]], channel_multiplier=1))
        core.restart()
        with nc.sbuf_tensor("ln_count", [P, NT, N], F32) as ln_count:
            edge_counts(nc, core, a["src"], a["dst"], flag_dram, window_dram, ln_count)
            gnn(nc, core, a, ln_count, xn_dram, gnn_dram)
        performer(nc, core, a, xn_dram, gnn_dram, sum_dram)
        moe(nc, core, a, sum_dram, out)
        core.restart()


def rows_view(dram):
    return dram[:, :].rearrange("(t p) d -> p t d", p=P)


def layer_norm_rows(nc, core, x, out, stat, mv, rstd, after=(), out_free=()):
    dve, act = core.dve, core.act
    for t in range(NT):
        dve.need(*after)
        s = dve.did(nc.vector.bn_stats(stat[:, t, :], x[:, t, :]))
    dve.need(s)
    for t in range(NT):
        s = dve.did(nc.vector.bn_aggr(mv[:, t, :], stat[:, t, :]))
    dve.need(s)
    s = dve.did(nc.vector.tensor_scalar(rstd[:, 0:NT], mv[:, :, 1], EPS, None, ALU.add))
    act.need(s)
    s = act.did(nc.scalar.activation(rstd[:, NT:2 * NT], rstd[:, 0:NT], ACT.Sqrt))
    dve.need(s)
    s = dve.did(nc.vector.reciprocal(rstd[:, 0:NT], rstd[:, NT:2 * NT]))
    dve.need(s, *out_free)
    return [dve.did(nc.vector.tensor_scalar(out[:, t, :], x[:, t, :], mv[:, t, 0:1], rstd[:, t:t + 1],
                                            ALU.subtract, ALU.mult)) for t in range(NT)]


def turn_tile(nc, core, src, n_chunks, done, width=128):
    pe = core.pe
    pe.need(done)
    b = core.bank()
    for c in range(n_chunks):
        ins = nc.tensor.transpose(core.psum[0:width, b * BANK + c * P:b * BANK + (c + 1) * P],
                                  src[:, c * width:(c + 1) * width], core.ident[0:P, 0:P])
    return b, pe.did(ins)


def turned(core, b, rows=128, n=KC):
    return core.psum[0:rows, b * BANK:b * BANK + n * P].rearrange("p (c n) -> p c n", n=P)


def rows_to_cols(nc, core, rows, cols, ready, free=()):
    out = []
    for t in range(NT):
        b, s = turn_tile(nc, core, rows[:, t, :], KC, ready[t])
        q = core.act if t % 2 else core.dve
        q.need(s, *free)
        dst = cols[:, :, t * P:(t + 1) * P]
        ins = nc.scalar.copy(dst, turned(core, b)) if t % 2 else nc.vector.tensor_copy(dst, turned(core, b))
        core.bank_free[b] = q.did(ins)
        out.append(core.bank_free[b])
    return out


def cols_product(nc, core, w, x, n_out, k_chunks, ready, evacuate):
    pe = core.pe
    for start, width in SPANS:
        pe.need(*ready)
        for o in range(n_out):
            b = core.bank()
            for k in range(k_chunks):
                ins = nc.tensor.matmul(core.psum[0:128, b * BANK:b * BANK + width], w(k, o), x(k, start, width),
                                       start=(k == 0), stop=(k == k_chunks - 1))
            s = pe.did(ins)
            core.bank_free[b] = evacuate(o, start, width, core.psum[0:128, b * BANK:b * BANK + width], s)


def rows_product(nc, core, x, w, k_chunks, ready, evacuate):
    pe = core.pe
    for t in range(NT):
        pe.need(*ready)
        b = core.bank()
        acc = core.psum[0:P, b * BANK:b * BANK + D]
        for k in range(k_chunks):
            ins = nc.tensor.matmul(acc, x(k, t * P, P), w(k), start=(k == 0), stop=(k == k_chunks - 1))
        core.bank_free[b] = evacuate(t, acc, pe.did(ins))


def edge_counts(nc, core, src, dst, flag_dram, window_dram, ln_count):
    pe, dve, act, pool = core.pe, core.dve, core.act, core.pool
    T, G, W = EDGE_TILES, EDGE_GROUPS, WINDOW
    whole = G - 1
    rest = E_EDGES - whole * 128 * T
    rest_p, rest_e = rest // T, rest % T
    psum = core.psum
    with ExitStack() as ctx:
        sb = lambda name, shape, dt=F32: ctx.enter_context(nc.sbuf_tensor(name, shape, dt))
        ends_i = sb("ends_i", [128, 2, G, T], I32)
        ends = sb("ends", [128, 2, G, T])
        low = sb("low", [128, G, T])
        iota = sb("iota", [128, N], F16)
        iota_f = sb("iota_f", [NT, G])
        edge_of = sb("block_starts", [G, 2, NT])
        cur = sb("cur", [128, 2, W, T])
        cur_dst = sb("cur_dst", [128, W, T], F16)
        block_iota = sb("block_iota", [128, P], F16)
        hot_src = sb("hot_src", [128, HOT_RING, N], F16)
        hot_dst = sb("hot_dst", [128, 2, HOT_DST, P], F16)
        span = sb("span", [128, 2, G])
        span_g = sb("span_g", [G, 2])
        meets = sb("meets", [G, 2, NT])
        meets_b = sb("meets_b", [NT, G])
        outside = sb("outside", [NT, G])
        outside_i = sb("outside_i", [NT, G], I32)
        first = sb("first", [NT, 4])
        window_i = sb("window_i", [NT, 2], I32)
        flags = sb("flags", [1, NT * G], I32)
        windows = sb("windows", [1, NT * 2], I32)
        counts = sb("counts", [P, NT, N])
        none = sb("none", [P, 2, N])

        fill = dve.did(nc.vector.memset(ends_i[:], -1))
        pool.did(nc.gpsimd.iota(iota[:], [[1, N]], base=0, channel_multiplier=0,
                                allow_small_or_imprecise_dtypes=True))
        pool.did(nc.gpsimd.iota(iota_f[:], [[1, G]], base=0, channel_multiplier=0,
                                allow_small_or_imprecise_dtypes=True))
        pool.did(nc.gpsimd.iota(edge_of[:, 0, :], [[P, NT]], base=0, channel_multiplier=0,
                                allow_small_or_imprecise_dtypes=True))
        consts = pool.did(nc.gpsimd.iota(edge_of[:, 1, :], [[P, NT]], base=P - 1, channel_multiplier=0,
                                         allow_small_or_imprecise_dtypes=True))
        got = []
        for n, e in enumerate((src, dst)):
            got.append(core.load(ends_i[:, n, 0:whole, :],
                                 e[0:whole * 128 * T].rearrange("(g p t) -> p g t", p=128, t=T), fill))
            got.append(core.load(ends_i[0:rest_p, n, whole, :],
                                 e[whole * 128 * T:whole * 128 * T + rest_p * T].rearrange("(p t) -> p t", t=T)))
            if rest_e:
                got.append(core.load(ends_i[rest_p:rest_p + 1, n, whole, 0:rest_e],
                                     e[E_EDGES - rest_e:E_EDGES].rearrange("(p t) -> p t", t=rest_e)))
        dve.need(*got)
        e = dve.did(nc.vector.tensor_copy(ends[:], ends_i[:]))
        dve.need(e)
        s = dve.did(nc.vector.tensor_scalar(low[:], ends[:, 1], 0.0, 4096.0, ALU.is_lt, ALU.mult))
        dve.need(s)
        s = dve.did(nc.vector.tensor_tensor(low[:], low[:], ends[:, 1], ALU.add))
        dve.need(s)
        dve.did(nc.vector.tensor_reduce(span[:, 0, :], low[:], AX.X, ALU.min))
        s = dve.did(nc.vector.tensor_reduce(span[:, 1, :], ends[:, 1], AX.X, ALU.max))
        pe.need(s)
        for n in range(2):
            ins = nc.tensor.transpose(psum[0:G, n * 128:(n + 1) * 128], span[:, n, :], core.ident[:, :])
        s = pe.did(ins)
        dve.need(s)
        dve.did(nc.vector.tensor_reduce(span_g[:, 0:1], psum[0:G, 0:128], AX.X, ALU.min))
        s = dve.did(nc.vector.tensor_reduce(span_g[:, 1:2], psum[0:G, 128:256], AX.X, ALU.max))
        dve.need(s, consts)
        dve.did(nc.vector.tensor_scalar(meets[:, 0, :], edge_of[:, 1, :], span_g[:, 0:1], None, ALU.is_ge))
        s = dve.did(nc.vector.tensor_scalar(meets[:, 1, :], edge_of[:, 0, :], span_g[:, 1:2], None, ALU.is_le))
        dve.need(s)
        s = dve.did(nc.vector.tensor_tensor(meets[:, 0, :], meets[:, 0, :], meets[:, 1, :], ALU.mult))
        pe.need(s)
        s = pe.did(nc.tensor.transpose(psum[0:NT, BANK:BANK + G], meets[:, 0, :], core.ident[0:G, 0:G]))
        dve.need(s)
        s = dve.did(nc.vector.tensor_copy(meets_b[:], psum[0:NT, BANK:BANK + G]))
        dve.need(s)
        s = dve.did(nc.vector.tensor_scalar(outside[:], meets_b[:], -4096.0, 4096.0, ALU.mult, ALU.add))
        dve.need(s)
        s = dve.did(nc.vector.tensor_tensor(outside[:], outside[:], iota_f[:], ALU.add))
        dve.need(s)
        s = dve.did(nc.vector.tensor_reduce(first[:, 0:1], outside[:], AX.X, ALU.min))
        dve.need(s)
        s = dve.did(nc.vector.tensor_scalar(first[:, 0:1], first[:, 0:1], float(G - W), None, ALU.min))
        dve.need(s)
        s = dve.did(nc.vector.tensor_scalar(first[:, 2:3], first[:, 0:1], float(W), None, ALU.add))
        dve.need(s)
        s = dve.did(nc.vector.tensor_scalar(outside[:], iota_f[:], first[:, 2:3], None, ALU.is_ge))
        dve.need(s)
        s = dve.did(nc.vector.tensor_tensor(outside[:], outside[:], meets_b[:], ALU.mult))
        dve.need(s)
        s = dve.did(nc.vector.tensor_reduce(first[:, 1:2], outside[:], AX.X, ALU.max))
        dve.did(nc.vector.tensor_copy(outside_i[:], outside[:]))
        dve.need(s)
        s = dve.did(nc.vector.tensor_copy(window_i[:], first[:, 0:2]))
        s1 = core.load(flag_dram[:, :], outside_i[:], s)
        s2 = core.load(window_dram[:, :], window_i[:], s)
        row = lambda v, p: v[:, :].rearrange("j g -> (j g)").rearrange("(a f) -> a f", a=1)
        core.load(flags[:, :], row(flag_dram, 0), s1)
        core.load(windows[:, :], row(window_dram, 0), s2)
        core.restart()

        def sum_tile(lhs, rhs, first_tile):
            for start in range(0, N, BANK):
                width = min(BANK, N - start)
                ins = nc.tensor.matmul(psum[0:P, start:start + width], lhs, rhs[:, start:start + width],
                                       start=first_tile, stop=True, skip_group_check=True)
            return ins

        with nc.Fori(0, NT) as j:
            start = nc.vector.value_load(windows[0:1, ds(2 * j, 1)], min_val=0, max_val=G - W)
            s = dve.did(nc.vector.tensor_copy(cur[:], ends[:, :, ds(start, W), :]))
            s2 = dve.did(nc.vector.tensor_copy(block_iota[:], iota[:, ds(j * P, P)]))
            dve.need(s, s2)
            s = dve.did(nc.vector.tensor_copy(cur_dst[:], cur[:, 1]))
            dve.need(s)
            summed = []
            for n in range(W * T):
                g, t = n // T, n % T
                if n % HOT_DST == 0:
                    if n >= 2 * HOT_DST:
                        dve.need(summed[n - HOT_DST - 1])
                    lot = cur_dst[:].rearrange("p g t -> p (g t)")[:, n:n + HOT_DST].unsqueeze(2).broadcast_to([128, HOT_DST, P])
                    d = dve.did(nc.vector.tensor_tensor(hot_dst[:, n // HOT_DST % 2], lot,
                                                        block_iota[:].unsqueeze(1).broadcast_to([128, HOT_DST, P]),
                                                        ALU.is_equal))
                if n >= HOT_RING:
                    dve.need(summed[n - HOT_RING])
                s = dve.did(nc.vector.tensor_scalar(hot_src[:, n % HOT_RING, :], iota[:, :],
                                                    cur[:, 0, g, t:t + 1], None, ALU.is_equal))
                pe.need(s)
                summed.append(pe.did(sum_tile(hot_dst[:, n // HOT_DST % 2, n % HOT_DST, :],
                                              hot_src[:, n % HOT_RING, :], n == 0)))
            core.restart()
            beyond = nc.values_load(windows[0:1, ds(2 * j + 1, 1)], min_val=0, max_val=1)
            with nc.If(beyond == 1):
                with nc.Fori(0, G) as g:
                    flag = nc.values_load(flags[0:1, ds(j * G + g, 1)], min_val=0, max_val=1)
                    with nc.If(flag == 1):
                        s = dve.did(nc.vector.tensor_copy(cur[:, :, 0:1, :], ends[:, :, ds(g, 1), :]))
                        dve.need(s)
                        for t in range(T):
                            dve.did(nc.vector.tensor_scalar(hot_dst[:, 0, t, :], block_iota[:],
                                                            cur[:, 1, 0, t:t + 1], None, ALU.is_equal))
                            s = dve.did(nc.vector.tensor_scalar(hot_src[:, t, :], iota[:, :], cur[:, 0, 0, t:t + 1],
                                                                None, ALU.is_equal))
                            pe.need(s)
                            pe.did(sum_tile(hot_dst[:, 0, t, :], hot_src[:, t, :], False))
                        core.restart()
            dve.did(nc.vector.tensor_copy(counts[:, ds(j, 1), :].rearrange("p j n -> p (j n)"), psum[0:P, 0:N]))
            core.restart()

        none_free = [None, None]
        added = {}

        def turn_block(j):
            pe.need(added[j])
            for b0, n in ((0, 4), (4, 4), (8, 2)):
                b = core.bank()
                for i in range(n):
                    ins = nc.tensor.transpose(psum[0:P, b * BANK + i * P:b * BANK + (i + 1) * P],
                                              none[:, j % 2, (b0 + i) * P:(b0 + i + 1) * P], core.ident[0:P, 0:P])
                s = none_free[j % 2] = pe.did(ins)
                q = act if b0 == 4 else dve
                q.need(s)
                o = ln_count[:, b0:b0 + n, j * P:(j + 1) * P]
                v = psum[0:P, b * BANK:b * BANK + n * P].rearrange("p (i j) -> p i j", j=P)
                core.bank_free[b] = q.did(nc.scalar.copy(o, v) if b0 == 4 else nc.vector.tensor_copy(o, v))

        for j in range(NT):
            dve.need(none_free[j % 2])
            dve.did(nc.vector.tensor_scalar(none[:, j % 2, :], counts[:, j, :], 0.0, NOT_AN_EDGE, ALU.is_equal,
                                            ALU.mult))
            s = dve.did(nc.vector.tensor_scalar(counts[:, j, :], counts[:, j, :], 1.0, None, ALU.max))
            act.need(s)
            s = act.did(nc.scalar.activation(counts[:, j, :], counts[:, j, :], ACT.Ln))
            if j >= 1:
                turn_block(j - 1)
            dve.need(s)
            added[j] = dve.did(nc.vector.tensor_tensor(none[:, j % 2, :], counts[:, j, :], none[:, j % 2, :], ALU.add))
        turn_block(NT - 1)
        core.restart()


def gnn(nc, core, a, ln_count, xn_dram, gnn_dram):
    pe, dve, act, pool = core.pe, core.dve, core.act, core.pool
    psum = core.psum
    H = GNN_HEADS
    Q_SCALE = float(128) ** -0.5
    with ExitStack() as ctx:
        sb = lambda name, shape, dt=F32: ctx.enter_context(nc.sbuf_tensor(name, shape, dt))
        x = sb("g_x", [P, NT, D])
        y_cols = sb("g_y_cols", [128, KC, N])
        q_cols = sb("g_q_cols", [128, KC, N])
        k_cols = sb("g_k_cols", [128, KC, N])
        v_rows = sb("g_v_rows", [P, NT, D])
        w = [sb(f"g_w{i}", [128, KC, D]) for i in range(3)]
        cond = sb("g_cond", [COND + 2, N])
        cond_w = sb("g_cond_w", [COND + 2, 4, D])
        prob = sb("g_prob", [P, 2, N])
        bias_rows = sb("g_bias_rows", [P, D])
        bias_cols = sb("g_bias_cols", [128, 3, KC])
        stat = sb("g_stat", [P, NT, 6])
        mv = sb("g_mv", [P, NT, 2])
        rstd = sb("g_rstd", [P, 2 * NT])
        row_max = sb("g_row_max", [P, 2, 4])
        f_w1 = sb("g_f_w1", [2 * FREQ, COND])
        f_w2 = sb("g_f_w2", [COND, COND])
        f_b = sb("g_f_b", [COND, 2])
        freq = sb("g_freq", [2 * FREQ, 2])
        turned_prob = y_cols[0:P, :, :].rearrange("p a b -> p (a b)").rearrange("p (u j i) -> p u j i", u=2, i=2 * P)

        noise = q_cols[0:2 * FREQ, 0, :]
        emb = q_cols[0:2 * FREQ, 1, :]
        whole_turns = q_cols[0:2 * FREQ, 2, :]
        hidden = q_cols[0:COND, 3, :]
        gate = k_cols[0:COND, 0, :]
        f = pool.did(nc.gpsimd.iota(freq[0:FREQ, 0:1], [[0, 1]], base=1, channel_multiplier=1,
                                    allow_small_or_imprecise_dtypes=True))
        f2 = pool.did(nc.gpsimd.iota(freq[FREQ:2 * FREQ, 0:1], [[0, 1]], base=1, channel_multiplier=1,
                                     allow_small_or_imprecise_dtypes=True))
        dve.did(nc.vector.memset(freq[0:FREQ, 1:2], 0.0))
        dve.did(nc.vector.memset(freq[FREQ:2 * FREQ, 1:2], 0.25))
        ones = dve.did(nc.vector.memset(cond[:], 1.0))
        dve.did(nc.vector.memset(cond_w[:, 1, :], 0.0))
        dve.did(nc.vector.memset(cond_w[:, 3, :], 0.0))
        dve.did(nc.vector.memset(cond_w[:, 0, :], 1.0))
        s = dve.did(nc.vector.memset(cond_w[:, 2, :], 1.0))
        got_x = core.load(x[:], a["x"].rearrange("(t p) d -> p t d", p=P))
        got_n = core.load(noise, a["node_vec1"].rearrange("n a -> (n a)").partition_broadcast(2 * FREQ))
        got_f = [core.load(f_w1[:], a["L0_gnn_f_w1"]), core.load(f_w2[:], a["L0_gnn_f_w2"]),
                 core.load(f_b[:, 0:1], a["L0_gnn_f_b1"].rearrange("(p a) -> p a", a=1)),
                 core.load(f_b[:, 1:2], a["L0_gnn_f_b2"].rearrange("(p a) -> p a", a=1))]
        dve.need(f, f2)
        s = dve.did(nc.vector.tensor_scalar(freq[:, 0:1], freq[:, 0:1], 1.0 / 16.0, None, ALU.mult))
        dve.need(got_n, s)
        s = dve.did(nc.vector.tensor_scalar(emb, noise, freq[:, 0:1], freq[:, 1:2], ALU.mult, ALU.add))
        dve.need(s)
        s = dve.did(nc.vector.tensor_scalar(whole_turns, emb, 12582912.0, None, ALU.add))
        dve.need(s)
        s = dve.did(nc.vector.tensor_scalar(whole_turns, whole_turns, -12582912.0, None, ALU.add))
        dve.need(s)
        s = dve.did(nc.vector.tensor_tensor(emb, emb, whole_turns, ALU.subtract))
        act.need(s)
        s = act.did(nc.scalar.activation(emb, emb, ACT.Sin, scale=6.2831850))
        pe.need(s, *got_f)
        act.need(*got_f)
        for n, (start, width) in enumerate(SPANS):
            ins = nc.tensor.matmul(psum[0:COND, n * BANK:n * BANK + width], f_w1[:, :], emb[:, start:start + width],
                                   start=True, stop=True)
            s = pe.did(ins)
            act.need(s)
            act.did(nc.scalar.activation(hidden[:, start:start + width], psum[0:COND, n * BANK:n * BANK + width],
                                         ACT.Identity, bias=f_b[:, 0:1]))
            act.did(nc.scalar.activation(gate[:, start:start + width], psum[0:COND, n * BANK:n * BANK + width],
                                         ACT.Sigmoid, bias=f_b[:, 0:1]))
        dve.need((act.sem, act.count))
        s = dve.did(nc.vector.tensor_tensor(hidden, hidden, gate, ALU.mult))
        pe.need(s)
        dve.need(*got_f)
        for n, (start, width) in enumerate(SPANS):
            ins = nc.tensor.matmul(psum[0:COND, (3 + n) * BANK:(3 + n) * BANK + width], f_w2[:, :],
                                   hidden[:, start:start + width], start=True, stop=True)
            s = pe.did(ins)
            dve.need(s)
            dve.did(nc.vector.tensor_scalar(cond[0:COND, start:start + width],
                                            psum[0:COND, (3 + n) * BANK:(3 + n) * BANK + width],
                                            f_b[:, 1:2], None, ALU.add))
        done = layer_norm_rows(nc, core, x, x, stat, mv, rstd, after=(got_x,))
        core.load(rows_view(xn_dram), x[:], done[-1])
        core.restart()

        def weight_rows(name, layer):
            return a[name][ds(layer, 1), :, :].rearrange("l (c p) o -> p (l c) o", p=128)

        def bias_row(name, layer, n=P):
            return a[name][ds(layer, 1), :].rearrange("l o -> (l o)").partition_broadcast(n)

        def conditioned_norm(which, got, x_free_rows):
            y = v_rows
            done = layer_norm_rows(nc, core, x, y, stat, mv, rstd)
            pe.need(*got)
            out = []
            for t in range(NT):
                pair = []
                for n in range(2):
                    b = core.bank()
                    ins = nc.tensor.matmul(psum[0:P, b * BANK:b * BANK + D], cond[:, t * P:(t + 1) * P],
                                           cond_w[:, 2 * which + n, :], start=True, stop=True)
                    pair.append((b, pe.did(ins)))
                dve.need(done[t], pair[0][1])
                b = pair[0][0]
                s = dve.did(nc.vector.tensor_tensor(y[:, t, :], y[:, t, :], psum[0:P, b * BANK:b * BANK + D],
                                                    ALU.mult))
                core.bank_free[b] = s
                b = pair[1][0]
                dve.need(s, pair[1][1])
                s = dve.did(nc.vector.tensor_tensor(y[:, t, :], y[:, t, :], psum[0:P, b * BANK:b * BANK + D],
                                                    ALU.add))
                core.bank_free[b] = s
                out.append(s)
                if t >= 1:
                    turn(t - 1, out[t - 1])
            turn(NT - 1, out[NT - 1])
            return (act.sem, act.count)

        def turn(t, ready):
            b, s = turn_tile(nc, core, v_rows[:, t, :], KC, ready)
            act.need(s)
            core.bank_free[b] = act.did(nc.scalar.copy(y_cols[:, :, t * P:(t + 1) * P], turned(core, b)))

        with nc.Fori(0, GNN_LAYERS) as layer:
            got_c = []
            for n, (wn, bn) in enumerate((("s1_w", "s1_b"), ("b1_w", "b1_b"), ("s2_w", "s2_b"), ("b2_w", "b2_b"))):
                got_c.append(core.load(cond_w[0:COND, n, :], a["L0_gnn_" + wn][ds(layer, 1), :, :].rearrange(
                    "l c d -> (l c) d")))
                got_c.append(core.load(cond_w[COND:COND + 1, n, :], a["L0_gnn_" + bn][ds(layer, 1), :]))
            got_w = {}
            for n, name in enumerate(("wq", "wk", "wv")):
                got_w[name] = core.load(w[n][:], weight_rows("L0_gnn_" + name, layer))
            got_bc = [core.load(bias_cols[:, n, :], a["L0_gnn_" + name][ds(layer, 1), :].rearrange(
                "l (c p) -> p (l c)", p=128)) for n, name in enumerate(("bq", "bk", "m_b1"))]
            got_bv = core.load(bias_rows[:, :], bias_row("L0_gnn_bv", layer))

            y_ready = conditioned_norm(0, got_c, None)
            act.need(*got_bc)
            dve.need(*got_bc)
            s = act.did(nc.scalar.mul(bias_cols[:, 0, :], bias_cols[:, 0, :], Q_SCALE))
            act.need(s)

            def to_q(o, start, width, acc, s):
                act.need(s)
                return act.did(nc.scalar.activation(q_cols[:, o, start:start + width], acc, ACT.Identity,
                                                    bias=bias_cols[:, 0, o:o + 1], scale=Q_SCALE))

            def to_k(o, start, width, acc, s):
                dve.need(s)
                return dve.did(nc.vector.tensor_scalar(k_cols[:, o, start:start + width], acc,
                                                       bias_cols[:, 1, o:o + 1], None, ALU.add))

            def to_v(t, acc, s):
                dve.need(s)
                return dve.did(nc.vector.tensor_tensor(v_rows[:, t, :], acc, bias_rows[:, :], ALU.add))

            ys = lambda k, start, width: y_cols[:, k, start:start + width]
            cols_product(nc, core, lambda k, o: w[0][:, k, o * 128:(o + 1) * 128], ys, KC, KC,
                         (y_ready, got_w["wq"]), to_q)
            q_done, pe_q = (act.sem, act.count), (pe.sem, pe.count)
            got_wo = core.load(w[0][:], weight_rows("L0_gnn_wo", layer), pe_q)
            cols_product(nc, core, lambda k, o: w[1][:, k, o * 128:(o + 1) * 128], ys, KC, KC,
                         (y_ready, got_w["wk"]), to_k)
            k_done, pe_k = (dve.sem, dve.count), (pe.sem, pe.count)
            got_m1 = core.load(w[1][:], weight_rows("L0_gnn_m_w1", layer), pe_k)
            dve.need(got_bv)
            rows_product(nc, core, ys, lambda k: w[2][:, k, :], KC, (y_ready, got_w["wv"]), to_v)
            v_done, pe_v = (dve.sem, dve.count), (pe.sem, pe.count)
            got_m2 = core.load(w[2][:], weight_rows("L0_gnn_m_w2", layer), pe_v)
            got_bo = core.load(bias_rows[:, :], bias_row("L0_gnn_bo", layer), v_done)
            pool.need(got_bo, v_done)
            for t in range(NT):
                x_bo = pool.did(nc.gpsimd.tensor_tensor(x[:, t, :], x[:, t, :], bias_rows[:, :], ALU.add))
            got_b2 = core.load(bias_rows[:, :], bias_row("L0_gnn_m_b2", layer), x_bo)

            steps = [(h, t) for h in range(H) for t in range(NT)]
            soft = {}
            scores_free = core.bank_free[:]
            turn_free = [core.bank_free[3:6]]
            out_free = [core.bank_free[6], core.bank_free[7]]
            prob_free = [None, None]
            pair_done, out_done = {}, {}
            pe.need(*core.bank_free)
            s_free = None

            def scores(n):
                nonlocal s_free
                h, t = steps[n]
                u = n % 2
                pe.need(q_done, k_done, s_free)
                for start in range(0, N, BANK):
                    width = min(BANK, N - start)
                    ins = nc.tensor.matmul(psum[0:P, start:start + width], q_cols[:, h, t * P:(t + 1) * P],
                                           k_cols[:, h, start:start + width], start=True, stop=True)
                s = pe.did(ins)
                dve.need(s, prob_free[u])
                s = s_free = dve.did(nc.vector.tensor_tensor_reduce(
                    prob[:, u, :], psum[0:P, 0:N], ln_count[:, t, :], 1.0, NOT_AN_EDGE / 10, ALU.add, ALU.max,
                    row_max[:, u, 0:1]))
                dve.need(s)
                s = dve.did(nc.vector.tensor_scalar(row_max[:, u, 1:2], row_max[:, u, 0:1], -1.0, None, ALU.mult))
                act.need(s)
                s = act.did(nc.scalar.activation(prob[:, u, :], prob[:, u, :], ACT.Exp, bias=row_max[:, u, 1:2],
                                                 accum_out=row_max[:, u, 2:3]))
                return s

            def normalise(n, s):
                u = n % 2
                dve.need(s)
                s = dve.did(nc.vector.tensor_scalar(row_max[:, u, 2:3], row_max[:, u, 2:3], 1e-30, None, ALU.max))
                dve.need(s)
                s = dve.did(nc.vector.reciprocal(row_max[:, u, 3:4], row_max[:, u, 2:3]))
                dve.need(s)
                return dve.did(nc.vector.tensor_scalar(prob[:, u, :], prob[:, u, :], row_max[:, u, 3:4], None,
                                                       ALU.mult))

            def turn_probs(n, ready):
                u, g = n % 2, n // 2
                half = (n % 2) * P
                pe.need(ready, *turn_free[0])
                frees = []
                for b, j0, nj in ((3, 0, 4), (4, 4, 4), (5, 8, 2)):
                    for j in range(nj):
                        ins = nc.tensor.transpose(psum[0:P, b * BANK + j * P:b * BANK + (j + 1) * P],
                                                  prob[:, u, (j0 + j) * P:(j0 + j + 1) * P],
                                                  core.ident[0:P, 0:P])
                    s = pe.did(ins)
                    q = dve if b == 4 else act
                    q.need(s, out_done.get(g - 2))
                    dst = turned_prob[:, g % 2, j0:j0 + nj, half:half + P]
                    src_ = psum[0:P, b * BANK:b * BANK + nj * P].rearrange("p (j i) -> p j i", i=P)
                    ins = nc.vector.tensor_copy(dst, src_) if b == 4 else nc.scalar.copy(dst, src_)
                    frees.append(q.did(ins))
                prob_free[u] = s
                turn_free[0] = frees
                pair_done[g] = (pair_done.get(g) or []) + frees

            def weigh(g, part):
                h, t = steps[2 * g]
                b = 6 + g % 2
                pe.need(v_done, *pair_done[g])
                if part == 0:
                    pe.need(out_free[g % 2])
                for j in range(5 * part, 5 * part + 5):
                    ins = nc.tensor.matmul(psum[0:128, b * BANK:b * BANK + 2 * P],
                                           v_rows[:, j, h * 128:(h + 1) * 128], turned_prob[:, g % 2, j, :],
                                           start=(j == 0), stop=(j == NT - 1))
                s = pe.did(ins)
                if part == 1:
                    out_done[g] = s
                    act.need(s)
                    out_free[g % 2] = act.did(nc.scalar.copy(q_cols[:, h, t * P:(t + 2) * P],
                                                             psum[0:128, b * BANK:b * BANK + 2 * P]))

            act.need(pe_v)
            dve.need(pe_v)
            pending = {}
            last = len(steps)
            for n in range(last + 1):
                ready = normalise(n - 1, pending[n - 1]) if n >= 1 else None
                if n < last:
                    pending[n] = scores(n)
                g = (n - 3) // 2
                if g >= 0 and n <= last:
                    if (n - 3) % 2 == 0:
                        weigh(g, 0)
                    else:
                        weigh(g, 1)
                if n >= 1:
                    turn_probs(n - 1, ready)
            weigh(last // 2 - 2, 1) if out_done.get(last // 2 - 2) is None else None
            weigh(last // 2 - 1, 0)
            weigh(last // 2 - 1, 1)
            o_done = (act.sem, act.count)
            core.bank_free = [s_free] * 3 + turn_free[0] + out_free
            core.next_bank = 0

            def add_to_x(t, acc, s):
                dve.need(s, x_bo)
                return dve.did(nc.vector.tensor_tensor(x[:, t, :], x[:, t, :], acc, ALU.add))

            os_ = lambda k, start, width: q_cols[:, k, start:start + width]
            rows_product(nc, core, os_, lambda k: w[0][:, k, :], KC, (o_done, got_wo), add_to_x)
            dve.need((dve.sem, dve.count))

            y_ready = conditioned_norm(1, got_c, None)
            pool.need(got_b2, y_ready, (dve.sem, dve.count))
            for t in range(NT):
                x_b2 = pool.did(nc.gpsimd.tensor_tensor(x[:, t, :], x[:, t, :], bias_rows[:, :], ALU.add))

            def to_hidden(o, start, width, acc, s):
                act.need(s)
                return act.did(nc.scalar.activation(k_cols[:, o, start:start + width], acc, ACT.Relu,
                                                    bias=bias_cols[:, 2, o:o + 1]))

            def add_mlp(t, acc, s):
                dve.need(s, x_b2)
                return dve.did(nc.vector.tensor_tensor(x[:, t, :], x[:, t, :], acc, ALU.add))

            cols_product(nc, core, lambda k, o: w[1][:, k, o * 128:(o + 1) * 128], ys, KC, KC,
                         (y_ready, got_m1), to_hidden)
            h_done = (act.sem, act.count)
            rows_product(nc, core, lambda k, s0, n: k_cols[:, k, s0:s0 + n], lambda k: w[2][:, k, :], KC,
                         (h_done, got_m2), add_mlp)
            core.restart()
        core.load(rows_view(gnn_dram), x[:])
        core.restart()


def performer(nc, core, a, xn_dram, gnn_dram, sum_dram):
    pe, dve, act, pool = core.pe, core.dve, core.act, core.pool
    psum = core.psum
    H, DH, F = MIX_HEADS, MIX_DH, MIX_F
    K_SUM_SMALL = 1e-6 * 16.0
    with ExitStack() as ctx:
        sb = lambda name, shape, dt=F32: ctx.enter_context(nc.sbuf_tensor(name, shape, dt))
        x = sb("p_x", [P, NT, D])
        h_rows = sb("p_h_rows", [P, NT, D])
        cols = sb("p_cols", [128, KC, N])
        v_rows = sb("p_v_rows", [P, NT, H, DH + 1])
        q_cols = sb("p_q_cols", [128, KC, N])
        k_cols = sb("p_k_cols", [128, KC, N])
        w = [sb(f"p_w{i}", [128, KC, D]) for i in range(4)]
        pmat = sb("p_pmat", [128, F])
        kf = sb("p_kf", [P, 4, F])
        qf_cols = sb("p_qf_cols", [128, 2, 2, P])
        kv = sb("p_kv", [128, H, 2, DH + 1])
        bias_rows = sb("p_bias_rows", [P, 3, D])
        gb = sb("p_gb", [128, 4, KC])
        bqk = sb("p_bqk", [128, 2, KC])
        b1 = sb("p_b1", [128, MIX_H // 128])
        stat = sb("p_stat", [P, NT, 6])
        mv = sb("p_mv", [P, NT, 2])
        rstd = sb("p_rstd", [P, 2 * NT])
        mx = sb("p_mx", [P, 8])
        rden = sb("p_rden", [P, 4])

        got_x = core.load(x[:], rows_view(xn_dram))
        wqkv = a["L0_mix_Wqkv"].rearrange("(c p) o -> p c o", p=128)
        got_w = [core.load(w[n][:], wqkv[:, :, n * D:(n + 1) * D]) for n in range(3)]
        got_p = [core.load(pmat[0:64, :], a["L0_mix_Pmat"]), core.load(pmat[64:128, :], a["L0_mix_Pmat"])]
        cvec = lambda v: v.rearrange("(c p) -> p c", p=128)
        got_gb = [core.load(gb[:, n, :], cvec(a["L0_mix_" + s])) for n, s in enumerate(("g1", "be1", "g2", "be2"))]
        got_bqk = [core.load(bqk[:, n, :], cvec(a["L0_mix_bqkv"][n * D:(n + 1) * D])) for n in range(2)]
        got_b1 = core.load(b1[:, :], cvec(a["L0_mix_b1"]))
        got_br = [core.load(bias_rows[:, 0, :], a["L0_mix_bqkv"][2 * D:3 * D].partition_broadcast(P)),
                  core.load(bias_rows[:, 1, :], a["L0_mix_bproj"].partition_broadcast(P)),
                  core.load(bias_rows[:, 2, :], a["L0_mix_b2"].partition_broadcast(P))]
        got_wp = core.load(w[3][:], a["L0_mix_Wproj"].rearrange("(c p) o -> p c o", p=128))
        act.need(*got_gb, *got_bqk, got_b1)
        dve.need(*got_bqk, *got_br)

        def norm_to_cols(which, after):
            done = layer_norm_rows(nc, core, x, h_rows, stat, mv, rstd, after=after)
            for t in range(NT):
                b, s = turn_tile(nc, core, h_rows[:, t, :], KC, done[t])
                act.need(s)
                for c in range(KC):
                    ins = nc.scalar.activation(cols[:, c, t * P:(t + 1) * P],
                                               psum[0:128, b * BANK + c * P:b * BANK + (c + 1) * P], ACT.Identity,
                                               bias=gb[:, 2 * which + 1, c:c + 1], scale=gb[:, 2 * which, c:c + 1])
                    core.bank_free[b] = act.did(ins)
            return core.bank_free[b]

        ready = norm_to_cols(0, (got_x,))
        cs = lambda k, start, width: cols[:, k, start:start + width]

        def to_q(o, start, width, acc, s):
            act.need(s)
            return act.did(nc.scalar.activation(q_cols[:, o, start:start + width], acc, ACT.Identity,
                                                bias=bqk[:, 0, o:o + 1]))

        def to_k(o, start, width, acc, s):
            dve.need(s)
            return dve.did(nc.vector.tensor_scalar(k_cols[:, o, start:start + width], acc, bqk[:, 1, o:o + 1],
                                                   None, ALU.add))

        def to_v(t, acc, s):
            dve.need(s)
            return dve.did(nc.vector.tensor_tensor(v_rows[:, t, :, 0:DH], acc.rearrange("p (h d) -> p h d", d=DH),
                                                   bias_rows[:, 0, :].rearrange("p (h d) -> p h d", d=DH), ALU.add))

        one = dve.did(nc.vector.memset(v_rows[:, :, :, DH:DH + 1], 1.0))
        for n, evac in ((1, to_k), (0, to_q)):
            cols_product(nc, core, lambda k, o: w[n][:, k, o * 128:(o + 1) * 128], cs, KC, KC,
                         (ready, got_w[n]), evac)
        rows_product(nc, core, cs, lambda k: w[2][:, k, :], KC, (ready, got_w[2]), to_v)
        qkv_done = [(act.sem, act.count), (dve.sem, dve.count)]
        w1_view = a["L0_mix_W1"].rearrange("(c p) o -> p c o", p=128)
        w2_view = a["L0_mix_W2"].rearrange("(c p) o -> p c o", p=128)
        pe_qkv = (pe.sem, pe.count)
        got_w1 = [core.load(w[0][:], w1_view[:, :, 0:D], pe_qkv), core.load(w[1][:], w1_view[:, :, D:2 * D], pe_qkv)]

        kf_free = [None] * 4

        def feature_map(src, h, t, slot):
            r0 = (h % 2) * DH
            b = core.bank()
            pe.need(*qkv_done, *got_p)
            s = pe.did(nc.tensor.matmul(psum[0:P, b * BANK:b * BANK + F],
                                        src[r0:r0 + DH, h // 2, t * P:(t + 1) * P], pmat[r0:r0 + DH, :],
                                        start=True, stop=True))
            dve.need(s, kf_free[slot])
            s = dve.did(nc.vector.tensor_reduce(mx[:, slot:slot + 1], psum[0:P, b * BANK:b * BANK + F], AX.X,
                                                ALU.max, negate=True))
            act.need(s, kf_free[slot])
            core.bank_free[b] = act.did(nc.scalar.activation(kf[:, slot, :], psum[0:P, b * BANK:b * BANK + F],
                                                             ACT.Exp, bias=mx[:, slot:slot + 1]))
            return core.bank_free[b]

        LAG = 2
        work = [(h, t) for h in range(H) for t in range(NT)]
        got_f = {}
        held = {}
        core.next_bank = 0
        free_acc = {6: core.bank_free[6], 7: core.bank_free[7]}
        for n in range(len(work) + LAG):
            if n < len(work):
                if core.next_bank >= 6:
                    core.next_bank = 0
                got_f[n] = feature_map(k_cols, *work[n], n % 4)
            if n >= LAG:
                m = n - LAG
                h, t = work[m]
                pe.need(got_f[m])
                for half in range(2):
                    if t == 0:
                        pe.need(free_acc[6 + half])
                    ins = nc.tensor.matmul(psum[0:128, (6 + half) * BANK:(6 + half) * BANK + DH + 1],
                                           kf[:, m % 4, half * 128:(half + 1) * 128], v_rows[:, t, h, :],
                                           start=(t == 0), stop=(t == NT - 1))
                s = pe.did(ins)
                kf_free[m % 4] = s
                if t == NT - 1:
                    for half in range(2):
                        dve.need(s)
                        free_acc[6 + half] = dve.did(nc.vector.tensor_copy(
                            kv[:, h, half, :], psum[0:128, (6 + half) * BANK:(6 + half) * BANK + DH + 1]))
        kv_done = free_acc[7]
        dve.need(kv_done)
        kv_done = dve.did(nc.vector.tensor_scalar(kv[:, :, :, DH:DH + 1], kv[:, :, :, DH:DH + 1], K_SUM_SMALL,
                                                  None, ALU.add))
        core.bank_free[6], core.bank_free[7] = free_acc[6], free_acc[7]

        work = [(h, t) for t in range(NT) for h in range(H)]
        qf_free = [None, None]
        qf_ready = {}
        tile_done = {}
        for n in range(len(work) + 2 * LAG):
            if n < len(work):
                h, t = work[n]
                got_f[n] = feature_map(q_cols, h, t, n % 4)
            if LAG <= n < len(work) + LAG:
                m = n - LAG
                b, s = turn_tile(nc, core, kf[:, m % 4, :], 2, got_f[m])
                kf_free[m % 4] = s
                q = act
                q.need(s, qf_free[m % 2])
                core.bank_free[b] = q.did(nc.scalar.copy(qf_cols[:, m % 2, :, :], turned(core, b, n=2)))
                qf_ready[m] = core.bank_free[b]
            if n >= LAG + 1 and n - LAG - 1 < len(work):
                m = n - LAG - 1
                h, t = work[m]
                b = core.bank()
                pe.need(qf_ready[m], kv_done)
                for half in range(2):
                    ins = nc.tensor.matmul(psum[0:P, b * BANK:b * BANK + DH + 1], qf_cols[:, m % 2, half, :],
                                           kv[:, h, half, :], start=(half == 0), stop=(half == 1))
                s = pe.did(ins)
                qf_free[m % 2] = s
                dve.need(s)
                s = dve.did(nc.vector.reciprocal(rden[:, m % 4:m % 4 + 1],
                                                 psum[0:P, b * BANK + DH:b * BANK + DH + 1]))
                dve.need(s)
                core.bank_free[b] = dve.did(nc.vector.tensor_scalar(
                    h_rows[:, t, h * DH:(h + 1) * DH], psum[0:P, b * BANK:b * BANK + DH], rden[:, m % 4:m % 4 + 1],
                    None, ALU.mult))
                tile_done[t] = core.bank_free[b]

        pool.need(*got_br, *qkv_done)
        for t in range(NT):
            x_b = pool.did(nc.gpsimd.tensor_tensor(x[:, t, :], x[:, t, :], bias_rows[:, 1, :], ALU.add))
        rows_to_cols(nc, core, h_rows, cols, tile_done)
        c_done = [(act.sem, act.count), (dve.sem, dve.count)]

        def add_to_x(t, acc, s):
            dve.need(s, x_b)
            return dve.did(nc.vector.tensor_tensor(x[:, t, :], x[:, t, :], acc, ALU.add))

        rows_product(nc, core, cs, lambda k: w[3][:, k, :], KC, (*c_done, got_wp), add_to_x)
        proj_done = (pe.sem, pe.count)
        got_w2 = [core.load(w[2][:], w2_view[:, 0:KC, :], proj_done), core.load(w[3][:], w2_view[:, KC:2 * KC, :], proj_done)]
        ready = norm_to_cols(1, ((dve.sem, dve.count),))
        pool.need(ready, (dve.sem, dve.count))
        for t in range(NT):
            x_b = pool.did(nc.gpsimd.tensor_tensor(x[:, t, :], x[:, t, :], bias_rows[:, 2, :], ALU.add))

        def to_hidden(o, start, width, acc, s):
            act.need(s)
            dst = q_cols if o < KC else k_cols
            return act.did(nc.scalar.activation(dst[:, o % KC, start:start + width], acc, ACT.Gelu,
                                                bias=b1[:, o:o + 1]))

        cols_product(nc, core, lambda k, o: w[o // KC][:, k, (o % KC) * 128:(o % KC + 1) * 128], cs, 2 * KC, KC,
                     (ready, *got_w1), to_hidden)
        h_done = (act.sem, act.count)
        cols_read = (pe.sem, pe.count)
        h2 = v_rows[:, :, :, :].rearrange("p t h d -> p (t h d)")[:, 0:NT * D].rearrange("p (t d) -> p t d", d=D)
        got_g = core.load(h_rows[:], rows_view(gnn_dram), cols_read)
        got_i = core.load(h2, a["x"].rearrange("(t p) d -> p t d", p=P), cols_read)
        pool.need(got_g, got_i)
        for t in range(NT):
            other = pool.did(nc.gpsimd.tensor_tensor(h_rows[:, t, :], h_rows[:, t, :], h2[:, t, :], ALU.add))
        pool.need(other, x_b)
        for t in range(NT):
            x_b = pool.did(nc.gpsimd.tensor_tensor(x[:, t, :], x[:, t, :], h_rows[:, t, :], ALU.add))
        rows_product(nc, core, lambda k, s0, n: (q_cols if k < KC else k_cols)[:, k % KC, s0:s0 + n],
                     lambda k: w[2 + k // KC][:, k % KC, :], 2 * KC, (h_done, *got_w2), add_to_x)
        core.load(rows_view(sum_dram), x[:], (dve.sem, dve.count))
        core.restart()


def moe(nc, core, a, sum_dram, out):
    pe, dve, act, pool = core.pe, core.dve, core.act, core.pool
    psum = core.psum
    S = SLOT_TILES_PADDED
    xf_dram = nc.dram_tensor("normed_rows", [N, D], F32)
    slot_dram = nc.dram_tensor("slot_nodes", [S * 128, 1], I32)
    expert_dram = nc.dram_tensor("slot_experts", [S, 1], I32)
    param_dram = nc.dram_tensor("swiglu_params", [EXPERTS + 1, 8], F32)
    y_dram = nc.dram_tensor("slot_outputs", [SLOT_UNROLL * SLOT_ROUNDS * 128, D], F32)
    with ExitStack() as ctx:
        sb = lambda name, shape, dt=F32: ctx.enter_context(nc.sbuf_tensor(name, shape, dt))
        x = sb("m_x", [P, NT, D])
        weight = sb("m_weight", [P, NT, 2])
        pos = sb("m_pos", [P, 2 * NT], U32)
        slot_node = sb("m_slot_node", [128, S], U32)
        slot_rows_x = sb("m_slot_rows_x", [128, S, D])
        slot_expert = sb("m_slot_expert", [1, S], I32)
        with ExitStack() as first:
            sb1 = lambda name, shape, dt=F32: first.enter_context(nc.sbuf_tensor(name, shape, dt))
            n_rows = sb1("m_n_rows", [P, NT, D])
            cols = sb1("m_cols", [128, KC, N])
            w1 = sb1("m_w1", [128, KC, 2 * FFN_I])
            w2 = sb1("m_w2", [128, IC, D])
            hidden = sb1("m_hidden", [128, IC, N])
            scratch = [sb1(f"m_scratch{i}", [128, 3, 500]) for i in range(2)]
            gate_w = sb1("m_gate_w", [128, KC, EXPERTS])
            gate_b = sb1("m_gate_b", [P, EXPERTS])
            cw = sb1("m_cw", [P, NT, EXPERTS])
            cw_cols = sb1("m_cw_cols", [EXPERTS, N])
            b2 = sb1("m_b2", [EXPERTS, D])
            shared_b2 = sb1("m_shared_b2", [P, D])
            b1 = sb1("m_b1", [128, 2, IC])
            shared_prm = sb1("m_shared_prm", [128, 8])
            stat = sb1("m_stat", [P, NT, 6])
            mv = sb1("m_mv", [P, NT, 2])
            rstd = sb1("m_rstd", [P, 2 * NT])
            logit = sb1("m_logit", [P, NT, EXPERTS])
            top = sb1("m_top", [P, NT, 8])
            top_i = sb1("m_top_i", [P, NT, 8], U32)
            top_f = sb1("m_top_f", [P, NT, 2])
            small = sb1("m_small", [P, NT, 4])
            lane = sb1("m_lane", [P, EXPERTS])
            node_id = sb1("m_node_id", [P, NT], I32)
            zero_slots = sb1("m_zero_slots", [S, 128], I32)
            slot_rows_i = sb1("m_slot_rows_i", [S, 128], I32)
            slot_rows = sb1("m_slot_rows", [S, 128])
            pick = sb1("m_pick", [P, 2, NT, EXPERTS])
            member = sb1("m_member", [P, NT, EXPERTS])
            before = sb1("m_before", [P, P])
            ones = sb1("m_ones", [P, P])
            start_of = sb1("m_start_of", [P, NT + 1, EXPERTS])
            place = sb1("m_place", [P, NT, EXPERTS])
            total = sb1("m_total", [P, EXPERTS])
            tiles_of = sb1("m_tiles_of", [P, 3, EXPERTS])
            pos_f = sb1("m_pos_f", [P, 2, NT])
            slot_id = sb1("m_slot_id", [S, 1])
            passed = sb1("m_passed", [S, EXPERTS])
            expert_f = sb1("m_expert_f", [S, 1])
            expert_i = sb1("m_expert_i", [S, 1], I32)
            prm = sb1("m_prm", [EXPERTS + 1, 8])
            raw = sb1("m_raw", [EXPERTS + 1, 2])

            got_x = core.load(x[:], rows_view(sum_dram))
            got_a = [core.load(prm[0:EXPERTS, 0:5], a["L0_ffn_expert_act"]),
                     core.load(prm[EXPERTS:EXPERTS + 1, 0:5], a["L0_ffn_shared_act"].rearrange("(a n) -> a n", a=1))]
            got = [core.load(gate_w[:], a["L0_ffn_gate_w"].rearrange("(c p) e -> p c e", p=128)),
                   core.load(gate_b[:], a["L0_ffn_gate_b"].partition_broadcast(P)),
                   core.load(b2[:], a["L0_ffn_expert_b2"]),
                   core.load(shared_b2[:], a["L0_ffn_shared_b2"].partition_broadcast(P))]
            got_w1 = core.load(w1[:], a["L0_ffn_shared_w1"].rearrange("(c p) o -> p c o", p=128))
            got_w2 = core.load(w2[:], a["L0_ffn_shared_w2"].rearrange("(c p) o -> p c o", p=128))
            got_b1 = [core.load(b1[:, n, :], a["L0_ffn_shared_b1"].rearrange("(c p n) -> p n c", p=128, n=2)[:, n, :])
                      for n in range(2)]
            pool.did(nc.gpsimd.iota(lane[:], [[1, EXPERTS]], base=0, channel_multiplier=0,
                                    allow_small_or_imprecise_dtypes=True))
            pool.did(nc.gpsimd.iota(slot_id[:], [[0, 1]], base=0, channel_multiplier=1,
                                    allow_small_or_imprecise_dtypes=True))
            s = pool.did(nc.gpsimd.iota(node_id[:], [[P, NT]], base=0, channel_multiplier=1))
            pool.did(nc.gpsimd.memset(ones[:], 1.0))
            pool.did(nc.gpsimd.memset(zero_slots[:], 0))
            s = pool.did(nc.gpsimd.memset(before[:], 1.0))
            pool.need(s)
            consts = pool.did(nc.gpsimd.affine_select(out=before[:], in_=before[:], compare_op=ALU.is_gt, fill=0.0,
                                                      base=0, pattern=[[1, P]], channel_multiplier=-1))
            zeroed = core.load(slot_dram[:, :].rearrange("(s p) a -> s (p a)", p=128), zero_slots[:], consts)

            dve.need(*got_a)
            s = dve.did(nc.vector.scalar_tensor_tensor(raw[:], prm[:, 3:5], -1.0, prm[:, 3:5], ALU.mult, ALU.max))
            act.need(s)
            s = act.did(nc.scalar.activation(raw[:], raw[:], ACT.Exp, scale=-1.0))
            act.need(s)
            s = act.did(nc.scalar.activation(raw[:], raw[:], ACT.Ln, bias=1.0))
            dve.need(s)
            s = dve.did(nc.vector.scalar_tensor_tensor(prm[:, 3:5], prm[:, 3:5], 0.0, raw[:], ALU.max, ALU.add))
            dve.need(s)
            dve.did(nc.vector.tensor_scalar(prm[:, 5:7], prm[:, 3:5], -1.0, None, ALU.mult))
            s = dve.did(nc.vector.memset(prm[:, 7:8], 0.0))
            s = core.load(param_dram[:, :], prm[:], s)
            got_prm = core.load(shared_prm[:], param_dram[EXPERTS, :].partition_broadcast(128), s)

            done = layer_norm_rows(nc, core, x, n_rows, stat, mv, rstd, after=(got_x,))
            xf_stored = core.load(rows_view(xf_dram), n_rows[:], done[-1])
            rows_to_cols(nc, core, n_rows, cols, done)
            ready = [(act.sem, act.count), (dve.sem, dve.count)]
            pe.need(*ready, *got)
            dve.need(*got, consts)
            for t in range(NT):
                b = core.bank()
                for k in range(KC):
                    ins = nc.tensor.matmul(psum[0:P, b * BANK:b * BANK + EXPERTS], cols[:, k, t * P:(t + 1) * P],
                                           gate_w[:, k, :], start=(k == 0), stop=(k == KC - 1))
                s = pe.did(ins)
                dve.need(s)
                core.bank_free[b] = s = dve.did(nc.vector.tensor_tensor(
                    logit[:, t, :], psum[0:P, b * BANK:b * BANK + EXPERTS], gate_b[:, :], ALU.add))
            dve.need(s)
            s = dve.did(nc.vector.tensor_reduce(small[:, :, 0], logit[:], AX.X, ALU.max))
            dve.need(s)
            s = dve.did(nc.vector.tensor_scalar(small[:, :, 0], small[:, :, 0], -1.0, None, ALU.mult))
            act.need(s)
            for t in range(NT):
                s = act.did(nc.scalar.activation(logit[:, t, :], logit[:, t, :], ACT.Exp, bias=small[:, t, 0:1],
                                                 accum_out=small[:, t, 1:2]))
            dve.need(s)
            s = dve.did(nc.vector.reciprocal(small[:, :, 2], small[:, :, 1]))
            dve.need(s)
            for t in range(NT):
                s = dve.did(nc.vector.tensor_scalar(logit[:, t, :], logit[:, t, :], small[:, t, 2:3], None, ALU.mult))
            dve.need(s)
            for t in range(NT):
                s = dve.did(nc.vector.max(top[:, t, :], logit[:, t, :]))
            dve.need(s)
            for t in range(NT):
                s = dve.did(nc.vector.max_index(top_i[:, t, :], top[:, t, :], logit[:, t, :]))
            dve.need(s)
            s = dve.did(nc.vector.tensor_copy(top_f[:], top_i[:, :, 0:2]))
            s = dve.did(nc.vector.tensor_tensor(small[:, :, 0], top[:, :, 0], top[:, :, 1], ALU.add))
            dve.need(s)
            s = dve.did(nc.vector.reciprocal(small[:, :, 1], small[:, :, 0]))
            dve.need(s)
            for n in range(2):
                s = dve.did(nc.vector.tensor_tensor(weight[:, :, n], top[:, :, n], small[:, :, 1], ALU.mult))
            dve.need(s)
            for t in range(NT):
                for n in range(2):
                    s = dve.did(nc.vector.tensor_scalar(pick[:, n, t, :], lane[:, :], top_f[:, t, n:n + 1], None,
                                                        ALU.is_equal))
            dve.need(s)
            s = dve.did(nc.vector.tensor_tensor(member[:], pick[:, 0], pick[:, 1], ALU.add))
            flat = lambda v: v.rearrange("p t e -> p (t e)")
            pe.need(s, consts)
            b_rank, b_tot = core.bank(), core.bank()
            bank = lambda b, n=NT * EXPERTS, p=P: psum[0:p, b * BANK:b * BANK + n]
            nc.tensor.matmul(bank(b_rank), before[:, :], flat(member[:]), start=True, stop=True)
            s = pe.did(nc.tensor.matmul(bank(b_tot), ones[:, :], flat(member[:]), start=True, stop=True))
            dve.need(s)
            s = dve.did(nc.vector.tensor_reduce(total[:], bank(b_tot).rearrange("p (t e) -> p e t", e=EXPERTS), AX.X,
                                                ALU.add))
            dve.need(s)
            s = dve.did(nc.vector.tensor_scalar(tiles_of[:, 0, :], total[:], 1.0 / 128, 127.0 / 256, ALU.mult, ALU.add))
            dve.need(s)
            s = dve.did(nc.vector.tensor_scalar(tiles_of[:, 0, :], tiles_of[:, 0, :], ROUND, None, ALU.add))
            dve.need(s)
            s = dve.did(nc.vector.tensor_scalar(tiles_of[:, 0, :], tiles_of[:, 0, :], -ROUND, None, ALU.add))
            dve.need(s)
            s = dve.did(nc.vector.tensor_copy(tiles_of[:, 1, :], tiles_of[:, 0, :]))
            dve.need(s)
            cur, step = 1, 1
            while step < EXPERTS:
                other = 3 - cur
                dve.did(nc.vector.tensor_copy(tiles_of[:, other, 0:step], tiles_of[:, cur, 0:step]))
                s = dve.did(nc.vector.tensor_tensor(tiles_of[:, other, step:], tiles_of[:, cur, step:],
                                                    tiles_of[:, cur, 0:EXPERTS - step], ALU.add))
                dve.need(s)
                cur, step = other, 2 * step
            ends = tiles_of[:, cur, :]
            s = dve.did(nc.vector.tensor_tensor(start_of[:, 0, :], ends, tiles_of[:, 0, :], ALU.subtract))
            s2 = dve.did(nc.vector.tensor_scalar(passed[:], tiles_of[0:S, cur, :], slot_id[:, 0:1], None, ALU.is_le))
            dve.need(s, s2)
            s = dve.did(nc.vector.tensor_scalar(start_of[:, 0, :], start_of[:, 0, :], 128.0, None, ALU.mult))
            s2 = dve.did(nc.vector.tensor_reduce(expert_f[:], passed[:], AX.X, ALU.add))
            dve.need(s, s2)
            s2 = dve.did(nc.vector.tensor_scalar(expert_i[:], expert_f[:], float(EXPERTS - 1), None, ALU.min))
            s2 = core.load(expert_dram[:, :], expert_i[:], s2)
            got_e = core.load(slot_expert[:], expert_dram[:, :].rearrange("s a -> (s a)").rearrange(
                "(a s) -> a s", a=1), s2)
            for t in range(NT):
                s = dve.did(nc.vector.tensor_tensor(start_of[:, t + 1, :], start_of[:, t, :],
                                                    psum[0:P, b_tot * BANK + t * EXPERTS:b_tot * BANK + (t + 1) * EXPERTS],
                                                    ALU.add))
                dve.need(s)
            s = dve.did(nc.vector.tensor_tensor(flat(place[:]), bank(b_rank), flat(start_of[:, 0:NT, :]), ALU.add))
            core.bank_free[b_rank] = core.bank_free[b_tot] = s
            dve.need(s)
            for n in range(2):
                s = dve.did(nc.vector.tensor_tensor(member[:], place[:], pick[:, n], ALU.mult))
                dve.need(s)
                s = dve.did(nc.vector.tensor_reduce(pos_f[:, n, :], member[:], AX.X, ALU.add))
                dve.need(s)
            s = dve.did(nc.vector.tensor_copy(pos[:, :], pos_f[:].rearrange("p n t -> p (n t)")))
            pool.need(s, zeroed)
            scattered = []
            for n in range(2):
                for t in range(NT):
                    i = n * NT + t
                    scattered.append(core.indirect(slot_dram[:, :], node_id[:, t:t + 1], pos[:, i:i + 1], scatter=True))
            got_s = core.load(slot_rows_i[:], slot_dram[:, :].rearrange("(s p) a -> s (p a)", p=128), *scattered)

            dve.need(got_s)
            s = dve.did(nc.vector.tensor_copy(slot_rows[:], slot_rows_i[:]))
            pe.need(s)
            b = core.bank()
            s = pe.did(nc.tensor.transpose(psum[0:128, b * BANK:b * BANK + S], slot_rows[:, :], core.ident[0:S, 0:S]))
            dve.need(s)
            core.bank_free[b] = dve.did(nc.vector.tensor_copy(slot_node[:], psum[0:128, b * BANK:b * BANK + S]))
            pool.need(core.bank_free[b], xf_stored)
            for i in range(S):
                core.indirect(xf_dram[:, :], slot_rows_x[:, i, :], slot_node[:, i:i + 1], scatter=False)

            for t in range(NT):
                for n in range(2):
                    s = dve.did(nc.vector.tensor_scalar(pick[:, n, t, :], pick[:, n, t, :], weight[:, t, n:n + 1],
                                                        None, ALU.mult))
            dve.need(s)
            s = dve.did(nc.vector.tensor_tensor(cw[:], pick[:, 0], pick[:, 1], ALU.add))
            for t in range(NT):
                b, s2 = turn_tile(nc, core, cw[:, t, :], 1, s, width=EXPERTS)
                dve.need(s2)
                core.bank_free[b] = last = dve.did(nc.vector.tensor_copy(cw_cols[:, t * P:(t + 1) * P],
                                                                         psum[0:EXPERTS, b * BANK:b * BANK + P]))
            pool.need(*got, done[-1])
            for t in range(NT):
                x_b = pool.did(nc.gpsimd.tensor_tensor(x[:, t, :], x[:, t, :], shared_b2[:, :], ALU.add))
            pe.need(last)
            for t in range(NT):
                b = core.bank()
                s = pe.did(nc.tensor.matmul(psum[0:P, b * BANK:b * BANK + D], cw_cols[:, t * P:(t + 1) * P],
                                            b2[:, :], start=True, stop=True))
                dve.need(s, x_b)
                core.bank_free[b] = dve.did(nc.vector.tensor_tensor(x[:, t, :], x[:, t, :],
                                                                    psum[0:P, b * BANK:b * BANK + D], ALU.add))

            act.need(got_prm, *got_b1)
            dve.need(got_prm)
            q = shared_prm
            free = [None, None]
            n = 0
            for start, width in SPANS:
                for c in range(IC):
                    g_, u_, sg = (scratch[n % 2][:, i, 0:width] for i in range(3))
                    banks = []
                    for half in range(2):
                        b = core.bank()
                        pe.need(got_w1)
                        for k in range(KC):
                            col = c * 256 + half
                            ins = nc.tensor.matmul(psum[0:128, b * BANK:b * BANK + width],
                                                   w1[:, k, col:col + 255:2], cols[:, k, start:start + width],
                                                   start=(k == 0), stop=(k == KC - 1))
                        banks.append((b, pe.did(ins)))
                    act.need(free[n % 2])
                    for half, dst in enumerate((g_, u_)):
                        b, s = banks[half]
                        act.need(s)
                        core.bank_free[b] = act.did(nc.scalar.activation(
                            dst, psum[0:128, b * BANK:b * BANK + width], ACT.Identity, bias=b1[:, half, c:c + 1]))
                        dve.need(core.bank_free[b])
                        s = dve.did(nc.vector.tensor_scalar(dst, dst, q[:, 3 + half:4 + half],
                                                            q[:, 5 + half:6 + half], ALU.min, ALU.max))
                        if half == 0:
                            act.need(s)
                            sig = act.did(nc.scalar.activation(sg, g_, ACT.Sigmoid, scale=q[:, 0:1]))
                    dve.need(sig)
                    s = dve.did(nc.vector.scalar_tensor_tensor(sg, g_, q[:, 1:2], sg, ALU.mult, ALU.mult))
                    dve.need(s)
                    free[n % 2] = dve.did(nc.vector.scalar_tensor_tensor(
                        hidden[:, c, start:start + width], u_, q[:, 2:3], sg, ALU.add, ALU.mult))
                    n += 1
            h_done = (dve.sem, dve.count)

            def add_shared(t, acc, s):
                dve.need(s)
                return dve.did(nc.vector.tensor_tensor(x[:, t, :], x[:, t, :], acc, ALU.add))

            rows_product(nc, core, lambda k, s0, m: hidden[:, k, s0:s0 + m], lambda k: w2[:, k, :], IC,
                         (h_done, got_w2), add_shared)
            core.restart()

        U = SLOT_UNROLL
        loop = ctx.enter_context(ExitStack())
        sb = lambda name, shape, dt=F32: loop.enter_context(nc.sbuf_tensor(name, shape, dt))
        rows = [sb(f"m_rows{i}", [128, D]) for i in range(2)]
        ew1 = [sb(f"m_ew1_{i}", [128, KC, 2 * FFN_I]) for i in range(U)]
        ew2 = [sb(f"m_ew2_{i}", [128, IC, D]) for i in range(U)]
        eb1 = [sb(f"m_eb1_{i}", [128, 2 * FFN_I]) for i in range(U)]
        eprm = [sb(f"m_eprm{i}", [128, 8]) for i in range(U)]
        x_cols = [sb(f"m_x_cols{i}", [128, KC, 128]) for i in range(2)]
        h = [sb(f"m_h{i}", [128, 2 * FFN_I]) for i in range(2)]
        gate = [sb(f"m_gate{i}", [128, FFN_I]) for i in range(2)]
        t_cols = [sb(f"m_t_cols{i}", [128, IC, 128]) for i in range(2)]
        y = [sb(f"m_y{i}", [128, D]) for i in range(2)]

        def load_tile(slot, u, *free):
            core.sp.need(*free)
            e = nc.sync.value_load(slot_expert[0:1, ds(slot, 1)], min_val=0, max_val=EXPERTS - 1)
            got = []
            got.append(core.load(ew1[u][:], a["L0_ffn_expert_w1"][ds(e, 1), :, :].rearrange(
                "l (c p) o -> p (l c) o", p=128)))
            got.append(core.load(eb1[u][:], a["L0_ffn_expert_b1"][ds(e, 1), :].rearrange("l o -> (l o)")
                                 .partition_broadcast(128)))
            got.append(core.load(eprm[u][:], param_dram[ds(e, 1), :].rearrange("l o -> (l o)")
                                 .partition_broadcast(128)))
            got.append(core.load(ew2[u][:], a["L0_ffn_expert_w2"][ds(e, 1), :, :].rearrange(
                "l (c p) o -> p (l c) o", p=128)))
            return got

        def turn_into(src, n, dst, ready, free):
            pe.need(ready)
            b = core.bank()
            for c in range(n):
                ins = nc.tensor.transpose(psum[0:128, b * BANK + c * 128:b * BANK + (c + 1) * 128],
                                          src[:, c * 128:(c + 1) * 128], core.ident[:, :])
            s = pe.did(ins)
            act.need(s, free)
            core.bank_free[b] = act.did(nc.scalar.copy(dst, psum[0:128, b * BANK:b * BANK + n * 128].rearrange(
                "p (c n) -> p c n", n=128)))
            return core.bank_free[b]

        UP_BANKS = (0, 2)
        load_tile(0, 0)
        load_tile(1, 1)
        core.restart()
        with nc.Fori(0, SLOT_ROUNDS) as it:
            got = {}
            h_free = [None, None]
            up_free = [None, None]
            rows_free = [None, None]
            x_free, t_free, y_free = [None, None], [None, None], [None, None]
            done1, done2 = {}, {}
            core.next_bank = 4

            def bank_small():
                if core.next_bank < 4 or core.next_bank > 7:
                    core.next_bank = 4
                b = core.next_bank
                core.next_bank = 4 + (b - 3) % 4
                pe.need(core.bank_free[b])
                return b

            core.bank, kept = bank_small, core.bank
            for u in range(2, U):
                got[u] = load_tile(U * it + u, u)

            def up(u):
                v = u % 2
                need = got.get(u, [])
                pe.need(*need)
                pool.need(rows_free[v])
                s = pool.did(nc.gpsimd.tensor_copy(rows[v][:], slot_rows_x[:, ds(U * it + u, 1), :].rearrange(
                    "p a d -> p (a d)")))
                s = rows_free[v] = turn_into(rows[v], KC, x_cols[v][:], s, x_free[v])
                pe.need(s, up_free[v])
                base = UP_BANKS[v] * BANK
                for c0, cn in ((0, 512), (512, 256)):
                    for k in range(KC):
                        ins = nc.tensor.matmul(psum[0:128, base + c0:base + c0 + cn], x_cols[v][:, k, :],
                                               ew1[u][:, k, c0:c0 + cn], start=(k == 0), stop=(k == KC - 1))
                s = x_free[v] = pe.did(ins)
                done1[u] = s
                q = eprm[u]
                dve.need(s, *need, h_free[v])
                act.need(*need)
                up_free[v] = s = dve.did(nc.vector.tensor_tensor(h[v][:], psum[0:128, base:base + 2 * FFN_I],
                                                                 eb1[u][:], ALU.add))
                dve.need(s)
                g_, u_ = h[v][:, 0:2 * FFN_I:2], h[v][:, 1:2 * FFN_I:2]
                s = dve.did(nc.vector.tensor_scalar(g_, g_, q[:, 3:4], q[:, 5:6], ALU.min, ALU.max))
                dve.did(nc.vector.tensor_scalar(u_, u_, q[:, 4:5], q[:, 6:7], ALU.min, ALU.max))
                act.need(s)
                s = act.did(nc.scalar.activation(gate[v][:], g_, ACT.Sigmoid, scale=q[:, 0:1]))
                dve.need(s)
                s = dve.did(nc.vector.scalar_tensor_tensor(gate[v][:], g_, q[:, 1:2], gate[v][:], ALU.mult, ALU.mult))
                dve.need(s)
                return dve.did(nc.vector.scalar_tensor_tensor(gate[v][:], u_, q[:, 2:3], gate[v][:],
                                                              ALU.add, ALU.mult))

            def down(u, ready):
                v = u % 2
                s = turn_into(gate[v], IC, t_cols[v][:], ready, t_free[v])
                h_free[v] = s
                b = core.bank()
                pe.need(s)
                for k in range(IC):
                    ins = nc.tensor.matmul(psum[0:128, b * BANK:b * BANK + D], t_cols[v][:, k, :], ew2[u][:, k, :],
                                           start=(k == 0), stop=(k == IC - 1))
                s = t_free[v] = done2[u] = pe.did(ins)
                act.need(s, y_free[v])
                core.bank_free[b] = s = act.did(nc.scalar.copy(y[v][:], psum[0:128, b * BANK:b * BANK + D]))
                y_free[v] = core.load(y_dram[ds((U * it + u) * 128, 128), :], y[v][:], s, by=core.act)

            swiglu = {}
            for u in range(U + 1):
                if u < U:
                    swiglu[u] = up(u)
                if u >= 1:
                    down(u - 1, swiglu[u - 1])
                if 1 <= u <= 2:
                    load_tile(U * it + U + u - 1, u - 1, done1[u - 1], done2[u - 1], swiglu[u - 1])
            core.bank = kept
            core.restart()

        loop.close()
        sb = lambda name, shape, dt=F32: ctx.enter_context(nc.sbuf_tensor(name, shape, dt))
        back = [sb(f"m_back{i}", [P, D]) for i in range(4)]
        free = [None] * 4
        for i in range(2 * NT):
            n, t = i % 2, i // 2
            j = n * NT + t
            pool.need(free[i % 4])
            s = core.indirect(y_dram[:, :], back[i % 4][:], pos[:, j:j + 1], scatter=False)
            dve.need(s)
            free[i % 4] = s = dve.did(nc.vector.scalar_tensor_tensor(x[:, t, :], back[i % 4][:], weight[:, t, n:n + 1],
                                                                     x[:, t, :], ALU.mult, ALU.add))
            dve.need(s)
            if n == 1:
                core.load(out[t * P:(t + 1) * P, :], x[:, t, :], s)
        core.restart()


_INS = ['x', 'src', 'dst', 'node_vec1', 'L0_gnn_f_w1', 'L0_gnn_f_b1', 'L0_gnn_f_w2', 'L0_gnn_f_b2', 'L0_gnn_s1_w',
        'L0_gnn_s1_b', 'L0_gnn_b1_w', 'L0_gnn_b1_b', 'L0_gnn_wq', 'L0_gnn_bq', 'L0_gnn_wk', 'L0_gnn_bk',
        'L0_gnn_wv', 'L0_gnn_bv', 'L0_gnn_wo', 'L0_gnn_bo', 'L0_gnn_s2_w', 'L0_gnn_s2_b', 'L0_gnn_b2_w',
        'L0_gnn_b2_b', 'L0_gnn_m_w1', 'L0_gnn_m_b1', 'L0_gnn_m_w2', 'L0_gnn_m_b2', 'L0_mix_Wqkv', 'L0_mix_bqkv',
        'L0_mix_Pmat', 'L0_mix_Wproj', 'L0_mix_bproj', 'L0_mix_W1', 'L0_mix_b1', 'L0_mix_W2', 'L0_mix_b2',
        'L0_mix_g1', 'L0_mix_be1', 'L0_mix_g2', 'L0_mix_be2', 'L0_ffn_gate_w', 'L0_ffn_gate_b',
        'L0_ffn_shared_w1', 'L0_ffn_shared_b1', 'L0_ffn_shared_w2', 'L0_ffn_shared_b2', 'L0_ffn_shared_act',
        'L0_ffn_expert_w1', 'L0_ffn_expert_b1', 'L0_ffn_expert_w2', 'L0_ffn_expert_b2', 'L0_ffn_expert_act']


def kernel(**inputs):
    import numpy as _np
    import concourse.bacc as _bacc
    from concourse import mybir as _mybir
    from concourse.bass_utils import run_bass_kernel_spmd as _run

    nc = _bacc.Bacc("TRN2", target_bir_lowering=False, num_devices=1)
    arrays, aps = {}, {}
    for name in _INS:
        v = _np.ascontiguousarray(inputs[name])
        arrays[f"in_{name}"] = v
        aps[name] = nc.dram_tensor(f"in_{name}", v.shape, _mybir.dt.from_np(v.dtype), kind="ExternalInput").ap()
    out = nc.dram_tensor("out_0", (N, D), F32, kind="ExternalOutput").ap()
    build(nc, aps, out)
    r = _run(nc, [arrays], core_ids=[0])
    return r.results[0]["out_0"]
```

```python
from contextlib import ExitStack

import concourse.bass as bass
from concourse import mybir

F32 = mybir.dt.float32
F16 = mybir.dt.float16
BF16 = mybir.dt.bfloat16
I32 = mybir.dt.int32
U32 = mybir.dt.uint32
ALU = mybir.AluOpType
ACT = mybir.ActivationFunctionType
AX = mybir.AxisListType
ENG = mybir.EngineType
ds = bass.ds

N = 1250
D = 512
P = 125
NT = N // P
KC = D // 128
EPS = 1e-5
NOT_AN_EDGE = -1e30
BANK = 512
SPANS = [(0, 500), (500, 500), (1000, 250)]
GNN_LAYERS = 4
GNN_HEADS = 4
COND = 16
COND_ROWS = COND + 2
PART_PAIRS = [(0, 0), (0, 1), (1, 0), (0, 2), (1, 1), (2, 0)]
FREQ = 32
E_EDGES = 41250
EDGE_TILES = 4
HOT_RING = 8
HOT_DST = 8
EDGE_GROUPS = -(-E_EDGES // (128 * EDGE_TILES))
WINDOW = E_EDGES * P * 11 // (N * 10 * 128 * EDGE_TILES) + 2
MIX_HEADS = 8
MIX_DH = 64
MIX_F = 256
MIX_H = 1024
EXPERTS = 16
FFN_I = 384
IC = FFN_I // 128
SLOT_TILES = (2 * N + EXPERTS * 127) // 128
SLOT_UNROLL = 3
SLOT_ROUNDS = -(-SLOT_TILES // SLOT_UNROLL)
SLOT_COLS_TILES = SLOT_UNROLL * SLOT_ROUNDS
SLOT_TILES_PADDED = SLOT_COLS_TILES + 1
HW_DMAS, SW_DMAS = 24, 8
ROUND = 1.5 * 2.0 ** 23


class Queue:

    def __init__(self, eng, sem, loop):
        self.eng, self.sem, self.loop = eng, sem, loop
        self.count, self.seen = 0, {}

    def did(self, ins):
        ins.then_inc(self.sem, 1)
        self.count += 1
        return (self.sem, self.count)

    def need(self, *done):
        for d in done:
            if d is None:
                continue
            sem, value = d
            if self.seen.get(sem.name, -(1 << 30)) < value:
                self.loop.wait(self.eng, sem, value)
                self.seen[sem.name] = value


class Loop:

    def __init__(self):
        self.before, self.each, self.iteration = {}, {}, 0

    def wait(self, eng, sem, value):
        value = value + self.before.get(sem.name, 0)
        each = self.each.get(sem.name, 0)
        if each:
            eng.wait_ge(sem, self.iteration * each + value)
        elif value > 0:
            eng.wait_ge(sem, value)


class Core:
    def __init__(self, nc, ctx):
        self.nc = nc
        self.loop = Loop()
        mk = lambda name: ctx.enter_context(nc.semaphore(name))
        self.pe = Queue(nc.tensor, mk("pe_done"), self.loop)
        self.dve = Queue(nc.vector, mk("dve_done"), self.loop)
        self.act = Queue(nc.scalar, mk("act_done"), self.loop)
        self.pool = Queue(nc.gpsimd, mk("pool_done"), self.loop)
        self.sp = Queue(nc.sync, mk("sp_unused"), self.loop)
        self.dma_sems = [mk(f"dma_done{i}") for i in range(HW_DMAS)]
        self.queues = [self.pe, self.dve, self.act, self.pool, self.sp]
        sems = [q.sem for q in self.queues] + self.dma_sems
        self.first = min(s.num for s in sems)
        self.last = max(s.num for s in sems)
        assert self.last - self.first == len(sems) - 1
        self.dma_count = [0] * len(self.dma_sems)
        self.next_dma = 0
        self.sw_sems = [mk(f"pool_dma_done{i}") for i in range(SW_DMAS)]
        self.sw_count, self.next_sw_dma = [0] * SW_DMAS, 0
        self.bank_free = [None] * 8
        self.next_bank = 0
        self.ring = 8

    def load(self, out, in_, *after, by=None):
        q = by or self.sp
        q.need(*after)
        n = self.next_dma
        self.next_dma = (n + 1) % HW_DMAS
        q.need((self.dma_sems[n], 16 * self.dma_count[n]))
        q.eng.dma_start(out, in_, allow_slow_non_contiguous=True).then_inc(self.dma_sems[n], 16)
        self.dma_count[n] += 1
        return (self.dma_sems[n], 16 * self.dma_count[n])

    def indirect(self, dram, sbuf, index, scatter):
        n = self.next_sw_dma
        self.next_sw_dma = (n + 1) % SW_DMAS
        if self.sw_count[n]:
            self.pool.need((self.sw_sems[n], 16 * self.sw_count[n]))
        at = bass.IndirectOffsetOnAxis(ap=index, axis=0)
        if scatter:
            ins = self.nc.gpsimd.indirect_dma_start(out=dram, out_offset=at, in_=sbuf, in_offset=None)
        else:
            ins = self.nc.gpsimd.indirect_dma_start(out=sbuf, out_offset=None, in_=dram, in_offset=at)
        ins.then_inc(self.sw_sems[n], 16)
        self.sw_count[n] += 1
        return (self.sw_sems[n], 16 * self.sw_count[n])

    def restart(self):
        for n, c in enumerate(self.dma_count):
            if c:
                self.sp.need((self.dma_sems[n], 16 * c))
        for n, c in enumerate(self.sw_count):
            if c:
                self.sp.need((self.sw_sems[n], 16 * c))
        self.nc.all_engine_barrier(sems_to_clear=range(self.first, self.last + 1))
        for q in self.queues:
            q.count, q.seen = 0, {}
        self.dma_count = [0] * len(self.dma_sems)
        self.next_dma = 0
        self.bank_free = [None] * 8
        self.next_bank = 0

    def counted(self):
        n = {q.sem.name: q.count for q in self.queues}
        n.update({sem.name: 16 * c for sem, c in zip(self.dma_sems, self.dma_count)})
        return n

    def count_anew(self):
        for q in self.queues:
            q.count, q.seen = 0, {}
        self.dma_count = [0] * len(self.dma_sems)
        self.next_dma = 0

    def enter_loop(self):
        self.loop.before = self.counted()
        self.count_anew()
        return self.loop.before

    def next_iterations(self, iteration):
        self.loop.each, self.loop.iteration = self.counted(), iteration
        self.count_anew()
        return self.loop.each

    def leave_loop(self, iterations):
        assert self.counted() == self.loop.each
        total = {k: v + iterations * self.loop.each[k] for k, v in self.loop.before.items()}
        since = {k: self.loop.each[k] - v for k, v in total.items()}
        self.loop.before, self.loop.each, self.loop.iteration = {}, {}, 0
        for q in self.queues:
            q.count, q.seen = total[q.sem.name], {}
        self.dma_count = [total[sem.name] // 16 for sem in self.dma_sems]
        return since

    def bank(self):
        b = self.next_bank
        self.next_bank = (b + 1) % self.ring
        self.pe.need(self.bank_free[b])
        return b


def earlier(tokens, counted):
    return {key: [(sem, value - counted.get(sem.name, 0)) for sem, value in group] for key, group in tokens.items()}


def build(nc, a, out):
    with ExitStack() as ctx:
        core = Core(nc, ctx)
        psum = ctx.enter_context(nc.psum_tensor("psum", [128, 8 * BANK], F32))
        ident = ctx.enter_context(nc.sbuf_tensor("ident", [128, 128], F32))
        xn_dram = nc.dram_tensor("xn_scratch", [N, D], F32)
        flag_dram = nc.dram_tensor("flag_scratch", [NT, EDGE_GROUPS], I32)
        window_dram = nc.dram_tensor("window_scratch", [NT, 2], I32)
        core.psum, core.ident = psum, ident

        m = core.pool.did(nc.gpsimd.memset(ident[:], 0.0))
        core.pool.need(m)
        core.pool.did(nc.gpsimd.affine_select(out=ident[:], in_=ident[:], compare_op=ALU.not_equal, fill=1.0,
                                              base=0, pattern=[[-1, 128]], channel_multiplier=1))
        core.restart()
        x = ctx.enter_context(nc.sbuf_tensor("x", [P, NT, D], F32))
        with nc.sbuf_tensor("ln_count", [P, NT, N], F32) as ln_count:
            with nc.sbuf_tensor("cond", [COND_ROWS, N], F32) as cond:
                edge_counts(nc, core, a, flag_dram, window_dram, ln_count, x, xn_dram, cond)
                gnn(nc, core, a, x, cond, ln_count)
        performer(nc, core, a, x, xn_dram)
        moe(nc, core, a, x, out)
        core.restart()


def rows_view(dram):
    return dram[:, :].rearrange("(t p) d -> p t d", p=P)


def layer_norm_rows(nc, core, x, out, stat, mv, rstd, after=(), out_free=()):
    dve, act = core.dve, core.act
    for t in range(NT):
        dve.need(*after)
        s = dve.did(nc.vector.bn_stats(stat[:, t, :], x[:, t, :]))
    dve.need(s)
    for t in range(NT):
        s = dve.did(nc.vector.bn_aggr(mv[:, t, :], stat[:, t, :]))
    dve.need(s)
    s = dve.did(nc.vector.tensor_scalar(rstd[:, 0:NT], mv[:, :, 1], EPS, None, ALU.add))
    act.need(s)
    s = act.did(nc.scalar.activation(rstd[:, NT:2 * NT], rstd[:, 0:NT], ACT.Sqrt))
    dve.need(s)
    s = dve.did(nc.vector.reciprocal(rstd[:, 0:NT], rstd[:, NT:2 * NT]))
    dve.need(s, *out_free)
    return [dve.did(nc.vector.tensor_scalar(out[:, t, :], x[:, t, :], mv[:, t, 0:1], rstd[:, t:t + 1],
                                            ALU.subtract, ALU.mult)) for t in range(NT)]


class TileNorm:

    def __init__(self, nc, core, x, out, stat, mv, rstd, turn):
        self.nc, self.core, self.x, self.out = nc, core, x, out
        self.stat, self.mv, self.rstd, self.turn = stat, mv, rstd, turn
        self.ready, self.normed = {}, {}

    def tile(self, t, x_done):
        if t < NT:
            self.start(t, x_done)
        if 1 <= t <= NT:
            self.normalise(t - 1)
        if t >= 2:
            self.turn(t - 2, self.normed[t - 2])

    def finish(self):
        self.tile(NT, None)
        self.tile(NT + 1, None)

    def start(self, t, x_done):
        nc, dve, act = self.nc, self.core.dve, self.core.act
        stat, mv, rstd = self.stat, self.mv, self.rstd
        dve.need(x_done)
        s = dve.did(nc.vector.bn_stats(stat[:, t, :], self.x[:, t, :]))
        dve.need(s)
        s = dve.did(nc.vector.bn_aggr(mv[:, t, :], stat[:, t, :]))
        dve.need(s)
        s = dve.did(nc.vector.tensor_scalar(rstd[:, t:t + 1], mv[:, t, 1:2], EPS, None, ALU.add))
        act.need(s)
        self.ready[t] = act.did(nc.scalar.activation(rstd[:, NT + t:NT + t + 1], rstd[:, t:t + 1], ACT.Sqrt))

    def normalise(self, t):
        nc, dve, mv, rstd = self.nc, self.core.dve, self.mv, self.rstd
        dve.need(self.ready[t])
        s = dve.did(nc.vector.reciprocal(rstd[:, t:t + 1], rstd[:, NT + t:NT + t + 1]))
        dve.need(s)
        self.normed[t] = dve.did(nc.vector.tensor_scalar(self.out[:, t, :], self.x[:, t, :], mv[:, t, 0:1],
                                                         rstd[:, t:t + 1], ALU.subtract, ALU.mult))


def turn_tile(nc, core, src, n_chunks, done, width=128):
    pe = core.pe
    pe.need(done)
    b = core.bank()
    for c in range(n_chunks):
        ins = nc.tensor.transpose(core.psum[0:width, b * BANK + c * P:b * BANK + (c + 1) * P],
                                  src[:, c * width:(c + 1) * width], core.ident[0:P, 0:P])
    return b, pe.did(ins)


def turned(core, b, rows=128, n=KC):
    return core.psum[0:rows, b * BANK:b * BANK + n * P].rearrange("p (c n) -> p c n", n=P)


def cols_product(nc, core, w, x, n_out, k_chunks, ready, evacuate):
    pe = core.pe
    for start, width in SPANS:
        pe.need(*ready)
        for o in range(n_out):
            b = core.bank()
            for k in range(k_chunks):
                ins = nc.tensor.matmul(core.psum[0:128, b * BANK:b * BANK + width], w(k, o), x(k, start, width),
                                       start=(k == 0), stop=(k == k_chunks - 1))
            s = pe.did(ins)
            core.bank_free[b] = evacuate(o, start, width, core.psum[0:128, b * BANK:b * BANK + width], s)


def rows_product(nc, core, x, w, k_chunks, ready, evacuate, tile_ready=None):
    pe = core.pe
    for t in range(NT):
        pe.need(*ready)
        if tile_ready:
            pe.need(tile_ready[t])
        b = core.bank()
        acc = core.psum[0:P, b * BANK:b * BANK + D]
        for k in range(k_chunks):
            ins = nc.tensor.matmul(acc, x(k, t * P, P), w(k), start=(k == 0), stop=(k == k_chunks - 1))
        core.bank_free[b] = evacuate(t, acc, pe.did(ins))


def condition(nc, core, a, sb, x, xn_dram, cond):
    pe, dve, act, pool = core.pe, core.dve, core.act, core.pool
    psum = core.psum
    noise, emb, whole_turns = (sb(name, [2 * FREQ, N])[:] for name in ("noise", "emb", "whole_turns"))
    hidden, gate = (sb(name, [COND, N])[:] for name in ("cond_hidden", "cond_gate"))
    f_w1 = sb("f_w1", [2 * FREQ, COND])
    f_w2 = sb("f_w2", [COND, COND])
    f_b = sb("f_b", [COND, 2])
    freq = sb("freq", [2 * FREQ, 2])
    stat = sb("x_stat", [P, NT, 6])
    mv = sb("x_mv", [P, NT, 2])
    rstd = sb("x_rstd", [P, 2 * NT])
    f = pool.did(nc.gpsimd.iota(freq[0:FREQ, 0:1], [[0, 1]], base=1, channel_multiplier=1,
                                allow_small_or_imprecise_dtypes=True))
    f2 = pool.did(nc.gpsimd.iota(freq[FREQ:2 * FREQ, 0:1], [[0, 1]], base=1, channel_multiplier=1,
                                 allow_small_or_imprecise_dtypes=True))
    dve.did(nc.vector.memset(freq[0:FREQ, 1:2], 0.0))
    dve.did(nc.vector.memset(freq[FREQ:2 * FREQ, 1:2], 0.25))
    dve.did(nc.vector.memset(cond[:], 1.0))
    got_x = core.load(x[:], a["x"].rearrange("(t p) d -> p t d", p=P))
    got_n = core.load(noise, a["node_vec1"].rearrange("n a -> (n a)").partition_broadcast(2 * FREQ))
    got_f = [core.load(f_w1[:], a["L0_gnn_f_w1"]), core.load(f_w2[:], a["L0_gnn_f_w2"]),
             core.load(f_b[:, 0:1], a["L0_gnn_f_b1"].rearrange("(p a) -> p a", a=1)),
             core.load(f_b[:, 1:2], a["L0_gnn_f_b2"].rearrange("(p a) -> p a", a=1))]
    yield
    dve.need(f, f2)
    s = dve.did(nc.vector.tensor_scalar(freq[:, 0:1], freq[:, 0:1], 1.0 / 16.0, None, ALU.mult))
    dve.need(got_n, s)
    s = dve.did(nc.vector.tensor_scalar(emb, noise, freq[:, 0:1], freq[:, 1:2], ALU.mult, ALU.add))
    dve.need(s)
    s = dve.did(nc.vector.tensor_scalar(whole_turns, emb, ROUND, None, ALU.add))
    dve.need(s)
    s = dve.did(nc.vector.tensor_scalar(whole_turns, whole_turns, -ROUND, None, ALU.add))
    dve.need(s)
    s = dve.did(nc.vector.tensor_tensor(emb, emb, whole_turns, ALU.subtract))
    yield
    act.need(s)
    s = act.did(nc.scalar.activation(emb, emb, ACT.Sin, scale=6.2831850))
    yield
    pe.need(s, *got_f)
    act.need(*got_f)
    for start, width in SPANS:
        b = core.bank()
        ins = nc.tensor.matmul(psum[0:COND, b * BANK:b * BANK + width], f_w1[:, :], emb[:, start:start + width],
                               start=True, stop=True)
        s = pe.did(ins)
        act.need(s)
        act.did(nc.scalar.activation(hidden[:, start:start + width], psum[0:COND, b * BANK:b * BANK + width],
                                     ACT.Identity, bias=f_b[:, 0:1]))
        core.bank_free[b] = act.did(nc.scalar.activation(gate[:, start:start + width],
                                                         psum[0:COND, b * BANK:b * BANK + width], ACT.Sigmoid,
                                                         bias=f_b[:, 0:1]))
    s = (act.sem, act.count)
    yield
    dve.need(s)
    s = dve.did(nc.vector.tensor_tensor(hidden, hidden, gate, ALU.mult))
    yield
    pe.need(s)
    dve.need(*got_f)
    for start, width in SPANS:
        b = core.bank()
        ins = nc.tensor.matmul(psum[0:COND, b * BANK:b * BANK + width], f_w2[:, :],
                               hidden[:, start:start + width], start=True, stop=True)
        s = pe.did(ins)
        dve.need(s)
        core.bank_free[b] = dve.did(nc.vector.tensor_scalar(cond[0:COND, start:start + width],
                                        psum[0:COND, b * BANK:b * BANK + width],
                                        f_b[:, 1:2], None, ALU.add))
    yield
    done = layer_norm_rows(nc, core, x, x, stat, mv, rstd, after=(got_x,))
    core.load(rows_view(xn_dram), x[:], done[-1])


def edge_counts(nc, core, a, flag_dram, window_dram, ln_count, x, xn_dram, cond):
    pe, dve, act, pool = core.pe, core.dve, core.act, core.pool
    T, G, W = EDGE_TILES, EDGE_GROUPS, WINDOW
    whole = G - 1
    rest = E_EDGES - whole * 128 * T
    rest_p, rest_e = rest // T, rest % T
    psum = core.psum
    with ExitStack() as ctx:
        sb = lambda name, shape, dt=F32: ctx.enter_context(nc.sbuf_tensor(name, shape, dt))
        ends_i = sb("ends_i", [128, 2, G, T], I32)
        ends = sb("ends", [128, 2, G, T])
        low = sb("low", [128, G, T])
        iota = sb("iota", [128, N], F16)
        iota_f = sb("iota_f", [NT, G])
        edge_of = sb("block_starts", [G, 2, NT])
        cur = sb("cur", [128, 2, 2, W, T])
        cur_dst = sb("cur_dst", [128, 2, W, T], F16)
        block_iota = sb("block_iota", [128, 2, P], F16)
        hot_src = sb("hot_src", [128, HOT_RING, N], F16)
        hot_dst = sb("hot_dst", [128, 2, HOT_DST, P], F16)
        span = sb("span", [128, 2, G])
        span_g = sb("span_g", [G, 2])
        meets = sb("meets", [G, 2, NT])
        meets_b = sb("meets_b", [NT, G])
        outside = sb("outside", [NT, G])
        outside_i = sb("outside_i", [NT, G], I32)
        first = sb("first", [NT, 4])
        window_i = sb("window_i", [NT, 2], I32)
        flags = sb("flags", [1, NT * G], I32)
        windows = sb("windows", [1, NT * 2], I32)
        any_beyond = sb("any_beyond", [1, 1], I32)
        counts = sb("counts", [P, NT, N])
        none = sb("none", [P, 2, N])

        fill = dve.did(nc.vector.memset(ends_i[:], -1))
        pool.did(nc.gpsimd.iota(iota[:], [[1, N]], base=0, channel_multiplier=0,
                                allow_small_or_imprecise_dtypes=True))
        pool.did(nc.gpsimd.iota(iota_f[:], [[1, G]], base=0, channel_multiplier=0,
                                allow_small_or_imprecise_dtypes=True))
        pool.did(nc.gpsimd.iota(edge_of[:, 0, :], [[P, NT]], base=0, channel_multiplier=0,
                                allow_small_or_imprecise_dtypes=True))
        consts = pool.did(nc.gpsimd.iota(edge_of[:, 1, :], [[P, NT]], base=P - 1, channel_multiplier=0,
                                         allow_small_or_imprecise_dtypes=True))
        got = []
        for n, e in enumerate((a["src"], a["dst"])):
            got.append(core.load(ends_i[:, n, 0:whole, :],
                                 e[0:whole * 128 * T].rearrange("(g p t) -> p g t", p=128, t=T), fill))
            got.append(core.load(ends_i[0:rest_p, n, whole, :],
                                 e[whole * 128 * T:whole * 128 * T + rest_p * T].rearrange("(p t) -> p t", t=T)))
            if rest_e:
                got.append(core.load(ends_i[rest_p:rest_p + 1, n, whole, 0:rest_e],
                                     e[E_EDGES - rest_e:E_EDGES].rearrange("(p t) -> p t", t=rest_e)))
        dve.need(*got)
        e = dve.did(nc.vector.tensor_copy(ends[:], ends_i[:]))
        dve.need(e)
        s = dve.did(nc.vector.tensor_scalar(low[:], ends[:, 1], 0.0, 4096.0, ALU.is_lt, ALU.mult))
        dve.need(s)
        s = dve.did(nc.vector.tensor_tensor(low[:], low[:], ends[:, 1], ALU.add))
        dve.need(s)
        dve.did(nc.vector.tensor_reduce(span[:, 0, :], low[:], AX.X, ALU.min))
        s = dve.did(nc.vector.tensor_reduce(span[:, 1, :], ends[:, 1], AX.X, ALU.max))
        pe.need(s)
        for n in range(2):
            ins = nc.tensor.transpose(psum[0:G, n * 128:(n + 1) * 128], span[:, n, :], core.ident[:, :])
        s = pe.did(ins)
        dve.need(s)
        dve.did(nc.vector.tensor_reduce(span_g[:, 0:1], psum[0:G, 0:128], AX.X, ALU.min))
        s = dve.did(nc.vector.tensor_reduce(span_g[:, 1:2], psum[0:G, 128:256], AX.X, ALU.max))
        dve.need(s, consts)
        dve.did(nc.vector.tensor_scalar(meets[:, 0, :], edge_of[:, 1, :], span_g[:, 0:1], None, ALU.is_ge))
        s = dve.did(nc.vector.tensor_scalar(meets[:, 1, :], edge_of[:, 0, :], span_g[:, 1:2], None, ALU.is_le))
        dve.need(s)
        s = dve.did(nc.vector.tensor_tensor(meets[:, 0, :], meets[:, 0, :], meets[:, 1, :], ALU.mult))
        pe.need(s)
        s = pe.did(nc.tensor.transpose(psum[0:NT, BANK:BANK + G], meets[:, 0, :], core.ident[0:G, 0:G]))
        dve.need(s)
        s = dve.did(nc.vector.tensor_copy(meets_b[:], psum[0:NT, BANK:BANK + G]))
        dve.need(s)
        s = dve.did(nc.vector.tensor_scalar(outside[:], meets_b[:], -4096.0, 4096.0, ALU.mult, ALU.add))
        dve.need(s)
        s = dve.did(nc.vector.tensor_tensor(outside[:], outside[:], iota_f[:], ALU.add))
        dve.need(s)
        s = dve.did(nc.vector.tensor_reduce(first[:, 0:1], outside[:], AX.X, ALU.min))
        dve.need(s)
        s = dve.did(nc.vector.tensor_scalar(first[:, 0:1], first[:, 0:1], float(G - W), None, ALU.min))
        dve.need(s)
        s = dve.did(nc.vector.tensor_scalar(first[:, 2:3], first[:, 0:1], float(W), None, ALU.add))
        dve.need(s)
        s = dve.did(nc.vector.tensor_scalar(outside[:], iota_f[:], first[:, 2:3], None, ALU.is_ge))
        dve.need(s)
        s = dve.did(nc.vector.tensor_tensor(outside[:], outside[:], meets_b[:], ALU.mult))
        dve.need(s)
        s = dve.did(nc.vector.tensor_reduce(first[:, 1:2], outside[:], AX.X, ALU.max))
        dve.did(nc.vector.tensor_copy(outside_i[:], outside[:]))
        dve.need(s)
        s = dve.did(nc.vector.tensor_copy(window_i[:], first[:, 0:2]))
        s1 = core.load(flag_dram[:, :], outside_i[:], s)
        s2 = core.load(window_dram[:, :], window_i[:], s)
        row = lambda v: v[:, :].rearrange("j g -> (j g)").rearrange("(a f) -> a f", a=1)
        core.load(flags[:, :], row(flag_dram), s1)
        got = core.load(windows[:, :], row(window_dram), s2)
        dve.need(got)
        dve.did(nc.vector.tensor_reduce(any_beyond[:], windows[:, 1:2 * NT:2], AX.X, ALU.max))
        core.restart()

        def sum_tile(lhs, rhs, bank, first_tile, last_tile):
            for start in range(0, N, BANK):
                width = min(BANK, N - start)
                ins = nc.tensor.matmul(psum[0:P, bank * BANK + start:bank * BANK + start + width], lhs,
                                       rhs[:, start:start + width], start=first_tile, stop=last_tile)
            return ins

        last = {}
        LOTS = W * T // HOT_DST
        assert W * T % HOT_DST == 0 and W * T % HOT_RING == 0

        def two_blocks(it):
            for half in range(2):
                j = 2 * it + half
                start = nc.vector.value_load(windows[0:1, ds(2 * j, 1)], min_val=0, max_val=G - W)
                s = dve.did(nc.vector.tensor_copy(cur[:, half], ends[:, :, ds(start, W), :]))
                s2 = dve.did(nc.vector.tensor_copy(block_iota[:, half], iota[:, ds(j * P, P)]))
                dve.need(s, s2)
                s = dve.did(nc.vector.tensor_copy(cur_dst[:, half], cur[:, half, 1]))
                dve.need(s)
                dst = cur_dst[:, half].rearrange("p g t -> p (g t)")
                for n in range(W * T):
                    g, t = n // T, n % T
                    lot = (half * LOTS + n // HOT_DST) % 2
                    if n % HOT_DST == 0:
                        dve.need(*last.get(("lot", lot), []))
                        dve.did(nc.vector.tensor_tensor(
                            hot_dst[:, lot], dst[:, n:n + HOT_DST].unsqueeze(2).broadcast_to([128, HOT_DST, P]),
                            block_iota[:, half].unsqueeze(1).broadcast_to([128, HOT_DST, P]), ALU.is_equal))
                    dve.need(*last.get(("src", n % HOT_RING), []))
                    s = dve.did(nc.vector.tensor_scalar(hot_src[:, n % HOT_RING, :], iota[:, :],
                                                        cur[:, half, 0, g, t:t + 1], None, ALU.is_equal))
                    if n == 0:
                        pe.need(*last.get(("sums", half), []))
                    pe.need(s)
                    s = pe.did(sum_tile(hot_dst[:, lot, n % HOT_DST, :], hot_src[:, n % HOT_RING, :], 3 * half,
                                        n == 0, n == W * T - 1))
                    last["src", n % HOT_RING] = [s]
                    last["lot", lot] = [s]
                act.need(s)
                last["sums", half] = [act.did(nc.scalar.copy(
                    counts[:, ds(j, 1), :].rearrange("p j n -> p (j n)"), psum[0:P, 3 * half * BANK:3 * half * BANK + N]))]

        core.enter_loop()
        two_blocks(0)
        last = earlier(last, core.next_iterations(None))
        with nc.Fori(1, NT // 2) as it:
            core.loop.iteration = it
            two_blocks(it)
        core.leave_loop(NT // 2)
        core.restart()

        anything = nc.values_load(any_beyond[0:1, 0:1], min_val=0, max_val=1)
        with nc.If(anything == 1):
            with nc.Fori(0, NT) as j:
                dve.did(nc.vector.tensor_copy(block_iota[:, 0], iota[:, ds(j * P, P)]))
                core.restart()
                with nc.Fori(0, G) as g:
                    flag = nc.values_load(flags[0:1, ds(j * G + g, 1)], min_val=0, max_val=1)
                    with nc.If(flag == 1):
                        s = dve.did(nc.vector.tensor_copy(cur[:, 0, :, 0:1, :], ends[:, :, ds(g, 1), :]))
                        dve.need(s)
                        for t in range(T):
                            dve.did(nc.vector.tensor_scalar(hot_dst[:, 0, t, :], block_iota[:, 0],
                                                            cur[:, 0, 1, 0, t:t + 1], None, ALU.is_equal))
                            s = dve.did(nc.vector.tensor_scalar(hot_src[:, t, :], iota[:, :],
                                                                cur[:, 0, 0, 0, t:t + 1], None, ALU.is_equal))
                            pe.need(s)
                            s = pe.did(sum_tile(hot_dst[:, 0, t, :], hot_src[:, t, :], 0, t == 0, t == T - 1))
                        dve.need(s)
                        block = counts[:, ds(j, 1), :].rearrange("p j n -> p (j n)")
                        dve.did(nc.vector.tensor_tensor(block, block, psum[0:P, 0:N], ALU.add))
                        core.restart()

        none_free = [None, None]
        added = {}

        def turn_block(j):
            pe.need(added[j])
            for b0, n in ((0, 4), (4, 4), (8, 2)):
                b = core.bank()
                for i in range(n):
                    ins = nc.tensor.transpose(psum[0:P, b * BANK + i * P:b * BANK + (i + 1) * P],
                                              none[:, j % 2, (b0 + i) * P:(b0 + i + 1) * P], core.ident[0:P, 0:P])
                s = none_free[j % 2] = pe.did(ins)
                q = act if b0 == 4 else dve
                q.need(s)
                o = ln_count[:, b0:b0 + n, j * P:(j + 1) * P]
                v = psum[0:P, b * BANK:b * BANK + n * P].rearrange("p (i j) -> p i j", j=P)
                core.bank_free[b] = q.did(nc.scalar.copy(o, v) if b0 == 4 else nc.vector.tensor_copy(o, v))

        conditioning = condition(nc, core, a, sb, x, xn_dram, cond)
        for j in range(NT):
            next(conditioning, None)
            dve.need(none_free[j % 2])
            dve.did(nc.vector.tensor_scalar(none[:, j % 2, :], counts[:, j, :], 0.0, NOT_AN_EDGE, ALU.is_equal,
                                            ALU.mult))
            s = dve.did(nc.vector.tensor_scalar(counts[:, j, :], counts[:, j, :], 1.0, None, ALU.max))
            act.need(s)
            s = act.did(nc.scalar.activation(counts[:, j, :], counts[:, j, :], ACT.Ln))
            if j >= 1:
                turn_block(j - 1)
            dve.need(s)
            added[j] = dve.did(nc.vector.tensor_tensor(none[:, j % 2, :], counts[:, j, :], none[:, j % 2, :], ALU.add))
        turn_block(NT - 1)
        for _ in conditioning:
            pass
        core.restart()


def gnn(nc, core, a, x, cond, ln_count):
    pe, dve, act, pool = core.pe, core.dve, core.act, core.pool
    psum = core.psum
    H = GNN_HEADS
    Q_SCALE = float(128) ** -0.5
    with ExitStack() as ctx:
        sb = lambda name, shape, dt=F32: ctx.enter_context(nc.sbuf_tensor(name, shape, dt))
        y_cols = sb("g_y_cols", [128, KC, N])
        q_cols = sb("g_q_cols", [128, KC, N])
        k_cols = sb("g_k_cols", [128, KC, N])
        v_rows = sb("g_v_rows", [P, NT, D])
        w = [sb(f"g_w{i}", [128, KC, D]) for i in range(3)]
        cond_w = sb("g_cond_w", [COND_ROWS, 4, D])
        cond_parts = sb("g_cond_parts", [len(PART_PAIRS) * COND_ROWS, N], BF16)
        cond_w_parts = sb("g_cond_w_parts", [len(PART_PAIRS) * COND_ROWS, 4, D], BF16)
        prob = sb("g_prob", [P, 2, N])
        bias_rows = sb("g_bias_rows", [P, D])
        bias_cols = sb("g_bias_cols", [128, 3, KC])
        stat = sb("g_stat", [P, NT, 6])
        mv = sb("g_mv", [P, NT, 2])
        rstd = sb("g_rstd", [P, 2 * NT])
        row_max = sb("g_row_max", [P, 2, 4])
        turned_prob = y_cols[0:P, :, :].rearrange("p a b -> p (a b)").rearrange("p (u j i) -> p u j i", u=2, i=2 * P)

        dve.did(nc.vector.memset(cond_w[:, 1, :], 0.0))
        dve.did(nc.vector.memset(cond_w[:, 3, :], 0.0))
        dve.did(nc.vector.memset(cond_w[:, 0, :], 1.0))
        s_cond_w = dve.did(nc.vector.memset(cond_w[:, 2, :], 1.0))
        copied = []

        def split(src, rest, parts, stacked, which, *after):
            dve.need(*after)
            for n in range(3):
                s = dve.did(nc.vector.tensor_copy(parts[n], src if n == 0 else rest))
                for row, pair in enumerate(PART_PAIRS):
                    if pair[which] == n:
                        copied.append(core.load(stacked[row * COND_ROWS:(row + 1) * COND_ROWS], parts[n], s))
                dve.need(s)
                if n < 2:
                    s = dve.did(nc.vector.tensor_tensor(rest, src if n == 0 else rest, parts[n], ALU.subtract))
                    dve.need(s)

        def weight_rows(name, layer):
            return a[name][ds(layer, 1), :, :].rearrange("l (c p) o -> p (l c) o", p=128)

        def bias_row(name, layer, n=P):
            return a[name][ds(layer, 1), :].rearrange("l o -> (l o)").partition_broadcast(n)

        def load_cond_w(layer, *after):
            got = []
            for n, (wn, bn) in enumerate((("s1_w", "s1_b"), ("b1_w", "b1_b"), ("s2_w", "s2_b"), ("b2_w", "b2_b"))):
                got.append(core.load(cond_w[0:COND, n, :], a["L0_gnn_" + wn][ds(layer, 1), :, :].rearrange(
                    "l c d -> (l c) d"), *after))
                got.append(core.load(cond_w[COND:COND + 1, n, :], a["L0_gnn_" + bn][ds(layer, 1), :]))
            return got

        def split_cond_w(*after):
            flat = v_rows[0:COND_ROWS, :, :].rearrange("p t d -> p (t d)")
            rest = flat[:, 0:4 * D]
            parts = flat[:, 4 * D:10 * D].bitcast(BF16)
            split(cond_w[:].rearrange("p n d -> p (n d)"), rest, [parts[:, n * 4 * D:(n + 1) * 4 * D] for n in range(3)],
                  cond_w_parts[:].rearrange("p n d -> p (n d)"), 1, *after)

        def load_bias_cols(layer, *after):
            return [core.load(bias_cols[:, n, :], a["L0_gnn_" + name][ds(layer, 1), :].rearrange(
                "l (c p) -> p (l c)", p=128), *after) for n, name in enumerate(("bq", "bk", "m_b1"))]

        class Norm:

            def __init__(self, which, got):
                self.which, self.got = which, got
                self.pair, self.ready, self.normed = {}, {}, {}

            def tile(self, t, x_done):
                if t < NT:
                    self.start(t, x_done)
                if 1 <= t <= NT:
                    self.scale(t - 1)
                if t >= 2:
                    self.turn(t - 2)

            def start(self, t, x_done):
                pe.need(*self.got)
                self.pair[t] = []
                for n in range(2):
                    b = core.bank()
                    ins = nc.tensor.matmul(psum[0:P, b * BANK:b * BANK + D], cond_parts[:, t * P:(t + 1) * P],
                                           cond_w_parts[:, 2 * self.which + n, :], start=True, stop=True)
                    self.pair[t].append((b, pe.did(ins)))
                dve.need(x_done)
                s = dve.did(nc.vector.bn_stats(stat[:, t, :], x[:, t, :]))
                dve.need(s)
                s = dve.did(nc.vector.bn_aggr(mv[:, t, :], stat[:, t, :]))
                dve.need(s)
                s = dve.did(nc.vector.tensor_scalar(rstd[:, t:t + 1], mv[:, t, 1:2], EPS, None, ALU.add))
                act.need(s)
                self.ready[t] = act.did(nc.scalar.activation(rstd[:, NT + t:NT + t + 1], rstd[:, t:t + 1], ACT.Sqrt))

            def scale(self, t):
                (b0, s0), (b1, s1) = self.pair[t]
                dve.need(self.ready[t], s0)
                r = dve.did(nc.vector.reciprocal(rstd[:, t:t + 1], rstd[:, NT + t:NT + t + 1]))
                core.bank_free[b0] = s = dve.did(nc.vector.scalar_tensor_tensor(
                    v_rows[:, t, :], x[:, t, :], mv[:, t, 0:1], psum[0:P, b0 * BANK:b0 * BANK + D],
                    ALU.subtract, ALU.mult))
                dve.need(r, s, s1)
                core.bank_free[b1] = self.normed[t] = dve.did(nc.vector.scalar_tensor_tensor(
                    v_rows[:, t, :], v_rows[:, t, :], rstd[:, t:t + 1], psum[0:P, b1 * BANK:b1 * BANK + D],
                    ALU.mult, ALU.add))

            def turn(self, t):
                b, s = turn_tile(nc, core, v_rows[:, t, :], KC, self.normed[t])
                act.need(s)
                core.bank_free[b] = act.did(nc.scalar.copy(y_cols[:, :, t * P:(t + 1) * P], turned(core, b)))

            def finish(self):
                self.tile(NT, None)
                self.tile(NT + 1, None)
                return (act.sem, act.count)

        flat = q_cols[0:COND_ROWS, 0, :]
        parts = q_cols[0:COND_ROWS, 1:3, :].rearrange("p a n -> p (a n)").bitcast(BF16)
        got_cond_w = load_cond_w(0, s_cond_w)
        core.load(w[0][:], weight_rows("L0_gnn_wq", 0))
        core.load(w[1][:], weight_rows("L0_gnn_wk", 0))
        load_bias_cols(0)
        split(cond[:, :], flat, [parts[:, n * N:(n + 1) * N] for n in range(3)], cond_parts[:], 0)
        split_cond_w(*got_cond_w)
        norm = Norm(0, copied)
        for t in range(NT):
            dve.need(*copied)
            norm.tile(t, None)
        norm.finish()
        core.restart()

        def one_layer(layer, last):
            nonlocal copied
            got_wv = core.load(w[2][:], weight_rows("L0_gnn_wv", layer))
            got_bv = core.load(bias_rows[:, :], bias_row("L0_gnn_bv", layer))

            s = act.did(nc.scalar.mul(bias_cols[:, 0, :], bias_cols[:, 0, :], Q_SCALE))
            act.need(s)

            def to_q(o, start, width, acc, s):
                act.need(s)
                return act.did(nc.scalar.activation(q_cols[:, o, start:start + width], acc, ACT.Identity,
                                                    bias=bias_cols[:, 0, o:o + 1], scale=Q_SCALE))

            def to_k(o, start, width, acc, s):
                dve.need(s)
                return dve.did(nc.vector.tensor_scalar(k_cols[:, o, start:start + width], acc,
                                                       bias_cols[:, 1, o:o + 1], None, ALU.add))

            def to_v(t, acc, s):
                dve.need(s)
                return dve.did(nc.vector.tensor_tensor(v_rows[:, t, :], acc, bias_rows[:, :], ALU.add))

            ys = lambda k, start, width: y_cols[:, k, start:start + width]
            cols_product(nc, core, lambda k, o: w[0][:, k, o * 128:(o + 1) * 128], ys, KC, KC,
                         (), to_q)
            q_done, pe_q = (act.sem, act.count), (pe.sem, pe.count)
            got_wo = core.load(w[0][:], weight_rows("L0_gnn_wo", layer), pe_q)
            cols_product(nc, core, lambda k, o: w[1][:, k, o * 128:(o + 1) * 128], ys, KC, KC,
                         (), to_k)
            k_done, pe_k = (dve.sem, dve.count), (pe.sem, pe.count)
            got_m1 = core.load(w[1][:], weight_rows("L0_gnn_m_w1", layer), pe_k)
            dve.need(got_bv)
            rows_product(nc, core, ys, lambda k: w[2][:, k, :], KC, (got_wv,), to_v)
            v_done, pe_v = (dve.sem, dve.count), (pe.sem, pe.count)
            got_m2 = core.load(w[2][:], weight_rows("L0_gnn_m_w2", layer), pe_v)
            got_bo = core.load(bias_rows[:, :], bias_row("L0_gnn_bo", layer), v_done)
            pool.need(got_bo, v_done)
            for t in range(NT):
                x_bo = pool.did(nc.gpsimd.tensor_tensor(x[:, t, :], x[:, t, :], bias_rows[:, :], ALU.add))
            got_b2 = core.load(bias_rows[:, :], bias_row("L0_gnn_m_b2", layer), x_bo)

            steps = [(h, t) for h in range(H) for t in range(NT)]
            soft = {}
            turn_free = [core.bank_free[3:6]]
            out_free = [core.bank_free[6], core.bank_free[7]]
            prob_free = [None, None]
            pair_done, out_done = {}, {}
            pe.need(*core.bank_free)
            s_free = None

            def scores(n):
                nonlocal s_free
                h, t = steps[n]
                u = n % 2
                pe.need(q_done, k_done, s_free)
                for start in range(0, N, BANK):
                    width = min(BANK, N - start)
                    ins = nc.tensor.matmul(psum[0:P, start:start + width], q_cols[:, h, t * P:(t + 1) * P],
                                           k_cols[:, h, start:start + width], start=True, stop=True)
                s = pe.did(ins)
                dve.need(s, prob_free[u])
                s = s_free = dve.did(nc.vector.tensor_tensor_reduce(
                    prob[:, u, :], psum[0:P, 0:N], ln_count[:, t, :], 1.0, NOT_AN_EDGE / 10, ALU.add, ALU.max,
                    row_max[:, u, 0:1]))
                dve.need(s)
                s = dve.did(nc.vector.tensor_scalar(row_max[:, u, 1:2], row_max[:, u, 0:1], -1.0, None, ALU.mult))
                act.need(s)
                s = act.did(nc.scalar.activation(prob[:, u, :], prob[:, u, :], ACT.Exp, bias=row_max[:, u, 1:2],
                                                 accum_out=row_max[:, u, 2:3]))
                return s

            def normalise(n, s):
                u = n % 2
                dve.need(s)
                s = dve.did(nc.vector.tensor_scalar(row_max[:, u, 2:3], row_max[:, u, 2:3], 1e-30, None, ALU.max))
                dve.need(s)
                s = dve.did(nc.vector.reciprocal(row_max[:, u, 3:4], row_max[:, u, 2:3]))
                dve.need(s)
                return dve.did(nc.vector.tensor_scalar(prob[:, u, :], prob[:, u, :], row_max[:, u, 3:4], None,
                                                       ALU.mult))

            def turn_probs(n, ready):
                u, g = n % 2, n // 2
                half = (n % 2) * P
                pe.need(ready, *turn_free[0])
                frees = []
                for b, j0, nj in ((3, 0, 4), (4, 4, 4), (5, 8, 2)):
                    for j in range(nj):
                        ins = nc.tensor.transpose(psum[0:P, b * BANK + j * P:b * BANK + (j + 1) * P],
                                                  prob[:, u, (j0 + j) * P:(j0 + j + 1) * P],
                                                  core.ident[0:P, 0:P])
                    s = pe.did(ins)
                    q = dve if b == 4 else act
                    q.need(s, out_done.get(g - 2))
                    dst = turned_prob[:, g % 2, j0:j0 + nj, half:half + P]
                    src_ = psum[0:P, b * BANK:b * BANK + nj * P].rearrange("p (j i) -> p j i", i=P)
                    ins = nc.vector.tensor_copy(dst, src_) if b == 4 else nc.scalar.copy(dst, src_)
                    frees.append(q.did(ins))
                prob_free[u] = s
                turn_free[0] = frees
                pair_done[g] = (pair_done.get(g) or []) + frees

            def weigh(g, part):
                h, t = steps[2 * g]
                b = 6 + g % 2
                pe.need(v_done, *pair_done[g])
                if part == 0:
                    pe.need(out_free[g % 2])
                for j in range(5 * part, 5 * part + 5):
                    ins = nc.tensor.matmul(psum[0:128, b * BANK:b * BANK + 2 * P],
                                           v_rows[:, j, h * 128:(h + 1) * 128], turned_prob[:, g % 2, j, :],
                                           start=(j == 0), stop=(j == NT - 1))
                s = pe.did(ins)
                if part == 1:
                    out_done[g] = s
                    act.need(s)
                    out_free[g % 2] = act.did(nc.scalar.copy(q_cols[:, h, t * P:(t + 2) * P],
                                                             psum[0:128, b * BANK:b * BANK + 2 * P]))

            act.need(pe_v)
            dve.need(pe_v)
            pending = {}
            n_steps = len(steps)
            for n in range(n_steps + 1):
                ready = normalise(n - 1, pending[n - 1]) if n >= 1 else None
                if n < n_steps:
                    pending[n] = scores(n)
                g = (n - 3) // 2
                if g >= 0:
                    if (n - 3) % 2 == 0:
                        weigh(g, 0)
                    else:
                        weigh(g, 1)
                if n >= 1:
                    turn_probs(n - 1, ready)
            if out_done.get(n_steps // 2 - 2) is None:
                weigh(n_steps // 2 - 2, 1)
            weigh(n_steps // 2 - 1, 0)
            weigh(n_steps // 2 - 1, 1)
            o_done = (act.sem, act.count)
            core.bank_free = [s_free] * 3 + turn_free[0] + out_free
            core.next_bank = 0

            norm = Norm(1, ())

            def add_to_x(t, acc, s):
                dve.need(s, x_bo)
                s = dve.did(nc.vector.tensor_tensor(x[:, t, :], x[:, t, :], acc, ALU.add))
                norm.tile(t, s)
                return s

            rows_product(nc, core, lambda k, s0, n: q_cols[:, k, s0:s0 + n], lambda k: w[0][:, k, :], KC,
                         (o_done, got_wo), add_to_x)
            pe_o = (pe.sem, pe.count)
            y_ready = norm.finish()
            normed, pe_norm = (dve.sem, dve.count), (pe.sem, pe.count)
            pool.need(got_b2, normed)
            for t in range(NT):
                x_b2 = pool.did(nc.gpsimd.tensor_tensor(x[:, t, :], x[:, t, :], bias_rows[:, :], ALU.add))
            if not last:
                core.load(w[0][:], weight_rows("L0_gnn_wq", layer + 1), pe_o)
                copied = []
                core.sp.need(pe_norm)
                split_cond_w(pe_norm, *load_cond_w(layer + 1))

            def to_hidden(o, start, width, acc, s):
                act.need(s)
                return act.did(nc.scalar.activation(k_cols[:, o, start:start + width], acc, ACT.Relu,
                                                    bias=bias_cols[:, 2, o:o + 1]))

            cols_product(nc, core, lambda k, o: w[1][:, k, o * 128:(o + 1) * 128], ys, KC, KC,
                         (y_ready, got_m1), to_hidden)
            h_done = (act.sem, act.count)
            if not last:
                core.load(w[1][:], weight_rows("L0_gnn_wk", layer + 1), (pe.sem, pe.count))
                load_bias_cols(layer + 1, h_done)
                norm = Norm(0, copied)
                dve.need(*copied)

            def add_mlp(t, acc, s):
                dve.need(s, x_b2)
                s = dve.did(nc.vector.tensor_tensor(x[:, t, :], x[:, t, :], acc, ALU.add))
                if not last:
                    norm.tile(t, s)
                return s

            rows_product(nc, core, lambda k, s0, n: k_cols[:, k, s0:s0 + n], lambda k: w[2][:, k, :], KC,
                         (h_done, got_m2), add_mlp)
            if not last:
                norm.finish()
            core.restart()

        with nc.Fori(0, GNN_LAYERS - 1) as layer:
            one_layer(layer, False)
        one_layer(GNN_LAYERS - 1, True)


def performer(nc, core, a, gnn_x, xn_dram):
    pe, dve, act, pool = core.pe, core.dve, core.act, core.pool
    psum = core.psum
    H, DH, F = MIX_HEADS, MIX_DH, MIX_F
    K_SUM_SMALL = 1e-6 * 16.0
    with ExitStack() as ctx:
        sb = lambda name, shape, dt=F32: ctx.enter_context(nc.sbuf_tensor(name, shape, dt))
        x = sb("p_x", [P, NT, D])
        h_rows = sb("p_h_rows", [P, NT, D])
        cols = sb("p_cols", [128, KC, N])
        v_rows = sb("p_v_rows", [P, NT, H, DH + 1])
        q_cols = sb("p_q_cols", [128, KC, N])
        k_cols = sb("p_k_cols", [128, KC, N])
        w = [sb(f"p_w{i}", [128, KC, D]) for i in range(4)]
        pmat = sb("p_pmat", [128, F])
        kf = sb("p_kf", [P, 4, F])
        qf_cols = sb("p_qf_cols", [128, 2, 2, P])
        kv = sb("p_kv", [128, H, 2, DH + 1])
        bias_rows = sb("p_bias_rows", [P, 3, D])
        gb = sb("p_gb", [128, 4, KC])
        bqk = sb("p_bqk", [128, 2, KC])
        b1 = sb("p_b1", [128, MIX_H // 128])
        stat = sb("p_stat", [P, NT, 6])
        mv = sb("p_mv", [P, NT, 2])
        rstd = sb("p_rstd", [P, 2 * NT])
        mx = sb("p_mx", [P, 8])
        rden = sb("p_rden", [P, 4])

        got_x = [core.load(x[:, t, :], xn_dram[t * P:(t + 1) * P, :]) for t in range(NT)]
        wqkv = a["L0_mix_Wqkv"].rearrange("(c p) o -> p c o", p=128)
        cvec = lambda v: v.rearrange("(c p) -> p c", p=128)
        got_gb = [core.load(gb[:, n, :], cvec(a["L0_mix_" + s])) for n, s in enumerate(("g1", "be1", "g2", "be2"))]
        got_w = {n: core.load(w[n][:], wqkv[:, :, n * D:(n + 1) * D]) for n in (2, 1, 0)}
        got_p = [core.load(pmat[0:64, :], a["L0_mix_Pmat"]), core.load(pmat[64:128, :], a["L0_mix_Pmat"])]
        got_bqk = [core.load(bqk[:, n, :], cvec(a["L0_mix_bqkv"][n * D:(n + 1) * D])) for n in range(2)]
        got_b1 = core.load(b1[:, :], cvec(a["L0_mix_b1"]))
        got_br = [core.load(bias_rows[:, 0, :], a["L0_mix_bqkv"][2 * D:3 * D].partition_broadcast(P)),
                  core.load(bias_rows[:, 1, :], a["L0_mix_bproj"].partition_broadcast(P)),
                  core.load(bias_rows[:, 2, :], a["L0_mix_b2"].partition_broadcast(P))]
        got_wp = core.load(w[3][:], a["L0_mix_Wproj"].rearrange("(c p) o -> p c o", p=128))
        act.need(*got_gb)

        def norm_to_cols(which):
            cols_ready = {}

            def turn(t, ready):
                b, s = turn_tile(nc, core, h_rows[:, t, :], KC, ready)
                act.need(s)
                for c in range(KC):
                    ins = nc.scalar.activation(cols[:, c, t * P:(t + 1) * P],
                                               psum[0:128, b * BANK + c * P:b * BANK + (c + 1) * P], ACT.Identity,
                                               bias=gb[:, 2 * which + 1, c:c + 1], scale=gb[:, 2 * which, c:c + 1])
                    core.bank_free[b] = cols_ready[t] = act.did(ins)

            return TileNorm(nc, core, x, h_rows, stat, mv, rstd, turn), cols_ready

        norm, cols_ready = norm_to_cols(0)
        for t in range(NT):
            norm.tile(t, got_x[t])
        norm.finish()
        cs = lambda k, start, width: cols[:, k, start:start + width]

        def to_q(o, start, width, acc, s):
            act.need(s)
            return act.did(nc.scalar.activation(q_cols[:, o, start:start + width], acc, ACT.Identity,
                                                bias=bqk[:, 0, o:o + 1]))

        def to_k(o, start, width, acc, s):
            dve.need(s)
            return dve.did(nc.vector.tensor_scalar(k_cols[:, o, start:start + width], acc, bqk[:, 1, o:o + 1],
                                                   None, ALU.add))

        def to_v(t, acc, s):
            dve.need(s)
            return dve.did(nc.vector.tensor_tensor(v_rows[:, t, :, 0:DH], acc.rearrange("p (h d) -> p h d", d=DH),
                                                   bias_rows[:, 0, :].rearrange("p (h d) -> p h d", d=DH), ALU.add))

        dve.need(*got_br)
        dve.did(nc.vector.memset(v_rows[:, :, :, DH:DH + 1], 1.0))
        rows_product(nc, core, cs, lambda k: w[2][:, k, :], KC, (got_w[2],), to_v, cols_ready)
        act.need(*got_bqk)
        dve.need(*got_bqk)
        for n, evac in ((1, to_k), (0, to_q)):
            cols_product(nc, core, lambda k, o: w[n][:, k, o * 128:(o + 1) * 128], cs, KC, KC,
                         (cols_ready[NT - 1], got_w[n]), evac)
        qkv_done = [(act.sem, act.count), (dve.sem, dve.count)]
        w1_view = a["L0_mix_W1"].rearrange("(c p) o -> p c o", p=128)
        w2_view = a["L0_mix_W2"].rearrange("(c p) o -> p c o", p=128)
        pe_qkv = (pe.sem, pe.count)
        got_w1 = [core.load(w[0][:], w1_view[:, :, 0:D], pe_qkv), core.load(w[1][:], w1_view[:, :, D:2 * D], pe_qkv)]

        kf_free = [None] * 4

        def feature_map(src, h, t, slot):
            r0 = (h % 2) * DH
            b = core.bank()
            pe.need(*qkv_done, *got_p)
            s = pe.did(nc.tensor.matmul(psum[0:P, b * BANK:b * BANK + F],
                                        src[r0:r0 + DH, h // 2, t * P:(t + 1) * P], pmat[r0:r0 + DH, :],
                                        start=True, stop=True))
            dve.need(s, kf_free[slot])
            s = dve.did(nc.vector.tensor_reduce(mx[:, slot:slot + 1], psum[0:P, b * BANK:b * BANK + F], AX.X,
                                                ALU.max, negate=True))
            act.need(s, kf_free[slot])
            core.bank_free[b] = act.did(nc.scalar.activation(kf[:, slot, :], psum[0:P, b * BANK:b * BANK + F],
                                                             ACT.Exp, bias=mx[:, slot:slot + 1]))
            return core.bank_free[b]

        LAG = 2
        work = [(h, t) for h in range(H) for t in range(NT)]
        got_f = {}
        held = {}
        core.next_bank = 0
        free_acc = {6: core.bank_free[6], 7: core.bank_free[7]}
        for n in range(len(work) + LAG):
            if n < len(work):
                if core.next_bank >= 6:
                    core.next_bank = 0
                got_f[n] = feature_map(k_cols, *work[n], n % 4)
            if n >= LAG:
                m = n - LAG
                h, t = work[m]
                pe.need(got_f[m])
                for half in range(2):
                    if t == 0:
                        pe.need(free_acc[6 + half])
                    ins = nc.tensor.matmul(psum[0:128, (6 + half) * BANK:(6 + half) * BANK + DH + 1],
                                           kf[:, m % 4, half * 128:(half + 1) * 128], v_rows[:, t, h, :],
                                           start=(t == 0), stop=(t == NT - 1))
                s = pe.did(ins)
                kf_free[m % 4] = s
                if t == NT - 1:
                    for half in range(2):
                        dve.need(s)
                        free_acc[6 + half] = dve.did(nc.vector.tensor_copy(
                            kv[:, h, half, :], psum[0:128, (6 + half) * BANK:(6 + half) * BANK + DH + 1]))
        kv_done = free_acc[7]
        dve.need(kv_done)
        kv_done = dve.did(nc.vector.tensor_scalar(kv[:, :, :, DH:DH + 1], kv[:, :, :, DH:DH + 1], K_SUM_SMALL,
                                                  None, ALU.add))
        core.bank_free[6], core.bank_free[7] = free_acc[6], free_acc[7]

        work = [(h, t) for t in range(NT) for h in range(H)]
        qf_free = [None, None]
        qf_ready = {}
        tile_done = {}
        cols_ready = {}

        def turn_output(t):
            b, s = turn_tile(nc, core, h_rows[:, t, :], KC, tile_done[t])
            act.need(s)
            core.bank_free[b] = cols_ready[t] = act.did(nc.scalar.copy(cols[:, :, t * P:(t + 1) * P],
                                                                       turned(core, b)))

        for n in range(len(work) + 2 * LAG):
            if n < len(work):
                h, t = work[n]
                got_f[n] = feature_map(q_cols, h, t, n % 4)
            if LAG <= n < len(work) + LAG:
                m = n - LAG
                b, s = turn_tile(nc, core, kf[:, m % 4, :], 2, got_f[m])
                kf_free[m % 4] = s
                q = act
                q.need(s, qf_free[m % 2])
                core.bank_free[b] = q.did(nc.scalar.copy(qf_cols[:, m % 2, :, :], turned(core, b, n=2)))
                qf_ready[m] = core.bank_free[b]
            if n >= LAG + 1 and n - LAG - 1 < len(work):
                m = n - LAG - 1
                h, t = work[m]
                b = core.bank()
                pe.need(qf_ready[m], kv_done)
                for half in range(2):
                    ins = nc.tensor.matmul(psum[0:P, b * BANK:b * BANK + DH + 1], qf_cols[:, m % 2, half, :],
                                           kv[:, h, half, :], start=(half == 0), stop=(half == 1))
                s = pe.did(ins)
                qf_free[m % 2] = s
                dve.need(s)
                s = dve.did(nc.vector.reciprocal(rden[:, m % 4:m % 4 + 1],
                                                 psum[0:P, b * BANK + DH:b * BANK + DH + 1]))
                dve.need(s)
                core.bank_free[b] = dve.did(nc.vector.tensor_scalar(
                    h_rows[:, t, h * DH:(h + 1) * DH], psum[0:P, b * BANK:b * BANK + DH], rden[:, m % 4:m % 4 + 1],
                    None, ALU.mult))
                tile_done[t] = core.bank_free[b]
                if t >= 1 and h == 1:
                    turn_output(t - 1)
        turn_output(NT - 1)

        pool.need(*got_br, *qkv_done)
        for t in range(NT):
            x_b = pool.did(nc.gpsimd.tensor_tensor(x[:, t, :], x[:, t, :], bias_rows[:, 1, :], ALU.add))
        def add_to_x(t, acc, s):
            dve.need(s, x_b)
            return dve.did(nc.vector.tensor_tensor(x[:, t, :], x[:, t, :], acc, ALU.add))

        norm, cols_ready2 = norm_to_cols(1)
        heads_turned = (pe.sem, pe.count)

        def project(t, acc, s):
            dve.need(heads_turned)
            s = add_to_x(t, acc, s)
            norm.tile(t, s)
            return s

        rows_product(nc, core, cs, lambda k: w[3][:, k, :], KC, (got_wp,), project, cols_ready)
        proj_done = (pe.sem, pe.count)
        got_w2 = [core.load(w[2][:], w2_view[:, 0:KC, :], proj_done), core.load(w[3][:], w2_view[:, KC:2 * KC, :], proj_done)]
        norm.finish()
        ready = cols_ready2[NT - 1]
        pool.need(ready, (dve.sem, dve.count))
        for t in range(NT):
            x_b = pool.did(nc.gpsimd.tensor_tensor(x[:, t, :], x[:, t, :], bias_rows[:, 2, :], ALU.add))

        act.need(got_b1)

        def to_hidden(o, start, width, acc, s):
            act.need(s)
            dst = q_cols if o < KC else k_cols
            return act.did(nc.scalar.activation(dst[:, o % KC, start:start + width], acc, ACT.Gelu,
                                                bias=b1[:, o:o + 1]))

        cols_product(nc, core, lambda k, o: w[o // KC][:, k, (o % KC) * 128:(o % KC + 1) * 128], cs, 2 * KC, KC,
                     (ready, *got_w1), to_hidden)
        h_done = (act.sem, act.count)
        cols_read = (pe.sem, pe.count)
        h2 = v_rows[:, :, :, :].rearrange("p t h d -> p (t h d)")[:, 0:NT * D].rearrange("p (t d) -> p t d", d=D)
        got_i = core.load(h2, a["x"].rearrange("(t p) d -> p t d", p=P), cols_read)
        pool.need(got_i)
        for t in range(NT):
            other = pool.did(nc.gpsimd.tensor_tensor(gnn_x[:, t, :], gnn_x[:, t, :], h2[:, t, :], ALU.add))
        pool.need(other, x_b)
        for t in range(NT):
            x_b = pool.did(nc.gpsimd.tensor_tensor(x[:, t, :], x[:, t, :], gnn_x[:, t, :], ALU.add))

        def add_all(t, acc, s):
            dve.need(s, x_b)
            return dve.did(nc.vector.tensor_tensor(gnn_x[:, t, :], x[:, t, :], acc, ALU.add))

        rows_product(nc, core, lambda k, s0, n: (q_cols if k < KC else k_cols)[:, k % KC, s0:s0 + n],
                     lambda k: w[2 + k // KC][:, k % KC, :], 2 * KC, (h_done, *got_w2), add_all)
        core.restart()


def moe(nc, core, a, x, out):
    pe, dve, act, pool = core.pe, core.dve, core.act, core.pool
    psum = core.psum
    S = SLOT_TILES_PADDED
    xf_dram = nc.dram_tensor("normed_rows", [N, D], F32)
    slot_dram = nc.dram_tensor("slot_nodes", [S * 128, 1], I32)
    expert_dram = nc.dram_tensor("slot_experts", [S, 1], I32)
    param_dram = nc.dram_tensor("swiglu_params", [EXPERTS + 1, 8], F32)
    y_dram = nc.dram_tensor("slot_outputs", [SLOT_UNROLL * SLOT_ROUNDS * 128, D], F32)
    with ExitStack() as ctx:
        sb = lambda name, shape, dt=F32: ctx.enter_context(nc.sbuf_tensor(name, shape, dt))
        weight = sb("m_weight", [P, NT, 2])
        pos = sb("m_pos", [P, 2 * NT], U32)
        slot_node = sb("m_slot_node", [128, S], U32)
        slot_cols = sb("m_slot_cols", [128, KC, SLOT_COLS_TILES * 128])
        slot_expert = sb("m_slot_expert", [1, S], I32)
        with ExitStack() as first:
            sb1 = lambda name, shape, dt=F32: first.enter_context(nc.sbuf_tensor(name, shape, dt))
            rows_ring = sb1("m_rows_ring", [128, NT, D])
            n_rows = rows_ring[0:P]
            cols = sb1("m_cols", [128, KC, N])
            w1 = sb1("m_w1", [128, KC, 2 * FFN_I])
            w2 = sb1("m_w2", [128, IC, D])
            hidden = sb1("m_hidden", [128, IC, N])
            scratch = [slot_cols[:, i, 0:1500].rearrange("p (n c) -> p n c", n=3) for i in range(2)]
            gate_w = sb1("m_gate_w", [128, KC, EXPERTS])
            gate_b = sb1("m_gate_b", [P, EXPERTS])
            cw = sb1("m_cw", [P, NT, EXPERTS])
            cw_cols = sb1("m_cw_cols", [EXPERTS, N])
            b2 = sb1("m_b2", [EXPERTS, D])
            shared_b2 = sb1("m_shared_b2", [P, D])
            b1 = sb1("m_b1", [128, 2, IC])
            shared_prm = sb1("m_shared_prm", [128, 8])
            stat = sb1("m_stat", [P, NT, 6])
            mv = sb1("m_mv", [P, NT, 2])
            rstd = sb1("m_rstd", [P, 2 * NT])
            logit = sb1("m_logit", [P, NT, EXPERTS])
            top = sb1("m_top", [P, NT, 8])
            top_i = sb1("m_top_i", [P, NT, 8], U32)
            top_f = sb1("m_top_f", [P, NT, 2])
            small = sb1("m_small", [P, NT, 4])
            lane = sb1("m_lane", [P, EXPERTS])
            node_id = sb1("m_node_id", [P, NT], I32)
            zero_slots = sb1("m_zero_slots", [S, 128], I32)
            slot_rows_i = sb1("m_slot_rows_i", [S, 128], I32)
            slot_rows = sb1("m_slot_rows", [S, 128])
            pick = sb1("m_pick", [P, 2, NT, EXPERTS])
            member = sb1("m_member", [P, NT, EXPERTS])
            before = sb1("m_before", [P, P])
            ones = sb1("m_ones", [P, P])
            start_of = sb1("m_start_of", [P, NT + 1, EXPERTS])
            place = sb1("m_place", [P, NT, EXPERTS])
            total = sb1("m_total", [P, EXPERTS])
            tiles_of = sb1("m_tiles_of", [P, 3, EXPERTS])
            pos_f = sb1("m_pos_f", [P, 2, NT])
            slot_id = sb1("m_slot_id", [S, 1])
            passed = sb1("m_passed", [S, EXPERTS])
            expert_f = sb1("m_expert_f", [S, 1])
            expert_i = sb1("m_expert_i", [S, 1], I32)
            prm = sb1("m_prm", [EXPERTS + 1, 8])
            raw = sb1("m_raw", [EXPERTS + 1, 2])

            got_a = [core.load(prm[0:EXPERTS, 0:5], a["L0_ffn_expert_act"]),
                     core.load(prm[EXPERTS:EXPERTS + 1, 0:5], a["L0_ffn_shared_act"].rearrange("(a n) -> a n", a=1))]
            got = [core.load(gate_w[:], a["L0_ffn_gate_w"].rearrange("(c p) e -> p c e", p=128)),
                   core.load(gate_b[:], a["L0_ffn_gate_b"].partition_broadcast(P)),
                   core.load(b2[:], a["L0_ffn_expert_b2"]),
                   core.load(shared_b2[:], a["L0_ffn_shared_b2"].partition_broadcast(P))]
            got_w1 = core.load(w1[:], a["L0_ffn_shared_w1"].rearrange("(c p) o -> p c o", p=128))
            got_w2 = core.load(w2[:], a["L0_ffn_shared_w2"].rearrange("(c p) o -> p c o", p=128))
            got_b1 = [core.load(b1[:, n, :], a["L0_ffn_shared_b1"].rearrange("(c p n) -> p n c", p=128, n=2)[:, n, :])
                      for n in range(2)]
            pool.did(nc.gpsimd.iota(lane[:], [[1, EXPERTS]], base=0, channel_multiplier=0,
                                    allow_small_or_imprecise_dtypes=True))
            pool.did(nc.gpsimd.iota(slot_id[:], [[0, 1]], base=0, channel_multiplier=1,
                                    allow_small_or_imprecise_dtypes=True))
            s = pool.did(nc.gpsimd.iota(node_id[:], [[P, NT]], base=0, channel_multiplier=1))
            pool.did(nc.gpsimd.memset(ones[:], 1.0))
            pool.did(nc.gpsimd.memset(zero_slots[:], 0))
            s = pool.did(nc.gpsimd.memset(before[:], 1.0))
            pool.need(s)
            consts = pool.did(nc.gpsimd.affine_select(out=before[:], in_=before[:], compare_op=ALU.is_gt, fill=0.0,
                                                      base=0, pattern=[[1, P]], channel_multiplier=-1))
            zeroed = core.load(slot_dram[:, :].rearrange("(s p) a -> s (p a)", p=128), zero_slots[:], consts)

            dve.need(*got_a)
            s = dve.did(nc.vector.scalar_tensor_tensor(raw[:], prm[:, 3:5], -1.0, prm[:, 3:5], ALU.mult, ALU.max))
            act.need(s)
            s = act.did(nc.scalar.activation(raw[:], raw[:], ACT.Exp, scale=-1.0))
            act.need(s)
            s = act.did(nc.scalar.activation(raw[:], raw[:], ACT.Ln, bias=1.0))
            dve.need(s)
            s = dve.did(nc.vector.scalar_tensor_tensor(prm[:, 3:5], prm[:, 3:5], 0.0, raw[:], ALU.max, ALU.add))
            dve.need(s)
            dve.did(nc.vector.tensor_scalar(prm[:, 5:7], prm[:, 3:5], -1.0, None, ALU.mult))
            s = dve.did(nc.vector.memset(prm[:, 7:8], 0.0))
            s = core.load(param_dram[:, :], prm[:], s)
            got_prm = core.load(shared_prm[:], param_dram[EXPERTS, :].partition_broadcast(128), s)

            cols_ready = {}

            def turn(t, ready):
                b, s = turn_tile(nc, core, n_rows[:, t, :], KC, ready)
                act.need(s)
                core.bank_free[b] = cols_ready[t] = act.did(nc.scalar.copy(cols[:, :, t * P:(t + 1) * P],
                                                                           turned(core, b)))

            norm = TileNorm(nc, core, x, n_rows, stat, mv, rstd, turn)
            for t in range(NT):
                norm.tile(t, None)
            norm.finish()
            normed = norm.normed[NT - 1]
            xf_stored = core.load(rows_view(xf_dram), n_rows[:], normed)
            pe.need(*got)
            dve.need(*got, consts)
            for t in range(NT):
                pe.need(cols_ready[t])
                b = core.bank()
                for k in range(KC):
                    ins = nc.tensor.matmul(psum[0:P, b * BANK:b * BANK + EXPERTS], cols[:, k, t * P:(t + 1) * P],
                                           gate_w[:, k, :], start=(k == 0), stop=(k == KC - 1))
                s = pe.did(ins)
                dve.need(s)
                core.bank_free[b] = s = dve.did(nc.vector.tensor_tensor(
                    logit[:, t, :], psum[0:P, b * BANK:b * BANK + EXPERTS], gate_b[:, :], ALU.add))
            logits = s

            gathered = []

            def gather(i, ready):
                pool.need(ready)
                gathered.append(core.indirect(xf_dram[:, :], rows_ring[:, i % NT, :], slot_node[:, i:i + 1],
                                              scatter=False))

            def assign():
                dve.need(logits)
                s = dve.did(nc.vector.tensor_reduce(small[:, :, 0], logit[:], AX.X, ALU.max))
                dve.need(s)
                s = dve.did(nc.vector.tensor_scalar(small[:, :, 0], small[:, :, 0], -1.0, None, ALU.mult))
                act.need(s)
                for t in range(NT):
                    s = act.did(nc.scalar.activation(logit[:, t, :], logit[:, t, :], ACT.Exp, bias=small[:, t, 0:1],
                                                     accum_out=small[:, t, 1:2]))
                dve.need(s)
                s = dve.did(nc.vector.reciprocal(small[:, :, 2], small[:, :, 1]))
                dve.need(s)
                for t in range(NT):
                    s = dve.did(nc.vector.tensor_scalar(logit[:, t, :], logit[:, t, :], small[:, t, 2:3], None, ALU.mult))
                dve.need(s)
                for t in range(NT):
                    s = dve.did(nc.vector.max(top[:, t, :], logit[:, t, :]))
                dve.need(s)
                for t in range(NT):
                    s = dve.did(nc.vector.max_index(top_i[:, t, :], top[:, t, :], logit[:, t, :]))
                dve.need(s)
                s = dve.did(nc.vector.tensor_copy(top_f[:], top_i[:, :, 0:2]))
                s = dve.did(nc.vector.tensor_tensor(small[:, :, 0], top[:, :, 0], top[:, :, 1], ALU.add))
                dve.need(s)
                s = dve.did(nc.vector.reciprocal(small[:, :, 1], small[:, :, 0]))
                dve.need(s)
                for n in range(2):
                    s = dve.did(nc.vector.tensor_tensor(weight[:, :, n], top[:, :, n], small[:, :, 1], ALU.mult))
                dve.need(s)
                for t in range(NT):
                    for n in range(2):
                        s = dve.did(nc.vector.tensor_scalar(pick[:, n, t, :], lane[:, :], top_f[:, t, n:n + 1], None,
                                                            ALU.is_equal))
                dve.need(s)
                s = dve.did(nc.vector.tensor_tensor(member[:], pick[:, 0], pick[:, 1], ALU.add))
                flat = lambda v: v.rearrange("p t e -> p (t e)")
                yield
                pe.need(s, consts)
                b_rank, b_tot = 6, 7
                bank = lambda b, n=NT * EXPERTS, p=P: psum[0:p, b * BANK:b * BANK + n]
                nc.tensor.matmul(bank(b_rank), before[:, :], flat(member[:]), start=True, stop=True)
                s = pe.did(nc.tensor.matmul(bank(b_tot), ones[:, :], flat(member[:]), start=True, stop=True))
                dve.need(s)
                s = dve.did(nc.vector.tensor_reduce(total[:], bank(b_tot).rearrange("p (t e) -> p e t", e=EXPERTS), AX.X,
                                                    ALU.add))
                dve.need(s)
                s = dve.did(nc.vector.tensor_scalar(tiles_of[:, 0, :], total[:], 1.0 / 128, 127.0 / 256, ALU.mult, ALU.add))
                dve.need(s)
                s = dve.did(nc.vector.tensor_scalar(tiles_of[:, 0, :], tiles_of[:, 0, :], ROUND, None, ALU.add))
                dve.need(s)
                s = dve.did(nc.vector.tensor_scalar(tiles_of[:, 0, :], tiles_of[:, 0, :], -ROUND, None, ALU.add))
                dve.need(s)
                s = dve.did(nc.vector.tensor_copy(tiles_of[:, 1, :], tiles_of[:, 0, :]))
                dve.need(s)
                cur, step = 1, 1
                while step < EXPERTS:
                    other = 3 - cur
                    dve.did(nc.vector.tensor_copy(tiles_of[:, other, 0:step], tiles_of[:, cur, 0:step]))
                    s = dve.did(nc.vector.tensor_tensor(tiles_of[:, other, step:], tiles_of[:, cur, step:],
                                                        tiles_of[:, cur, 0:EXPERTS - step], ALU.add))
                    dve.need(s)
                    cur, step = other, 2 * step
                ends = tiles_of[:, cur, :]
                s = dve.did(nc.vector.tensor_tensor(start_of[:, 0, :], ends, tiles_of[:, 0, :], ALU.subtract))
                s2 = dve.did(nc.vector.tensor_scalar(passed[:], tiles_of[0:S, cur, :], slot_id[:, 0:1], None, ALU.is_le))
                dve.need(s, s2)
                s = dve.did(nc.vector.tensor_scalar(start_of[:, 0, :], start_of[:, 0, :], 128.0, None, ALU.mult))
                s2 = dve.did(nc.vector.tensor_reduce(expert_f[:], passed[:], AX.X, ALU.add))
                dve.need(s, s2)
                s2 = dve.did(nc.vector.tensor_scalar(expert_i[:], expert_f[:], float(EXPERTS - 1), None, ALU.min))
                s2 = core.load(expert_dram[:, :], expert_i[:], s2)
                got_e = core.load(slot_expert[:], expert_dram[:, :].rearrange("s a -> (s a)").rearrange(
                    "(a s) -> a s", a=1), s2)
                for t in range(NT):
                    s = dve.did(nc.vector.tensor_tensor(start_of[:, t + 1, :], start_of[:, t, :],
                                                        psum[0:P, b_tot * BANK + t * EXPERTS:b_tot * BANK + (t + 1) * EXPERTS],
                                                        ALU.add))
                    dve.need(s)
                s = dve.did(nc.vector.tensor_tensor(flat(place[:]), bank(b_rank), flat(start_of[:, 0:NT, :]), ALU.add))
                core.bank_free[b_rank] = core.bank_free[b_tot] = s
                dve.need(s)
                for n in range(2):
                    s = dve.did(nc.vector.tensor_tensor(member[:], place[:], pick[:, n], ALU.mult))
                    dve.need(s)
                    s = dve.did(nc.vector.tensor_reduce(pos_f[:, n, :], member[:], AX.X, ALU.add))
                    dve.need(s)
                s = dve.did(nc.vector.tensor_copy(pos[:, :], pos_f[:].rearrange("p n t -> p (n t)")))
                pool.need(s, zeroed)
                scattered = []
                for n in range(2):
                    for t in range(NT):
                        i = n * NT + t
                        scattered.append(core.indirect(slot_dram[:, :], node_id[:, t:t + 1], pos[:, i:i + 1], scatter=True))
                got_s = core.load(slot_rows_i[:], slot_dram[:, :].rearrange("(s p) a -> s (p a)", p=128), *scattered)

                for t in range(NT):
                    for n in range(2):
                        s = dve.did(nc.vector.tensor_scalar(pick[:, n, t, :], pick[:, n, t, :], weight[:, t, n:n + 1],
                                                            None, ALU.mult))
                dve.need(s)
                s = dve.did(nc.vector.tensor_tensor(cw[:], pick[:, 0], pick[:, 1], ALU.add))
                yield
                for t in range(NT):
                    b, s2 = turn_tile(nc, core, cw[:, t, :], 1, s, width=EXPERTS)
                    dve.need(s2)
                    core.bank_free[b] = last = dve.did(nc.vector.tensor_copy(cw_cols[:, t * P:(t + 1) * P],
                                                                             psum[0:EXPERTS, b * BANK:b * BANK + P]))
                pool.need(*got, normed)
                for t in range(NT):
                    x_b = pool.did(nc.gpsimd.tensor_tensor(x[:, t, :], x[:, t, :], shared_b2[:, :], ALU.add))
                pe.need(last)
                for t in range(NT):
                    b = core.bank()
                    s = pe.did(nc.tensor.matmul(psum[0:P, b * BANK:b * BANK + D], cw_cols[:, t * P:(t + 1) * P],
                                                b2[:, :], start=True, stop=True))
                    dve.need(s, x_b)
                    core.bank_free[b] = dve.did(nc.vector.tensor_tensor(x[:, t, :], x[:, t, :],
                                                                        psum[0:P, b * BANK:b * BANK + D], ALU.add))
                yield
                dve.need(got_s)
                s = dve.did(nc.vector.tensor_copy(slot_rows[:], slot_rows_i[:]))
                pe.need(s)
                b = core.bank()
                s = pe.did(nc.tensor.transpose(psum[0:128, b * BANK:b * BANK + S], slot_rows[:, :], core.ident[0:S, 0:S]))
                dve.need(s)
                core.bank_free[b] = dve.did(nc.vector.tensor_copy(slot_node[:], psum[0:128, b * BANK:b * BANK + S]))
                pool.need(core.bank_free[b], xf_stored)
                for i in range(NT):
                    gather(i, None)
                yield

            core.ring = 6
            assignment = assign()
            next(assignment)

            act.need(got_prm, *got_b1)
            dve.need(got_prm)
            q = shared_prm
            free = [None, None]
            n = 0
            for start, width in SPANS:
                for c in range(IC):
                    g_, u_, sg = (scratch[n % 2][:, i, 0:width] for i in range(3))
                    banks = []
                    for half in range(2):
                        b = core.bank()
                        pe.need(got_w1)
                        for k in range(KC):
                            col = c * 256 + half
                            ins = nc.tensor.matmul(psum[0:128, b * BANK:b * BANK + width],
                                                   w1[:, k, col:col + 255:2], cols[:, k, start:start + width],
                                                   start=(k == 0), stop=(k == KC - 1))
                        banks.append((b, pe.did(ins)))
                    act.need(free[n % 2])
                    for half, dst in enumerate((g_, u_)):
                        b, s = banks[half]
                        act.need(s)
                        core.bank_free[b] = act.did(nc.scalar.activation(
                            dst, psum[0:128, b * BANK:b * BANK + width], ACT.Identity, bias=b1[:, half, c:c + 1]))
                        dve.need(core.bank_free[b])
                        s = dve.did(nc.vector.tensor_scalar(dst, dst, q[:, 3 + half:4 + half],
                                                            q[:, 5 + half:6 + half], ALU.min, ALU.max))
                        if half == 0:
                            act.need(s)
                            sig = act.did(nc.scalar.activation(sg, g_, ACT.Sigmoid, scale=q[:, 0:1]))
                    dve.need(sig)
                    s = dve.did(nc.vector.scalar_tensor_tensor(sg, g_, q[:, 1:2], sg, ALU.mult, ALU.mult))
                    dve.need(s)
                    free[n % 2] = dve.did(nc.vector.scalar_tensor_tensor(
                        hidden[:, c, start:start + width], u_, q[:, 2:3], sg, ALU.add, ALU.mult))
                    n += 1
                    if n in (2, 4, 9):
                        next(assignment)
            h_done = (dve.sem, dve.count)

            def add_shared(t, acc, s):
                dve.need(s)
                s = dve.did(nc.vector.tensor_tensor(x[:, t, :], x[:, t, :], acc, ALU.add))
                for i in range(t * SLOT_COLS_TILES // NT, (t + 1) * SLOT_COLS_TILES // NT):
                    turn_slots(i)
                return s

            def turn_slots(i):
                pe.need(gathered[i])
                b = core.bank()
                for c in range(KC):
                    ins = nc.tensor.transpose(psum[0:128, b * BANK + c * 128:b * BANK + (c + 1) * 128],
                                              rows_ring[:, i % NT, c * 128:(c + 1) * 128], core.ident[:, :])
                s = pe.did(ins)
                q = act if i % 2 else dve
                q.need(s, h_done)
                dst = slot_cols[:, :, i * 128:(i + 1) * 128]
                src = psum[0:128, b * BANK:(b + 1) * BANK].rearrange("p (c n) -> p c n", n=128)
                core.bank_free[b] = q.did(nc.scalar.copy(dst, src) if i % 2 else nc.vector.tensor_copy(dst, src))
                if i + NT < SLOT_COLS_TILES:
                    gather(i + NT, s)

            rows_product(nc, core, lambda k, s0, m: hidden[:, k, s0:s0 + m], lambda k: w2[:, k, :], IC,
                         (h_done, got_w2), add_shared)
            core.ring = 8
            core.restart()

        U = SLOT_UNROLL
        loop = ctx.enter_context(ExitStack())
        ring = lambda name, shape: [loop.enter_context(nc.sbuf_tensor(f"{name}{i}", shape, F32)) for i in range(U)]
        ew1 = ring("m_ew1_", [128, KC, 2 * FFN_I])
        ew2 = ring("m_ew2_", [128, IC, D])
        eb1 = ring("m_eb1_", [128, 2 * FFN_I])
        eprm = ring("m_eprm", [128, 8])
        x_cols = ring("m_x_cols", [128, KC, 128])
        h = ring("m_h", [128, 2 * FFN_I])
        gate = ring("m_gate", [128, FFN_I])
        t_cols = ring("m_t_cols", [128, IC, 128])
        TURN_BANK, OUT_BANK = 6, 7

        def expert_of(tile):
            return nc.scalar.value_load(slot_expert[0:1, ds(tile, 1)], min_val=0, max_val=EXPERTS - 1)

        def load_up(e, u, done):
            last["w1", u] = [
                core.load(ew1[u][:], a["L0_ffn_expert_w1"][ds(e, 1), :, :].rearrange("l (c p) o -> p (l c) o", p=128),
                          *done, by=core.act),
                core.load(eb1[u][:], a["L0_ffn_expert_b1"][ds(e, 1), :].rearrange("l o -> (l o)")
                          .partition_broadcast(128), by=core.act),
                core.load(eprm[u][:], param_dram[ds(e, 1), :].rearrange("l o -> (l o)").partition_broadcast(128),
                          by=core.act)]

        def load_down(e, u, done):
            last["w2", u] = [core.load(ew2[u][:], a["L0_ffn_expert_w2"][ds(e, 1), :, :].rearrange(
                "l (c p) o -> p (l c) o", p=128), *done, by=core.act)]

        last = {}

        def done(*key):
            return last.get(key, [])

        def take_x(tile, u):
            act.need(*done("up", u))
            last["x", u] = [act.did(nc.scalar.copy(x_cols[u][:], slot_cols[:, :, ds(tile * 128, 128)]))]

        def up(u, c0, cn):
            base = 2 * u * BANK + c0
            pe.need(*done("x", u), *done("w1", u), *done("bias", u))
            for k in range(KC):
                ins = nc.tensor.matmul(psum[0:128, base:base + cn], x_cols[u][:, k, :], ew1[u][:, k, c0:c0 + cn],
                                       start=(k == 0), stop=(k == KC - 1))
            if c0 + cn == 2 * FFN_I:
                last["up", u] = [pe.did(ins)]

        def swiglu(u):
            q = eprm[u]
            dve.need(*done("up", u), *done("w1", u), *done("stored", u))
            act.need(*done("w1", u), *done("turn", u))
            s = dve.did(nc.vector.tensor_tensor(h[u][:], psum[0:128, 2 * u * BANK:2 * u * BANK + 2 * FFN_I],
                                                eb1[u][:], ALU.add))
            last["bias", u] = [s]
            dve.need(s)
            g_, u_ = h[u][:, 0:2 * FFN_I:2], h[u][:, 1:2 * FFN_I:2]
            s = dve.did(nc.vector.tensor_scalar(g_, g_, q[:, 3:4], q[:, 5:6], ALU.min, ALU.max))
            dve.did(nc.vector.tensor_scalar(u_, u_, q[:, 4:5], q[:, 6:7], ALU.min, ALU.max))
            act.need(s)
            s = act.did(nc.scalar.activation(gate[u][:], g_, ACT.Sigmoid, scale=q[:, 0:1]))
            dve.need(s)
            s = dve.did(nc.vector.scalar_tensor_tensor(gate[u][:], g_, q[:, 1:2], gate[u][:], ALU.mult, ALU.mult))
            dve.need(s)
            last["swiglu", u] = [dve.did(nc.vector.scalar_tensor_tensor(gate[u][:], u_, q[:, 2:3], gate[u][:],
                                                                        ALU.add, ALU.mult))]

        def turn_gate(u):
            pe.need(*done("swiglu", u), *done("turn bank"))
            for c in range(IC):
                ins = nc.tensor.transpose(psum[0:128, TURN_BANK * BANK + c * 128:TURN_BANK * BANK + (c + 1) * 128],
                                          gate[u][:, c * 128:(c + 1) * 128], core.ident[:, :])
            s = pe.did(ins)
            last["turn", u] = [s]
            act.need(s, *done("down", u))
            last["turn bank",] = [act.did(nc.scalar.copy(
                t_cols[u][:], psum[0:128, TURN_BANK * BANK:TURN_BANK * BANK + FFN_I].rearrange("p (c n) -> p c n",
                                                                                             n=128)))]

        def down(u):
            pe.need(*done("turn bank"), *done("out bank"), *done("w2", u))
            for k in range(IC):
                ins = nc.tensor.matmul(psum[0:128, OUT_BANK * BANK:(OUT_BANK + 1) * BANK], t_cols[u][:, k, :],
                                       ew2[u][:, k, :], start=(k == 0), stop=(k == IC - 1))
            last["down", u] = [pe.did(ins)]

        def store(tile, u):
            act.need(*done("down", u), *done("swiglu", u))
            s = act.did(nc.scalar.copy(h[u][:, 0:D], psum[0:128, OUT_BANK * BANK:(OUT_BANK + 1) * BANK]))
            last["out bank",] = [s]
            last["stored", u] = [core.load(y_dram[ds(tile * 128, 128), :], h[u][:, 0:D], s, by=core.act)]

        def experts(it, ends=False):
            for u in range(U):
                v = (u + 1) % U
                more = not ends or u < U - 1
                if not ends:
                    e_down, e_up = expert_of(U * it + u + U), expert_of(U * it + u + 1 + U)
                if more:
                    up(v, 0, BANK)
                turn_gate(u)
                if more:
                    up(v, BANK, 2 * FFN_I - BANK)
                if not ends or u < U - 2:
                    take_x(U * it + u + 2, (u + 2) % U)
                if more:
                    swiglu(v)
                down(u)
                store(U * it + u, u)
                if not ends:
                    load_down(e_down, u, done("down", u))
                    load_up(e_up, v, done("up", v) + done("swiglu", v))

        for u in range(U):
            e = expert_of(u)
            load_up(e, u, ())
            load_down(e, u, ())
        take_x(0, 0)
        take_x(1, 1)
        up(0, 0, BANK)
        up(0, BANK, 2 * FFN_I - BANK)
        swiglu(0)
        load_up(expert_of(U), 0, done("up", 0) + done("swiglu", 0))
        last = earlier(last, core.enter_loop())
        experts(0)
        last = earlier(last, core.next_iterations(None))
        with nc.Fori(1, SLOT_ROUNDS - 1) as it:
            core.loop.iteration = it
            experts(it)
        last = earlier(last, core.leave_loop(SLOT_ROUNDS - 1))
        stored = [s for u in range(U) for s in done("stored", u)]
        experts(SLOT_ROUNDS - 1, ends=True)
        stored += [s for u in range(U) for s in done("stored", u)]
        pool.need(*stored)

        sb = lambda name, shape, dt=F32: loop.enter_context(nc.sbuf_tensor(name, shape, dt))
        back = [sb(f"m_back{i}", [P, D]) for i in range(4)]
        free = [None] * 4
        for i in range(2 * NT):
            n, t = i % 2, i // 2
            j = n * NT + t
            pool.need(free[i % 4])
            s = core.indirect(y_dram[:, :], back[i % 4][:], pos[:, j:j + 1], scatter=False)
            dve.need(s)
            free[i % 4] = s = dve.did(nc.vector.scalar_tensor_tensor(x[:, t, :], back[i % 4][:], weight[:, t, n:n + 1],
                                                                     x[:, t, :], ALU.mult, ALU.add))
            dve.need(s)
            if n == 1:
                core.load(out[t * P:(t + 1) * P, :], x[:, t, :], s)
        core.restart()


_INS = ['x', 'src', 'dst', 'node_vec1', 'L0_gnn_f_w1', 'L0_gnn_f_b1', 'L0_gnn_f_w2', 'L0_gnn_f_b2', 'L0_gnn_s1_w',
        'L0_gnn_s1_b', 'L0_gnn_b1_w', 'L0_gnn_b1_b', 'L0_gnn_wq', 'L0_gnn_bq', 'L0_gnn_wk', 'L0_gnn_bk',
        'L0_gnn_wv', 'L0_gnn_bv', 'L0_gnn_wo', 'L0_gnn_bo', 'L0_gnn_s2_w', 'L0_gnn_s2_b', 'L0_gnn_b2_w',
        'L0_gnn_b2_b', 'L0_gnn_m_w1', 'L0_gnn_m_b1', 'L0_gnn_m_w2', 'L0_gnn_m_b2', 'L0_mix_Wqkv', 'L0_mix_bqkv',
        'L0_mix_Pmat', 'L0_mix_Wproj', 'L0_mix_bproj', 'L0_mix_W1', 'L0_mix_b1', 'L0_mix_W2', 'L0_mix_b2',
        'L0_mix_g1', 'L0_mix_be1', 'L0_mix_g2', 'L0_mix_be2', 'L0_ffn_gate_w', 'L0_ffn_gate_b',
        'L0_ffn_shared_w1', 'L0_ffn_shared_b1', 'L0_ffn_shared_w2', 'L0_ffn_shared_b2', 'L0_ffn_shared_act',
        'L0_ffn_expert_w1', 'L0_ffn_expert_b1', 'L0_ffn_expert_w2', 'L0_ffn_expert_b2', 'L0_ffn_expert_act']


def kernel(**inputs):
    import numpy as _np
    import concourse.bacc as _bacc
    from concourse import mybir as _mybir
    from concourse.bass_utils import run_bass_kernel_spmd as _run

    nc = _bacc.Bacc("TRN2", target_bir_lowering=False, num_devices=1)
    arrays, aps = {}, {}
    for name in _INS:
        v = _np.ascontiguousarray(inputs[name])
        arrays[f"in_{name}"] = v
        aps[name] = nc.dram_tensor(f"in_{name}", v.shape, _mybir.dt.from_np(v.dtype), kind="ExternalInput").ap()
    out = nc.dram_tensor("out_0", (N, D), F32, kind="ExternalOutput").ap()
    build(nc, aps, out)
    r = _run(nc, [arrays], core_ids=[0])
    return r.results[0]["out_0"]
```
